# Optimizing a Trainium2 kernel written in Bass

```python
import numpy as np
import jax
import jax.numpy as jnp

def _softmax(x, axis=-1):
    return jax.nn.softmax(x, axis=axis)

def _gelu(x):
    return jax.nn.gelu(x, approximate=True)

def _silu(x):
    return jax.nn.silu(x)

def _sigmoid(x):
    return jax.nn.sigmoid(x)

def _layernorm(x, axis=-1, eps=1e-05):
    m = jnp.mean(x, axis=axis, keepdims=True)
    v = jnp.var(x, axis=axis, keepdims=True)
    return (x - m) / jnp.sqrt(v + eps)

def _scatter_add(tgt, idx, src, axis=0):
    return tgt.at[idx].add(src)

def _segment_sum(src, seg, n):
    return jax.ops.segment_sum(src, seg, n)
kernel_name = 'mk_flamingo_gated_d2_seqx_r8_cdb7c4'

def setup_inputs(seed: int=0):
    np.random.seed(seed)
    _w = jnp.asarray

    def _rec_inputs():
        import jax
        import jax.numpy as jnp
        _rk = jax.random.key(seed)
        x = -0.0002928 + 1 * jax.random.normal(jax.random.fold_in(_rk, 1), (64, 128, 128), jnp.float32)
        _lenS = 128 - jax.random.randint(jax.random.fold_in(_rk, 7), (64,), 0, max(1, 128 // 4) + 1, jnp.int32)
        _lenS2 = 120 - jax.random.randint(jax.random.fold_in(_rk, 8), (64,), 0, max(1, 120 // 4) + 1, jnp.int32)
        _ctx_1024P = jax.random.normal(jax.random.fold_in(_rk, 11), (64, 16, 128), jnp.float32)
        _ctx_1024c = jax.random.dirichlet(jax.random.fold_in(_rk, 511), 0.3 * jnp.ones((16,), jnp.float32), (64, 120))
        _ctx_1024t = jnp.einsum('bsk,bkd->bsd', _ctx_1024c, _ctx_1024P)
        _ctx_1024t = _ctx_1024t * jax.lax.rsqrt(jnp.mean(jnp.square(_ctx_1024t)) + 1e-12) * 0.953939
        ctx_1024 = 4.13588e-05 + 0.999923 * (_ctx_1024t + 0.3 * jax.random.normal(jax.random.fold_in(_rk, 611), (64, 120, 128), jnp.float32))
        _validS = jnp.arange(128)[None, :] < _lenS[:, None]
        _validS2 = jnp.arange(120)[None, :] < _lenS2[:, None]
        _causal = jnp.tril(jnp.ones((128, 128), dtype=bool))
        mask_BxS2_if1 = jnp.where(jnp.ones((64, 120), dtype=bool), 1, 0).astype(jnp.int32)
        _g = jax.random.normal(jax.random.fold_in(_rk, 9001), (2, 2), jnp.float32)
        _g = jnp.sign(_g) * jnp.maximum(jnp.abs(_g), 1.0) + (_g == 0) * 1.0
        g_xattn = _g[0]
        g_ffn = _g[1]
        return (x, ctx_1024, mask_BxS2_if1, g_xattn, g_ffn)
    x, ctx_1024, mask_BxS2_if1, g_xattn, g_ffn = _rec_inputs()

    def _L0_xattn_setup():
        import jax, jax.numpy as jnp
        import numpy as np
        HEADS = 16
        DIM_HEAD = 64
        LN_EPS = 1e-05
        COS_EPS = 1e-08

        def _layernorm(x, gamma, beta):
            mu = jnp.mean(x, axis=-1, keepdims=True)
            var = jnp.mean(jnp.square(x - mu), axis=-1, keepdims=True)
            return (x - mu) * jax.lax.rsqrt(var + LN_EPS) * gamma + beta

        def _project(t, gamma, beta, W_in):
            x = _layernorm(t, gamma, beta) @ W_in
            b, n, _ = x.shape
            return x.reshape(b, n, HEADS, DIM_HEAD).transpose(0, 2, 1, 3)
        key = jax.random.key(seed)
        ks = jax.random.split(key, 5)
        dim = 128
        inner = HEADS * DIM_HEAD
        q = jax.random.normal(ks[0], (4, 128, dim), dtype=jnp.float32)
        k = jax.random.normal(ks[1], (4, 256, dim), dtype=jnp.float32)
        v = jax.random.normal(ks[2], (4, 256, dim), dtype=jnp.float32)
        W_in = jax.random.normal(ks[3], (dim, inner), dtype=jnp.float32) * (1.0 / np.sqrt(dim))
        W_out = jax.random.normal(ks[4], (inner, dim), dtype=jnp.float32) * (1.0 / np.sqrt(inner))
        ln_gamma = jnp.ones((dim,), dtype=jnp.float32)
        ln_beta = jnp.zeros((dim,), dtype=jnp.float32)
        b_out = jnp.zeros((dim,), dtype=jnp.float32)
        return {'q': q, 'k': k, 'v': v, 'ln_gamma': ln_gamma, 'ln_beta': ln_beta, 'W_in': W_in, 'W_out': W_out, 'b_out': b_out}
    _L0_xattn_all = _L0_xattn_setup()
    _L0_xattn_in = {k: v for k, v in _L0_xattn_all.items() if k in ('ln_gamma', 'ln_beta', 'W_in', 'W_out', 'b_out')}
    del _L0_xattn_all

    def _L0_ffn_setup():
        import jax, jax.numpy as jnp
        import numpy as np
        B, S, H, I, E_ROUTED, TOP_K = (8, 256, 128, 256, 8, 2)

        def _expert(x, Wg, Wu, Wd):
            return jax.nn.silu(x @ Wg.T) * (x @ Wu.T) @ Wd.T
        key = jax.random.key(seed)
        ks = jax.random.split(key, 9)
        s = 0.02
        return {'x': jax.random.normal(ks[0], (B, S, H), dtype=jnp.float32), 'Wg_s': jax.random.normal(ks[1], (I, H), dtype=jnp.float32) * s, 'Wu_s': jax.random.normal(ks[2], (I, H), dtype=jnp.float32) * s, 'Wd_s': jax.random.normal(ks[3], (H, I), dtype=jnp.float32) * s, 'Wg': jax.random.normal(ks[4], (E_ROUTED, I, H), dtype=jnp.float32) * s, 'Wu': jax.random.normal(ks[5], (E_ROUTED, I, H), dtype=jnp.float32) * s, 'Wd': jax.random.normal(ks[6], (E_ROUTED, H, I), dtype=jnp.float32) * s, 'Wr': jax.random.normal(ks[7], (E_ROUTED, H), dtype=jnp.float32) * s, 'rb': jnp.zeros((E_ROUTED,), dtype=jnp.float32)}
    _L0_ffn_all = _L0_ffn_setup()
    _L0_ffn_in = {k: v for k, v in _L0_ffn_all.items() if k in ('Wg_s', 'Wu_s', 'Wd_s', 'Wg', 'Wu', 'Wd', 'Wr', 'rb')}
    del _L0_ffn_all

    def _L1_xattn_setup():
        import jax, jax.numpy as jnp
        import numpy as np
        import math
        N, T, D_MODEL, H, D = (4, 256, 128, 16, 64)
        key = jax.random.key(seed)
        ks = jax.random.split(key, 12)
        s = 0.02
        return {'xq': jax.random.normal(ks[0], (N, T, D_MODEL), dtype=jnp.float32), 'xk': jax.random.normal(ks[1], (N, T, D_MODEL), dtype=jnp.float32), 'xv': jax.random.normal(ks[2], (N, T, D_MODEL), dtype=jnp.float32), 'padding_mask': jnp.ones((N, T), dtype=jnp.int32), 'Wq': jax.random.normal(ks[3], (D_MODEL, H * D), dtype=jnp.float32) * s, 'bq': jnp.zeros((H * D,), dtype=jnp.float32), 'Wk': jax.random.normal(ks[4], (D_MODEL, H * D), dtype=jnp.float32) * s, 'bk': jnp.zeros((H * D,), dtype=jnp.float32), 'Wv': jax.random.normal(ks[5], (D_MODEL, H * D), dtype=jnp.float32) * s, 'bv': jnp.zeros((H * D,), dtype=jnp.float32), 'Wo': jax.random.normal(ks[6], (H * D, D_MODEL), dtype=jnp.float32) * s, 'bo': jnp.zeros((D_MODEL,), dtype=jnp.float32)}
    _L1_xattn_all = _L1_xattn_setup()
    _L1_xattn_in = {k: v for k, v in _L1_xattn_all.items() if k in ('Wq', 'bq', 'Wk', 'bk', 'Wv', 'bv', 'Wo', 'bo')}
    del _L1_xattn_all

    def _L1_ffn_setup():
        import jax, jax.numpy as jnp
        import numpy as np
        E, H, I = (8, 128, 64)
        NG, TKG, TOPK = (4, 2, 4)
        SCALE = 2.5

        def _mlp(x, wg, wu, wd):
            return jax.nn.silu(x @ wg) * (x @ wu) @ wd
        key = jax.random.key(seed)
        ks = jax.random.split(key, 8)
        s = 0.02
        return {'hidden_states': jax.random.normal(ks[0], (32, 32, H), jnp.float32), 'gate_w': jax.random.normal(ks[1], (E, H), jnp.float32) * np.float32(np.sqrt(2.0 / H)), 'correction_bias': jnp.zeros((E,), jnp.float32), 'Wg': jax.random.normal(ks[2], (E, H, I), jnp.float32) * s, 'Wu': jax.random.normal(ks[3], (E, H, I), jnp.float32) * s, 'Wd': jax.random.normal(ks[4], (E, I, H), jnp.float32) * s, 'Wg_s': jax.random.normal(ks[5], (H, I), jnp.float32) * s, 'Wu_s': jax.random.normal(ks[6], (H, I), jnp.float32) * s, 'Wd_s': jax.random.normal(ks[7], (I, H), jnp.float32) * s}
    _L1_ffn_all = _L1_ffn_setup()
    _L1_ffn_in = {k: v for k, v in _L1_ffn_all.items() if k in ('gate_w', 'correction_bias', 'Wg', 'Wu', 'Wd', 'Wg_s', 'Wu_s', 'Wd_s')}
    del _L1_ffn_all
    return {'x': x, 'ctx_1024': ctx_1024, 'mask_BxS2_if1': mask_BxS2_if1, 'g_xattn': g_xattn, 'g_ffn': g_ffn, 'L0_xattn_ln_gamma': _L0_xattn_in['ln_gamma'], 'L0_xattn_ln_beta': _L0_xattn_in['ln_beta'], 'L0_xattn_W_in': _L0_xattn_in['W_in'], 'L0_xattn_W_out': _L0_xattn_in['W_out'], 'L0_xattn_b_out': _L0_xattn_in['b_out'], 'L0_ffn_Wg_s': _L0_ffn_in['Wg_s'], 'L0_ffn_Wu_s': _L0_ffn_in['Wu_s'], 'L0_ffn_Wd_s': _L0_ffn_in['Wd_s'], 'L0_ffn_Wg': _L0_ffn_in['Wg'], 'L0_ffn_Wu': _L0_ffn_in['Wu'], 'L0_ffn_Wd': _L0_ffn_in['Wd'], 'L0_ffn_Wr': _L0_ffn_in['Wr'], 'L0_ffn_rb': _L0_ffn_in['rb'], 'L1_xattn_Wq': _L1_xattn_in['Wq'], 'L1_xattn_bq': _L1_xattn_in['bq'], 'L1_xattn_Wk': _L1_xattn_in['Wk'], 'L1_xattn_bk': _L1_xattn_in['bk'], 'L1_xattn_Wv': _L1_xattn_in['Wv'], 'L1_xattn_bv': _L1_xattn_in['bv'], 'L1_xattn_Wo': _L1_xattn_in['Wo'], 'L1_xattn_bo': _L1_xattn_in['bo'], 'L1_ffn_gate_w': _L1_ffn_in['gate_w'], 'L1_ffn_correction_bias': _L1_ffn_in['correction_bias'], 'L1_ffn_Wg': _L1_ffn_in['Wg'], 'L1_ffn_Wu': _L1_ffn_in['Wu'], 'L1_ffn_Wd': _L1_ffn_in['Wd'], 'L1_ffn_Wg_s': _L1_ffn_in['Wg_s'], 'L1_ffn_Wu_s': _L1_ffn_in['Wu_s'], 'L1_ffn_Wd_s': _L1_ffn_in['Wd_s']}

def reference(x, ctx_1024, mask_BxS2_if1, g_xattn, g_ffn, L0_xattn_ln_gamma, L0_xattn_ln_beta, L0_xattn_W_in, L0_xattn_W_out, L0_xattn_b_out, L0_ffn_Wg_s, L0_ffn_Wu_s, L0_ffn_Wd_s, L0_ffn_Wg, L0_ffn_Wu, L0_ffn_Wd, L0_ffn_Wr, L0_ffn_rb, L1_xattn_Wq, L1_xattn_bq, L1_xattn_Wk, L1_xattn_bk, L1_xattn_Wv, L1_xattn_bv, L1_xattn_Wo, L1_xattn_bo, L1_ffn_gate_w, L1_ffn_correction_bias, L1_ffn_Wg, L1_ffn_Wu, L1_ffn_Wd, L1_ffn_Wg_s, L1_ffn_Wu_s, L1_ffn_Wd_s):
    import jax
    import jax.numpy as jnp

    def _L0_xattn_ref(q, k, v, ln_gamma, ln_beta, W_in, W_out, b_out):
        import jax, jax.numpy as jnp
        import numpy as np
        HEADS = 16
        DIM_HEAD = 64
        LN_EPS = 1e-05
        COS_EPS = 1e-08

        def _layernorm(x, gamma, beta):
            mu = jnp.mean(x, axis=-1, keepdims=True)
            var = jnp.mean(jnp.square(x - mu), axis=-1, keepdims=True)
            return (x - mu) * jax.lax.rsqrt(var + LN_EPS) * gamma + beta

        def _project(t, gamma, beta, W_in):
            x = _layernorm(t, gamma, beta) @ W_in
            b, n, _ = x.shape
            return x.reshape(b, n, HEADS, DIM_HEAD).transpose(0, 2, 1, 3)
        f_q = _project(q, ln_gamma, ln_beta, W_in)
        f_k = _project(k, ln_gamma, ln_beta, W_in)
        f_v = _project(v, ln_gamma, ln_beta, W_in)
        dots = jnp.einsum('bhnd,bhmd->bhnm', f_q, f_k)
        qn = jnp.linalg.norm(f_q, axis=-1, keepdims=True)
        kn = jnp.linalg.norm(f_k, axis=-1, keepdims=True)
        attn = dots / (qn * kn.transpose(0, 1, 3, 2) + COS_EPS)
        out = jnp.einsum('bhnm,bhmd->bhnd', attn, f_v)
        b, h, n, d = out.shape
        out = out.transpose(0, 2, 1, 3).reshape(b, n, h * d)
        return out @ W_out + b_out

    def _L0_ffn_ref(x, Wg_s, Wu_s, Wd_s, Wg, Wu, Wd, Wr, rb):
        import jax, jax.numpy as jnp
        import numpy as np
        B, S, H, I, E_ROUTED, TOP_K = (8, 256, 128, 256, 8, 2)

        def _expert(x, Wg, Wu, Wd):
            return jax.nn.silu(x @ Wg.T) * (x @ Wu.T) @ Wd.T
        shared = _expert(x, Wg_s, Wu_s, Wd_s)
        logits = jnp.einsum('bsh,eh->bse', x, Wr) + rb
        probs = jax.nn.sigmoid(logits)
        scores, idx = jax.lax.top_k(probs, TOP_K)
        cw = (jax.nn.one_hot(idx, E_ROUTED, dtype=x.dtype) * scores[..., None]).sum(-2)
        out = shared
        for e in range(E_ROUTED):
            out = out + cw[..., e:e + 1] * _expert(x, Wg[e], Wu[e], Wd[e])
        return out

    def _L1_xattn_ref(xq, xk, xv, padding_mask, Wq, bq, Wk, bk, Wv, bv, Wo, bo):
        import jax, jax.numpy as jnp
        import numpy as np
        import math
        N, T, D_MODEL, H, D = (4, 256, 128, 16, 64)
        n, t_out, _ = xq.shape
        t_in = xk.shape[1]
        Q = (xq @ Wq + bq).reshape(n, t_out, H, D).transpose(0, 2, 1, 3)
        K = (xk @ Wk + bk).reshape(n, t_in, H, D).transpose(0, 2, 1, 3)
        V = (xv @ Wv + bv).reshape(n, t_in, H, D).transpose(0, 2, 1, 3)
        scores = jnp.einsum('bhqd,bhkd->bhqk', Q, K) / math.sqrt(D)
        neg_inf = jnp.float32(-jnp.inf)
        scores = jnp.where(padding_mask[:, None, None, :] == 0, neg_inf, scores)
        q_idx = jnp.arange(t_out)[:, None]
        k_idx = jnp.arange(t_in)[None, :]
        scores = jnp.where((k_idx <= q_idx)[None, None, :, :], scores, neg_inf)
        w = jax.nn.softmax(scores, axis=-1)
        attn = jnp.einsum('bhqk,bhkd->bhqd', w, V)
        attn = attn.transpose(0, 2, 1, 3).reshape(n, t_out, H * D)
        return attn @ Wo + bo

    def _L1_ffn_ref(hidden_states, gate_w, correction_bias, Wg, Wu, Wd, Wg_s, Wu_s, Wd_s):
        import jax, jax.numpy as jnp
        import numpy as np
        E, H, I = (8, 128, 64)
        NG, TKG, TOPK = (4, 2, 4)
        SCALE = 2.5

        def _mlp(x, wg, wu, wd):
            return jax.nn.silu(x @ wg) * (x @ wu) @ wd
        B, T, _ = hidden_states.shape
        x = hidden_states.reshape(-1, H)
        N = x.shape[0]
        logits = x @ gate_w.T
        scores = jax.nn.sigmoid(logits)
        scores_c = scores + correction_bias
        grp = scores_c.reshape(N, NG, E // NG)
        group_scores = jnp.sum(jax.lax.top_k(grp, 2)[0], axis=-1)
        grp_idx = jax.lax.top_k(group_scores, TKG)[1]
        group_mask = jnp.zeros_like(group_scores).at[jnp.arange(N)[:, None], grp_idx].set(1.0)
        score_mask = jnp.repeat(group_mask, E // NG, axis=-1) > 0.5
        scores_for_choice = jnp.where(score_mask, scores_c, 0.0)
        topk_idx = jax.lax.top_k(scores_for_choice, TOPK)[1]
        topk_w = jnp.take_along_axis(scores, topk_idx, axis=-1)
        topk_w = topk_w / (jnp.sum(topk_w, axis=-1, keepdims=True) + 1e-20)
        topk_w = topk_w * SCALE
        cw = jnp.sum(jax.nn.one_hot(topk_idx, E, dtype=topk_w.dtype) * topk_w[..., None], axis=1)
        g = jnp.einsum('nh,ehi->eni', x, Wg)
        u = jnp.einsum('nh,ehi->eni', x, Wu)
        y = jnp.einsum('eni,eih->enh', jax.nn.silu(g) * u, Wd)
        routed = jnp.einsum('enh,ne->nh', y, cw)
        out = routed + _mlp(x, Wg_s, Wu_s, Wd_s)
        return out.reshape(B, T, H)
    x = x + jnp.tanh(g_xattn[0]) * _L0_xattn_ref(_layernorm(x, axis=-1), ctx_1024, ctx_1024, L0_xattn_ln_gamma, L0_xattn_ln_beta, L0_xattn_W_in, L0_xattn_W_out, L0_xattn_b_out)
    x = x + jnp.tanh(g_ffn[0]) * _L0_ffn_ref(_layernorm(x, axis=-1), L0_ffn_Wg_s, L0_ffn_Wu_s, L0_ffn_Wd_s, L0_ffn_Wg, L0_ffn_Wu, L0_ffn_Wd, L0_ffn_Wr, L0_ffn_rb)
    x = x + jnp.tanh(g_xattn[1]) * _L1_xattn_ref(_layernorm(x, axis=-1), ctx_1024, ctx_1024, mask_BxS2_if1, L1_xattn_Wq, L1_xattn_bq, L1_xattn_Wk, L1_xattn_bk, L1_xattn_Wv, L1_xattn_bv, L1_xattn_Wo, L1_xattn_bo)
    x = x + jnp.tanh(g_ffn[1]) * _L1_ffn_ref(_layernorm(x, axis=-1), L1_ffn_gate_w, L1_ffn_correction_bias, L1_ffn_Wg, L1_ffn_Wu, L1_ffn_Wd, L1_ffn_Wg_s, L1_ffn_Wu_s, L1_ffn_Wd_s)
    return x

_drawn_inputs = setup_inputs


def setup_inputs(seed=0):
    import zlib

    import numpy as np

    out = dict(_drawn_inputs(seed))
    spreads = {'g_ffn': (-1.0, 0.6),
     'L0_xattn_ln_gamma': (1.0, 0.2),
     'L0_xattn_ln_beta': (0.0, 0.1),
     'L0_xattn_b_out': (0.0, 0.546),
     'L0_ffn_rb': (0.0, 0.8),
     'L1_xattn_bq': (0.0, 0.8),
     'L1_xattn_bk': (0.0, 0.8),
     'L1_xattn_bv': (0.0, 0.713),
     'L1_xattn_bo': (0.0, 0.501),
     'L1_ffn_correction_bias': (0.0, 0.8)}
    factors = {'L0_ffn_Wg_s': 8.0,
     'L0_ffn_Wu_s': 8.0,
     'L0_ffn_Wd_s': 8.0,
     'L0_ffn_Wg': 8.0,
     'L0_ffn_Wu': 8.0,
     'L0_ffn_Wd': 8.0,
     'L0_ffn_Wr': 8.0,
     'L1_xattn_Wq': 8.0,
     'L1_xattn_Wk': 8.0,
     'L1_xattn_Wv': 4.528,
     'L1_xattn_Wo': 3.51,
     'L1_ffn_gate_w': 8.0,
     'L1_ffn_Wg': 8.0,
     'L1_ffn_Wu': 8.0,
     'L1_ffn_Wd': 8.0,
     'L1_ffn_Wg_s': 8.0,
     'L1_ffn_Wu_s': 8.0,
     'L1_ffn_Wd_s': 8.0}
    for name, (base, spread) in spreads.items():
        noise = np.random.default_rng([zlib.crc32(name.encode()), seed]).standard_normal(out[name].shape)
        drawn = base * np.exp(spread * noise) if base else spread * noise
        out[name] = jnp.asarray(drawn.astype(out[name].dtype))
    for name, factor in factors.items():
        out[name] = (out[name] * factor).astype(out[name].dtype)
    return out
```

```python
from contextlib import ExitStack

import concourse.bass as bass
from concourse import mybir

F32 = mybir.dt.float32
I32 = mybir.dt.int32
ALU = mybir.AluOpType
ACT = mybir.ActivationFunctionType
AX_X = mybir.AxisListType.X

B, S, D = 64, 128, 128
SC = 120
H, DH = 16, 64
HD = H * DH
MT = HD // 128
NB = 4
G = B // NB
T = NB * S
TC = NB * SC
E = 8
I0 = 256
U0 = E + 1
U1 = E // 2 + 1
LN_EPS = 1e-5
COS_EPS = 1e-8
HALF_LOG_COS_EPS = -9.210340371976182
NORM2_MIN = 1e-19
MASKED = -1e30
ROUTE_SCALE = 2.5

HB = 4
BLK = NB * H // HB
A_BANKS, D_BANKS = 4, 3
RING = 4

A_JOBS = {"N": 0, "L0A": 2 + MT + 2 * NB, "L0B": 0, "L1": 2 + 2 * MT + BLK + 2 * NB, "F0": 1 + 2 * U0, "F1": 1 + U1}
D_JOBS = {"N": 0, "L0A": 2 * NB + 1, "L0B": BLK + 2 * NB, "L1": 2 * NB + BLK, "F0": 2 * U0 + U0, "F1": U1 + 2 * (U1 - 1) + 1}
M_JOBS = {"N": 0, "L0A": 1, "L0B": 1, "L1": 1, "F0": 1, "F1": 1}
LN1 = {"stat": NB, "aggr": NB, "rstd": 2}
RAISED = {
    "N": {"stat": 2 * NB, "aggr": 2 * NB, "rstd": 9, "xn0": 2 * NB, "x_in": 16, "c_in": 16},
    "L0A": {"vsq": NB, "kn2": NB, "qsq": MT, "nrm": 8, "logs": 2, "scr": 16, "vs": NB},
    "L0B": LN1 | {"xn1": NB, "zadd": BLK, "tanh": BLK, "res": 1, "zq_in": 16 * BLK // RING, "ab_in": 32 * NB},
    "L1": LN1 | {"xn3": NB, "mask": 2, "rmax": BLK, "sub": BLK, "exp": BLK, "rsum": 2 * BLK, "pnorm": BLK, "res": 1},
    "F0": LN1 | {"xn2": NB, "route": 7, "gate": 1, "craw_in": 16, "mask_in": 16},
    "F1": {"route": 20, "gate": 1, "out": 16, "added": 3 * 2 * (U1 - 1)},
}
for _s in RAISED:
    RAISED[_s] = RAISED[_s] | {"a_full": A_JOBS[_s], "a_done": A_JOBS[_s], "d_full": D_JOBS[_s], "d_done": D_JOBS[_s],
                               "m_full": M_JOBS[_s], "m_done": M_JOBS[_s]}

FIRST = [("N", 0), ("L0A", 0), ("L0B", 0), ("N", 1), ("F0", 0), ("L0A", 1)]
LOOP = [("L0B", 1), ("L1", 0), ("N", 2), ("F0", 1), ("L0A", 2), ("F1", 0)]
LAST = [("L0B", 1), ("L1", 0), ("F0", 1), ("F1", 0), ("L1", 1), ("F1", 1)]
TRIPS = G - 2


def raised(stages, sem):
    return sum(RAISED[s].get(sem, 0) for s, _ in stages)


class At:

    def __init__(self, section, index, t):
        self.section, self.index, self.t = section, index, t

    def __call__(self, sem, k=0):
        if self.section is FIRST:
            return raised(FIRST[: self.index], sem) + k
        if self.section is LOOP:
            each = raised(LOOP, sem)
            n = raised(FIRST, sem) + raised(LOOP[: self.index], sem) + k
            return self.t * each + n if each else n
        return raised(FIRST, sem) + TRIPS * raised(LOOP, sem) + raised(LAST[: self.index], sem) + k


def run_stages(eng, programs):
    for n, (stage, d) in enumerate(FIRST):
        programs[stage](d, At(FIRST, n, 0))
    with eng.Fori(0, TRIPS) as t:
        for n, (stage, d) in enumerate(LOOP):
            programs[stage](t + d, At(LOOP, n, t))
    for n, (stage, d) in enumerate(LAST):
        programs[stage](TRIPS + d, At(LAST, n, 0))


def nothing(g, at):
    pass


def s_job(n):
    return n + sum(1 for k in range(2 * NB) if 2 * k + 3 < n)


def av_job(k):
    return min(2 * k + 4, BLK) + k


T_LAG, AV_LAG = 4, 6


def t_job(n):
    return 2 + 2 * MT + n + sum(1 for k in range(2 * NB) if 2 * k + 1 + AV_LAG - 1 < n + T_LAG)


def ot_job(k):
    return 2 + 2 * MT + min(2 * k + AV_LAG - T_LAG + 1, BLK) + k


def u0_job(u, half):
    return half if u == 0 else 2 + 3 * (u - 1) + half


def y0_job(u):
    return 3 * u + 4 if u < U0 - 1 else 3 * u + 2


def u1_job(u):
    return (0, 1)[u] if u < 2 else 3 * u - 3


def y1_job(u, part=0):
    if u == 0:
        return 2
    return (3 * u + 1 if u < U1 - 1 else 3 * u) + part


def flamingo_kernel(nc, x, ctx_in, mask, g_xattn, g_ffn, ln_gamma, ln_beta, w_in, w_out, b_out,
                    w0g, w0u, w0d, w0r, r0b, wq, bq, wk, bk, wv, bv, wo, bo,
                    w1r, c1b, w1g, w1u, w1d, w1gs, w1us, w1ds, out, scratch):
    with ExitStack() as ctx:
        def sb(name, shape, dt=F32):
            return ctx.enter_context(nc.sbuf_tensor(name, shape, dt))

        def sem(name):
            return ctx.enter_context(nc.semaphore(name))

        win_sb = sb("win_sb", [128, HD])
        wout_sb = sb("wout_sb", [128, MT, D])
        wq_sb = sb("wq_sb", [128, HD])
        wk_sb = sb("wk_sb", [128, HD])
        wv_sb = sb("wv_sb", [128, HD])
        wo_sb = sb("wo_sb", [128, MT, D])
        w0g_sb = sb("w0g_sb", [128, U0, I0])
        w0u_sb = sb("w0u_sb", [128, U0, I0])
        w0d_sb = sb("w0d_sb", [128, U0, 2, D])
        w1g_sb = sb("w1g_sb", [128, U1, 128])
        w1u_sb = sb("w1u_sb", [128, U1, 128])
        w1d_sb = sb("w1d_sb", [128, U1, 2, D])
        w0r_sb = sb("w0r_sb", [128, E])
        w1r_sb = sb("w1r_sb", [128, E])
        r0b_sb = sb("r0b_sb", [128, E])
        c1b_sb = sb("c1b_sb", [128, E])
        bq_sb = sb("bq_sb", [128, MT])
        bk_sb = sb("bk_sb", [128, MT])
        bv_sb = sb("bv_sb", [128, MT])
        gamma_sb = sb("gamma_sb", [128, 1])
        beta_sb = sb("beta_sb", [128, 1])
        bias0_sb = sb("bias0_sb", [128, D])
        bias1_sb = sb("bias1_sb", [128, D])
        gates_in = sb("gates_in", [128, 4])
        gates = sb("gates", [128, 4])
        ident = sb("ident", [128, 128])
        causal = sb("causal", [128, SC])
        halves = sb("halves", [128, 2])
        before = sb("before", [128, E, E])
        before4 = sb("before4", [128, E // 2, E // 2])
        eps4 = sb("eps4", [128, NB])
        minus_half = sb("minus_half", [128, NB])
        x_in = sb("x_in", [128, NB, D])
        c_in = sb("c_in", [SC, NB, D])
        c_raw = sb("c_raw", [SC, NB, D])
        mask_in = sb("mask_in", [128, TC], I32)
        maskb = sb("maskb", [128, NB, SC])
        x1 = sb("x1", [128, NB, D])
        x2 = sb("x2", [128, NB, D])
        x3 = sb("x3", [128, NB, D])
        y_out = sb("y_out", [128, NB, D])
        stats = sb("stats", [128, 2 * NB, 6])
        mv = sb("mv", [128, 2 * NB, 2])
        rst = sb("rst", [128, 10, NB])
        held = sb("held", [128, 1])
        xn = {k: sb(f"xn_{k}", [128, NB, D]) for k in ("L0A", "F0", "L1", "F1")}
        xT = sb("xT", [128, T])
        xTf = sb("xTf", [128, T])
        cT = sb("cT", [128, NB, SC])
        qT = sb("qT", [128, MT, T])
        kz = sb("kz", [128, NB, MT, 2, SC])
        v_sb = sb("v_sb", [SC, NB, HD])
        qsq = sb("qsq", [128, 2, T])
        n2 = sb("n2", [128, 2, NB * H])
        lg2 = sb("lg2", [128, 2, NB * H])
        rn0 = sb("rn0", [128, 2, NB * H])
        nw = sb("nw", [128, 2, NB * H])
        nw2 = sb("nw2", [128, 2, NB * H])
        qrow = sb("qrow", [128, 2, NB * H])
        qrowT = sb("qrowT", [128, 128])
        zk = sb("zk", [SC, NB * H])
        rkh = sb("rkh", [SC, NB * H])
        er = sb("er", [128, RING, HB * S])
        pT_hid = sb("pT_hid", [128, RING * HB * S])
        pT = pT_hid[0:SC, :].rearrange("p (r h q) -> p r h q", r=RING, h=HB)
        hid = pT_hid[:].rearrange("p (u r t) -> p u r t", u=2, r=2)
        ab = sb("ab", [128, 2, NB, S])
        oT = sb("oT", [128, 2, NB, S])
        rmx = sb("rmx", [128, RING, HB])
        rsm = sb("rsm", [128, RING, HB])
        rrc = sb("rrc", [128, RING, HB])
        vsq = sb("vsq", [SC, HD])
        sg = oT[:].rearrange("p a b q -> p a (b q)")
        lgt = sb("lgt", [128, NB, E])
        gth = sb("gth", [128, NB, E])
        prob = sb("prob", [128, NB, E])
        biased = sb("biased", [128, NB, E])
        gsum = sb("gsum", [128, NB, E // 2])
        gsel = sb("gsel", [128, NB, E // 2])
        choice = sb("choice", [128, NB, E])
        cmp_a = sb("cmp_a", [128, NB, E, E])
        cmp_b = sb("cmp_b", [128, NB, E, E])
        rank = sb("rank", [128, NB, E])
        wsel = sb("wsel", [128, NB, E])
        wsum = sb("wsum", [128, NB])
        wrec = sb("wrec", [128, NB])
        cw0 = sb("cw0", [128, NB, E])
        cw1 = sb("cw1", [128, NB, E])

        PA = ctx.enter_context(nc.psum_tensor("PA", [128, A_BANKS, 512], F32))
        PD = ctx.enter_context(nc.psum_tensor("PD", [128, D_BANKS, 512], F32))
        PM = ctx.enter_context(nc.psum_tensor("PM", [128, 512], F32))

        w_attn0 = sem("w_attn0")
        w_small = sem("w_small")
        w_ffn0 = sem("w_ffn0")
        w_attn1 = sem("w_attn1")
        w_ffn1 = sem("w_ffn1")
        const = sem("const")
        gated = sem("gated")
        scaled = sem("scaled")
        bvb = sem("bvb")
        bias1_full = sem("bias1_full")
        a_full, a_done = sem("a_full"), sem("a_done")
        d_full, d_done = sem("d_full"), sem("d_done")
        m_full, m_done = sem("m_full"), sem("m_done")
        x_loaded, c_loaded = sem("x_loaded"), sem("c_loaded")
        craw_loaded, mask_loaded = sem("craw_loaded"), sem("mask_loaded")
        stat, aggr, rstd = sem("stat"), sem("aggr"), sem("rstd")
        xn0_ready, xn1_ready, xn2_ready, xn3_ready = sem("xn0_ready"), sem("xn1_ready"), sem("xn2_ready"), sem("xn3_ready")
        vsq_ready, kn2_ready, qsq_ready = sem("vsq_ready"), sem("kn2_ready"), sem("qsq_ready")
        nrm, logs, scr_written = sem("nrm"), sem("logs"), sem("scr_written")
        zq_loaded = [sem(f"zq_loaded{i}") for i in range(RING)]
        ab_loaded = [sem(f"ab_loaded{i}") for i in range(2)]
        zadd, vs_ready, tanh_ready = sem("zadd"), sem("vs_ready"), sem("tanh_ready")
        res = sem("res")
        mask_ready = sem("mask_ready")
        rmax, sub, exp_ready, rsum, pnorm = sem("rmax"), sem("sub"), sem("exp_ready"), sem("rsum"), sem("pnorm")
        route, gate_ready = sem("route"), sem("gate_ready")
        added = sem("added")
        out_written = sem("out_written")

        x_g = x.rearrange("(g b) s d -> g s b d", b=NB)
        c_g = ctx_in.rearrange("(g b) s d -> g s b d", b=NB)
        out_g = out.rearrange("(g b) s d -> g s b d", b=NB)
        mask_g = mask.rearrange("(g b) s -> g (b s)", b=NB)

        SMALL = [(gamma_sb[:], ln_gamma.rearrange("(p a) -> p a", a=1)), (beta_sb[:], ln_beta.rearrange("(p a) -> p a", a=1)),
                 (gates_in[:, 0:2], g_xattn.rearrange("(a n) -> a n", a=1).broadcast_to([128, 2])),
                 (gates_in[:, 2:4], g_ffn.rearrange("(a n) -> a n", a=1).broadcast_to([128, 2])),
                 (bias0_sb[:], b_out.rearrange("(a n) -> a n", a=1).broadcast_to([128, D])),
                 (bias1_sb[:], bo.rearrange("(a n) -> a n", a=1).broadcast_to([128, D])),
                 (r0b_sb[:], r0b.rearrange("(a n) -> a n", a=1).broadcast_to([128, E])),
                 (c1b_sb[:], c1b.rearrange("(a n) -> a n", a=1).broadcast_to([128, E])),
                 (bq_sb[:], bq), (bk_sb[:], bk), (bv_sb[:], bv), (w0r_sb[:], w0r), (w1r_sb[:], w1r)]
        N_SMALL = 16 * len(SMALL)
        N_FFN1 = 16 * 9

        block = ctx.enter_context(nc.Block())

        @block.sync
        def _(sp):
            for dst, src in SMALL:
                sp.dma_start(dst, src).then_inc(w_small, 16)

            def s_n(g, at):
                if at.section is LOOP:
                    sp.wait_ge(res, at("res", -1))
                elif at.index:
                    sp.wait_ge(res, at("res"))
                sp.dma_start(x_in[:], x_g[g]).then_inc(x_loaded, 16)
                sp.dma_start(c_in[:], c_g[g]).then_inc(c_loaded, 16)

            def load_logs(g, n):
                sp.dma_start(er[0:SC, n % RING, :].rearrange("p (h q) -> p h q", h=HB),
                             scratch[g, n * HB:(n + 1) * HB, :].unsqueeze(0)
                             .broadcast_to([SC, HB, S])).then_inc(zq_loaded[n % RING], 16)

            def s_l0a(g, at):
                if at.section is FIRST and at.index == 1:
                    sp.dma_start(win_sb[:], w_in).then_inc(w_attn0, 16)
                    sp.dma_start(wout_sb[:], w_out).then_inc(w_attn0, 16)
                    sp.dma_start(w0g_sb[:], w0g).then_inc(w_ffn0, 16)
                    sp.dma_start(w0u_sb[:], w0u).then_inc(w_ffn0, 16)
                    sp.dma_start(w0d_sb[:], w0d).then_inc(w_ffn0, 16)
                if at.section is FIRST and at.index > 1:
                    for dst, src in ((wq_sb, wq), (wk_sb, wk), (wv_sb, wv), (wo_sb, wo)):
                        sp.dma_start(dst[:], src).then_inc(w_attn1, 16)
                    sp.dma_start(w1g_sb[:, 0:U1 - 1, :], w1g).then_inc(w_ffn1, 16)
                    sp.dma_start(w1u_sb[:, 0:U1 - 1, :], w1u).then_inc(w_ffn1, 16)
                    sp.dma_start(w1g_sb[:, U1 - 1, 0:64], w1gs).then_inc(w_ffn1, 16)
                    sp.dma_start(w1u_sb[:, U1 - 1, 0:64], w1us).then_inc(w_ffn1, 16)
                    for p in range(2):
                        sp.dma_start(w1d_sb[64 * p:64 * p + 64, 0:U1 - 1, p, :], w1d[p]).then_inc(w_ffn1, 16)
                    sp.dma_start(w1d_sb[0:64, U1 - 1, 0, :], w1ds).then_inc(w_ffn1, 16)
                sp.wait_ge(d_done, at("d_done", D_JOBS["L0A"]))
                sp.dma_start(scratch[g], qrowT[:]).then_inc(scr_written, 16)
                sp.wait_ge(scr_written, at("scr", 16))
                for n in range(RING):
                    load_logs(g, n)

            def s_l0b(g, at):
                for k in range(2 * NB):
                    if k >= 2:
                        sp.wait_ge(d_done, at("d_done", av_job(k - 2) + 1))
                    rows = scratch[g, NB * H + k * 8:NB * H + k * 8 + 8, :].rearrange("(m r) q -> r m q", r=2)
                    for p in range(2):
                        sp.dma_start(ab[64 * p:64 * p + 64, k % 2, :, :],
                                     rows[p].unsqueeze(0).broadcast_to([64, NB, S])).then_inc(ab_loaded[k % 2], 16)
                    for n in (2 * k + RING, 2 * k + RING + 1):
                        if n < BLK:
                            sp.wait_ge(d_done, at("d_done", s_job(n - RING) + 1))
                            load_logs(g, n)

            def s_f0(g, at):
                if at.section is not FIRST:
                    sp.wait_ge(mask_ready, at("mask"))
                    sp.wait_ge(a_done, at("a_done"))
                sp.dma_start(c_raw[:], c_g[g]).then_inc(craw_loaded, 16)
                sp.dma_start(mask_in[:], mask_g[g].rearrange("(a n) -> a n", a=1).broadcast_to([128, TC])).then_inc(mask_loaded, 16)

            def s_f1(g, at):
                sp.wait_ge(d_done, at("d_done", D_JOBS["F1"]))
                sp.dma_start(out_g[g], y_out[:]).then_inc(out_written, 16)

            run_stages(sp, {"N": s_n, "L0A": s_l0a, "L0B": s_l0b, "L1": nothing, "F0": s_f0, "F1": s_f1})
            sp.wait_ge(out_written, 16 * G)
            sp.wait_ge(scr_written, 16 * G)

        N_CONST = 16

        @block.gpsimd
        def _(pool):
            for tile, value in ((ident, 0.0), (causal, 0.0), (halves, 0.0), (before, 1.0), (before4, 1.0),
                                (eps4, LN_EPS), (minus_half, -0.5), (w1d_sb, 0.0), (n2, 1.0)):
                pool.memset(tile[:], value).then_inc(const, 1)
            pool.memset(kz[:], 0.0).then_inc(const, 1)
            pool.wait_ge(const, 10)
            pool.affine_select(out=ident[:], in_=ident[:], compare_op=ALU.not_equal, fill=1.0, base=0,
                               pattern=[[-1, 128]], channel_multiplier=1).then_inc(const, 1)
            pool.affine_select(out=causal[:], in_=causal[:], compare_op=ALU.is_ge, fill=MASKED, base=0,
                               pattern=[[-1, SC]], channel_multiplier=1).then_inc(const, 1)
            pool.wait_ge(const, 12)
            pool.memset(halves[0:64, 0:1], 1.0).then_inc(const, 1)
            pool.wait_ge(const, 13)
            pool.memset(halves[64:128, 1:2], 1.0).then_inc(const, 1)
            pool.wait_ge(const, 14)
            pool.affine_select(out=before[:], in_=before[:], compare_op=ALU.is_ge, fill=0.0, base=-1,
                               pattern=[[1, E], [-1, E]], channel_multiplier=0).then_inc(const, 1)
            pool.affine_select(out=before4[:], in_=before4[:], compare_op=ALU.is_ge, fill=0.0, base=-1,
                               pattern=[[1, E // 2], [-1, E // 2]], channel_multiplier=0).then_inc(const, 1)
            pool.wait_ge(const, N_CONST)

            def rstd_of(at, k, n, src, dst, parts=128):
                pool.tensor_tensor(rst[0:parts, dst, :], src, eps4[0:parts, :], ALU.add).then_inc(rstd, 1)
                pool.wait_ge(rstd, at("rstd", k + 1))
                pool.tensor_tensor(rst[0:parts, dst, :], rst[0:parts, dst, :], minus_half[0:parts, :], ALU.pow).then_inc(rstd, 1)

            def p_n(g, at):
                pool.wait_ge(aggr, at("aggr", NB))
                rstd_of(at, 0, 2, mv[:, 0:NB, 1], 0)
                pool.wait_ge(rstd, at("rstd", 2))
                pool.tensor_tensor(rst[:, 1, :], rst[:, 0, :], rst[:, 0, :], ALU.mult).then_inc(rstd, 1)
                pool.wait_ge(rstd, at("rstd", 3))
                pool.tensor_tensor(rst[:, 1, :], rst[:, 1, :], mv[:, 0:NB, 1], ALU.mult).then_inc(rstd, 1)
                pool.wait_ge(rstd, at("rstd", 4))
                rstd_of(at, 4, 2, rst[:, 1, :], 2)
                pool.wait_ge(rstd, at("rstd", 6))
                pool.tensor_tensor(rst[:, 3, :], rst[:, 2, :], rst[:, 0, :], ALU.mult).then_inc(rstd, 1)
                pool.wait_ge(aggr, at("aggr", 2 * NB))
                rstd_of(at, 7, 2, mv[0:SC, NB:2 * NB, 1], 4, SC)

            def p_ln(at, slot):
                pool.wait_ge(aggr, at("aggr", NB))
                rstd_of(at, 0, 2, mv[:, 0:NB, 1], slot)

            def p_l0a(g, at):
                for m in range(MT):
                    pool.wait_ge(a_done, at("a_done", 2 + m + 1))
                    if m >= 2:
                        pool.wait_ge(a_full, at("a_full", 2 + m + 2))
                    pool.tensor_tensor(qsq[:, m % 2, :], qT[:, m, :], qT[:, m, :], ALU.mult).then_inc(qsq_ready, 1)

                pool.wait_ge(nrm, at("nrm", 7))
                pool.wait_ge(a_done, at("a_done", A_JOBS["L0A"]))
                for b in range(NB):
                    val = v_sb[:, b, :].rearrange("p (h d) -> p h d", h=H)
                    pool.tensor_tensor(val, val, rkh[:, b * H:(b + 1) * H].unsqueeze(2).broadcast_to([SC, H, DH]),
                                       ALU.mult).then_inc(vs_ready, 1)

            def p_l0b(g, at):
                pool.wait_ge(nrm, at("nrm"))
                for n in range(BLK):
                    pool.wait_ge(zq_loaded[n % RING], at("zq_in", 16 * (n // RING + 1)))
                    blk = er[0:SC, n % RING, :].rearrange("p (h q) -> p h q", h=HB)
                    pool.tensor_tensor(blk, blk, zk[:, n * HB:(n + 1) * HB].unsqueeze(2).broadcast_to([SC, HB, S]),
                                       ALU.add).then_inc(zadd, 1)
                p_ln(at, 5)

            def p_l1(g, at):
                for s in range(BLK + 2):
                    if s < BLK:
                        blk = er[:, s % RING, 0:HB * SC].rearrange("p (h k) -> p h k", h=HB)
                        pool.wait_ge(rmax, at("rmax", s + 1))
                        pool.tensor_tensor(blk, blk, rmx[:, s % RING, :].unsqueeze(2).broadcast_to([128, HB, SC]),
                                           ALU.subtract).then_inc(sub, 1)
                    if s >= 2:
                        n = s - 2
                        blk = er[:, n % RING, 0:HB * SC].rearrange("p (h k) -> p h k", h=HB)
                        pool.wait_ge(rsum, at("rsum", 2 * n + 2))
                        pool.tensor_tensor(blk, blk, rrc[:, n % RING, :].unsqueeze(2).broadcast_to([128, HB, SC]),
                                           ALU.mult).then_inc(pnorm, 1)
                p_ln(at, 6)

            def p_f0(g, at):
                p_ln(at, 7)

            run_stages(pool, {"N": p_n, "L0A": p_l0a, "L0B": p_l0b, "L1": p_l1, "F0": p_f0, "F1": nothing})

        @block.scalar
        def _(act):
            act.wait_ge(w_small, N_SMALL)
            nc.scalar.activation(gates[:], gates_in[:], ACT.Tanh).then_inc(gated, 1)

            def bank(at, k):
                act.wait_ge(a_full, at("a_full", k + 1))
                return PA[:, k % A_BANKS, :]

            def a_l0a(g, at):
                nc.scalar.activation(xT[:], bank(at, 0), ACT.Identity, bias=beta_sb[:, 0:1],
                                     scale=gamma_sb[:, 0:1]).then_inc(a_done, 1)
                nc.scalar.activation(cT[:], bank(at, 1)[:, 0:TC].rearrange("p (b k) -> p b k", b=NB), ACT.Identity,
                                     bias=beta_sb[:, 0:1], scale=gamma_sb[:, 0:1]).then_inc(a_done, 1)

                def square(b):
                    act.wait_ge(d_done, at("d_done", 2 * b + 2))
                    if b >= 1:
                        act.wait_ge(kn2_ready, at("kn2", b))
                    nc.scalar.activation(vsq[:], v_sb[:, b, :], ACT.Square).then_inc(vsq_ready, 1)

                for m in range(MT):
                    nc.scalar.activation(qT[:, m, :], bank(at, 2 + m), ACT.Copy).then_inc(a_done, 1)
                    if m >= 3 and m % 2 == 1:
                        square((m - 3) // 2)
                square(NB - 1)
                for j in range(2 * NB):
                    b, t0 = j // 2, 4 * (j % 2)
                    src = bank(at, 2 + MT + j)[:, 0:4 * SC].rearrange("p (t k) -> p t k", t=4)
                    nc.scalar.activation(kz[0:64, b, t0:t0 + 4, 0, :], src[0:64], ACT.Copy)
                    nc.scalar.activation(kz[64:128, b, t0:t0 + 4, 1, :], src[64:128], ACT.Copy).then_inc(a_done, 1)
                act.wait_ge(nrm, at("nrm", 2))
                nc.scalar.activation(lg2[:], n2[:], ACT.Ln).then_inc(logs, 1)
                act.wait_ge(logs, at("logs", 1))
                nc.scalar.activation(rn0[:], lg2[:], ACT.Exp, scale=-0.5).then_inc(logs, 1)

            def a_l0b(g, at):
                for n in range(BLK):
                    act.wait_ge(zadd, at("zadd", n + 1))
                    nc.scalar.activation(er[0:SC, n % RING, :], er[0:SC, n % RING, :], ACT.Tanh).then_inc(tanh_ready, 1)

            def a_l1(g, at):
                act.wait_ge(w_small, N_SMALL)
                nc.scalar.activation(xT[:], bank(at, 0), ACT.Copy).then_inc(a_done, 1)
                nc.scalar.activation(cT[:], bank(at, 1)[:, 0:TC].rearrange("p (b k) -> p b k", b=NB),
                                     ACT.Copy).then_inc(a_done, 1)
                for m in range(MT):
                    nc.scalar.activation(qT[:, m, :], bank(at, 2 + 2 * m), ACT.Identity,
                                         bias=bq_sb[:, m:m + 1]).then_inc(a_done, 1)
                    src = bank(at, 3 + 2 * m)[:, 0:TC].rearrange("p (b k) -> p b k", b=NB)
                    nc.scalar.activation(kz[0:64, :, m, 0, :], src[0:64], ACT.Identity, bias=bk_sb[0:64, m:m + 1])
                    nc.scalar.activation(kz[64:128, :, m, 1, :], src[64:128], ACT.Identity,
                                         bias=bk_sb[64:128, m:m + 1]).then_inc(a_done, 1)
                for s in range(BLK + AV_LAG):
                    if 1 <= s <= BLK:
                        n = s - 1
                        act.wait_ge(sub, at("sub", n + 1))
                        nc.scalar.activation(er[:, n % RING, 0:HB * SC], er[:, n % RING, 0:HB * SC], ACT.Exp,
                                             scale=DH ** -0.5).then_inc(exp_ready, 1)
                    if T_LAG <= s < BLK + T_LAG:
                        n = s - T_LAG
                        nc.scalar.activation(pT[:, n % RING, :, :], bank(at, t_job(n))[0:SC, :].rearrange(
                            "p (h q) -> p h q", h=HB), ACT.Copy).then_inc(a_done, 1)
                    if s >= AV_LAG and (s - AV_LAG) % 2 == 0:
                        k = (s - AV_LAG) // 2
                        nc.scalar.activation(oT[:, k % 2, :, :], bank(at, ot_job(k)).rearrange("p (m q) -> p m q", m=NB),
                                             ACT.Copy).then_inc(a_done, 1)

            def a_f0(g, at):
                nc.scalar.activation(xTf[:], bank(at, 0), ACT.Copy).then_inc(a_done, 1)
                act.wait_ge(m_done, at("m_done", 1))
                nc.scalar.activation(gth[:], lgt[:], ACT.Tanh, scale=0.5).then_inc(gate_ready, 1)
                for j in range(2 * U0):
                    if j >= 2:
                        act.wait_ge(d_done, at("d_done", u0_job((j - 2) // 2, j % 2) + 1))
                    nc.scalar.activation(sg[:, j % 2, :], bank(at, 1 + j), ACT.Silu).then_inc(a_done, 1)

            def a_f1(g, at):
                nc.scalar.activation(xTf[:], bank(at, 0), ACT.Copy).then_inc(a_done, 1)
                act.wait_ge(m_done, at("m_done", 1))
                nc.scalar.activation(gth[:], lgt[:], ACT.Tanh, scale=0.5).then_inc(gate_ready, 1)
                for j in range(U1):
                    if j >= 2:
                        act.wait_ge(d_done, at("d_done", u1_job(j - 2) + 1))
                    parts = 64 if j == 0 else 128
                    nc.scalar.activation(sg[0:parts, j % 2, :], bank(at, 1 + j)[0:parts, :], ACT.Silu).then_inc(a_done, 1)

            run_stages(act, {"N": nothing, "L0A": a_l0a, "L0B": a_l0b, "L1": a_l1, "F0": a_f0, "F1": a_f1})

        @block.vector
        def _(dve):
            dve.wait_ge(const, N_CONST)
            dve.wait_ge(gated, 1)
            dve.wait_ge(w_attn0, 32)
            nc.vector.tensor_scalar(wout_sb[:], wout_sb[:], gates[:, 0:1], 0.5, ALU.mult, ALU.mult).then_inc(scaled, 1)
            nc.vector.tensor_scalar(bias0_sb[:], bias0_sb[:], gates[:, 0:1], None, ALU.mult).then_inc(scaled, 1)
            nc.vector.tensor_scalar(bias1_sb[:], bias1_sb[:], gates[:, 1:2], None, ALU.mult).then_inc(scaled, 1)

            def scale_ffn0():
                dve.wait_ge(w_ffn0, 48)
                nc.vector.tensor_scalar(w0d_sb[:], w0d_sb[:], gates[:, 2:3], None, ALU.mult).then_inc(scaled, 1)

            def scale_rest():
                dve.wait_ge(w_attn1, 64)
                nc.vector.tensor_scalar(wo_sb[:], wo_sb[:], gates[:, 1:2], None, ALU.mult).then_inc(scaled, 1)
                for m in range(MT):
                    nc.vector.tensor_copy(oT[:].rearrange("p a b q -> p (a b) q")[:, m, :],
                                          bv_sb[:, m:m + 1].broadcast_to([128, 128])).then_inc(bvb, 1)
                dve.wait_ge(w_ffn1, 16 * 7)
                nc.vector.tensor_scalar(w1d_sb[:], w1d_sb[:], gates[:, 3:4], None, ALU.mult).then_inc(scaled, 1)
                dve.wait_ge(bias1_full, 1)
                nc.vector.tensor_tensor(bias1_sb[:], PM[:, 0:D], bias1_sb[:], ALU.add).then_inc(scaled, 1)

            def bank(at, k):
                dve.wait_ge(d_full, at("d_full", k + 1))
                return PD[:, k % D_BANKS, :]

            def row_stats(at, k, src, slot, parts):
                for b in range(NB):
                    nc.vector.bn_stats(stats[0:parts, slot + b, :], src[:, b, :]).then_inc(stat, 1)
                dve.wait_ge(stat, at("stat", k + NB))
                nc.vector.tensor_copy(held[0:parts, :], stats[0:parts, slot, 0:1])
                for b in range(NB):
                    nc.vector.bn_aggr(mv[0:parts, slot + b, :], stats[0:parts, slot + b, :]).then_inc(aggr, 1)

            def normalise(src, dst, slot, r, parts, ready):
                for b in range(NB):
                    nc.vector.tensor_scalar(dst[:, b, :], src[:, b, :], mv[0:parts, slot + b, 0:1],
                                            rst[0:parts, r, b:b + 1], ALU.subtract, ALU.mult).then_inc(ready, 1)

            def v_n(g, at):
                dve.wait_ge(x_loaded, at("x_in", 16))
                row_stats(at, 0, x_in, 0, 128)
                dve.wait_ge(c_loaded, at("c_in", 16))
                row_stats(at, NB, c_in, NB, SC)
                dve.wait_ge(rstd, at("rstd", 7))
                normalise(x_in, xn["L0A"], 0, 3, 128, xn0_ready)
                dve.wait_ge(rstd, at("rstd", 9))
                normalise(c_in, c_in, NB, 4, SC, xn0_ready)

            def v_l0a(g, at):
                def key_norms(b):
                    dve.wait_ge(vsq_ready, at("vsq", b + 1))
                    nc.vector.tensor_reduce(nw[0:SC, 1, b * H:(b + 1) * H],
                                            vsq[:].rearrange("p (h d) -> p h d", h=H), AX_X, ALU.add).then_inc(kn2_ready, 1)

                for j in range(2 * NB):
                    b, half = j // 2, j % 2
                    nc.vector.tensor_copy(v_sb[:, b, half * 512:half * 512 + 512], bank(at, j)[0:SC, :]).then_inc(d_done, 1)
                    if j >= 4 and j % 2 == 0:
                        key_norms((j - 4) // 2)
                key_norms(NB - 2)
                key_norms(NB - 1)
                dve.wait_ge(kn2_ready, at("kn2", NB))
                nc.vector.tensor_scalar(n2[0:SC, 1, :], nw[0:SC, 1, :], NORM2_MIN, None, ALU.max).then_inc(nrm, 1)
                dve.wait_ge(m_full, at("m_full", 1))
                nc.vector.tensor_scalar(n2[:, 0, :], PM[:, 0:NB * H], NORM2_MIN, None, ALU.max).then_inc(m_done, 1)
                dve.wait_ge(m_done, at("m_done", 1))
                nc.vector.tensor_scalar(nw[:], n2[:], -0.5, None, ALU.mult).then_inc(nrm, 1)
                dve.wait_ge(logs, at("logs", 2))
                dve.wait_ge(nrm, at("nrm", 2))
                nc.vector.tensor_tensor(nw2[:], rn0[:], rn0[:], ALU.mult).then_inc(nrm, 1)
                dve.wait_ge(nrm, at("nrm", 3))
                nc.vector.tensor_tensor(nw2[:], nw2[:], nw[:], ALU.mult).then_inc(nrm, 1)
                nc.vector.tensor_scalar(qrow[:, 0, :], lg2[:, 0, :], 0.25, None, ALU.mult).then_inc(nrm, 1)
                dve.wait_ge(nrm, at("nrm", 5))
                nc.vector.scalar_tensor_tensor(qrow[:, 1, :], nw2[:, 0, :], 1.5, rn0[:, 0, :], ALU.add, ALU.mult).then_inc(nrm, 1)
                nc.vector.scalar_tensor_tensor(rkh[:], nw2[0:SC, 1, :], 1.5, rn0[0:SC, 1, :], ALU.add, ALU.mult).then_inc(nrm, 1)
                nc.vector.tensor_scalar(zk[:], lg2[0:SC, 1, :], 0.25, -HALF_LOG_COS_EPS, ALU.mult, ALU.add).then_inc(nrm, 1)
                nc.vector.tensor_copy(qrowT[:], bank(at, 2 * NB)[:, 0:128]).then_inc(d_done, 1)

            def residual(at, src, bias, dst):
                dve.wait_ge(m_full, at("m_full", 1))
                nc.vector.tensor_tensor(dst[:], PM[:].rearrange("p (b d) -> p b d", b=NB), src[:], ALU.add).then_inc(m_done, 1)
                dve.wait_ge(m_done, at("m_done", 1))
                nc.vector.tensor_tensor(dst[:], dst[:], bias[:].unsqueeze(1).broadcast_to([128, NB, D]), ALU.add).then_inc(res, 1)
                dve.wait_ge(res, at("res", 1))

            def norm_of(at, src, dst, r, ready):
                row_stats(at, 0, src, 0, 128)
                dve.wait_ge(rstd, at("rstd", 2))
                normalise(src, dst, 0, r, 128, ready)

            def v_l0b(g, at):
                dve.wait_ge(scaled, 3)
                for s in range(BLK + 4):
                    if s < BLK:
                        dve.wait_ge(tanh_ready, at("tanh", s + 1))
                        nc.vector.scalar_tensor_tensor(pT[:, s % RING, :, :].rearrange("p h q -> p (h q)"),
                                                       er[0:SC, s % RING, :], 1.0, bank(at, s_job(s))[0:SC, :],
                                                       ALU.add, ALU.mult).then_inc(d_done, 1)
                    if s >= 3 and s % 2 == 1 and (s - 3) // 2 < 2 * NB:
                        k = (s - 3) // 2
                        dve.wait_ge(ab_loaded[k % 2], at("ab_in", 32 * (k // 2 + 1)))
                        nc.vector.tensor_tensor(oT[:, k % 2, :, :], bank(at, av_job(k)).rearrange("p (m q) -> p m q", m=NB),
                                                ab[:, k % 2, :, :], ALU.mult).then_inc(d_done, 1)
                residual(at, x_in, bias0_sb, x1)
                norm_of(at, x1, xn["F0"], 5, xn1_ready)

            def v_l1(g, at):
                for j in range(2 * NB):
                    b, half = j // 2, j % 2
                    nc.vector.tensor_copy(v_sb[:, b, half * 512:half * 512 + 512], bank(at, j)[0:SC, :]).then_inc(d_done, 1)
                dve.wait_ge(mask_loaded, at("mask_in"))
                nc.vector.tensor_scalar(maskb[:].rearrange("p b k -> p (b k)"), mask_in[:], 0.0, MASKED,
                                        ALU.is_equal, ALU.mult).then_inc(mask_ready, 1)
                dve.wait_ge(mask_ready, at("mask", 1))
                nc.vector.tensor_tensor(maskb[:], maskb[:], causal[:].unsqueeze(1).broadcast_to([128, NB, SC]),
                                        ALU.add).then_inc(mask_ready, 1)
                dve.wait_ge(mask_ready, at("mask", 2))
                for s in range(BLK + 2):
                    if s < BLK:
                        n, b = s, s * HB // H
                        blk = er[:, n % RING, 0:HB * SC].rearrange("p (h k) -> p h k", h=HB)
                        if n >= RING:
                            dve.wait_ge(a_full, at("a_full", t_job(n - RING) + 1))
                        nc.vector.tensor_tensor(blk, bank(at, 2 * NB + n)[:, 0:HB * SC].rearrange("p (h k) -> p h k", h=HB),
                                                maskb[:, b, :].unsqueeze(1).broadcast_to([128, HB, SC]),
                                                ALU.add).then_inc(d_done, 1)
                        dve.wait_ge(d_done, at("d_done", 2 * NB + n + 1))
                        nc.vector.tensor_reduce(rmx[:, n % RING, :], blk, AX_X, ALU.max).then_inc(rmax, 1)
                    if s >= 2:
                        n = s - 2
                        blk = er[:, n % RING, 0:HB * SC].rearrange("p (h k) -> p h k", h=HB)
                        dve.wait_ge(exp_ready, at("exp", n + 1))
                        nc.vector.tensor_reduce(rsm[:, n % RING, :], blk, AX_X, ALU.add).then_inc(rsum, 1)
                        dve.wait_ge(rsum, at("rsum", 2 * n + 1))
                        nc.vector.reciprocal(rrc[:, n % RING, :], rsm[:, n % RING, :]).then_inc(rsum, 1)
                residual(at, x2, bias1_sb, x3)
                norm_of(at, x3, xn["F1"], 6, xn3_ready)

            def ranks(at, k, scores, tri, n, beats, ties):
                mine = scores[:, :, 0:n].unsqueeze(3).broadcast_to([128, NB, n, n])
                other = scores[:, :, 0:n].unsqueeze(2).broadcast_to([128, NB, n, n])
                tri_b = tri[:].unsqueeze(1).broadcast_to([128, NB, n, n])
                nc.vector.tensor_tensor(beats, other, mine, ALU.is_gt).then_inc(route, 1)
                nc.vector.tensor_tensor(ties, other, mine, ALU.is_ge).then_inc(route, 1)
                dve.wait_ge(route, at("route", k + 2))
                nc.vector.tensor_tensor(ties, ties, tri_b, ALU.mult).then_inc(route, 1)
                dve.wait_ge(route, at("route", k + 3))
                nc.vector.tensor_tensor(beats, beats, ties, ALU.max).then_inc(route, 1)
                dve.wait_ge(route, at("route", k + 4))
                nc.vector.tensor_reduce(rank[:, :, 0:n], beats, AX_X, ALU.add).then_inc(route, 1)
                dve.wait_ge(route, at("route", k + 5))

            def logits(at, bias, k):
                dve.wait_ge(m_full, at("m_full", 1))
                nc.vector.tensor_tensor(lgt[:], PM[:, 0:NB * E].rearrange("p (b e) -> p b e", b=NB), bias, ALU.add).then_inc(m_done, 1)

            def probabilities(at):
                dve.wait_ge(gate_ready, at("gate", 1))
                nc.vector.tensor_scalar(prob[:], gth[:], 0.5, 0.5, ALU.mult, ALU.add).then_inc(route, 1)
                dve.wait_ge(route, at("route", 1))

            def flat(tile):
                return tile[:].rearrange("p b e -> p (b e)")

            def router0(at):
                probabilities(at)
                ranks(at, 1, prob, before, E, cmp_a[:], cmp_b[:])
                nc.vector.scalar_tensor_tensor(flat(cw0), flat(rank), 2.0, flat(prob), ALU.is_lt, ALU.mult).then_inc(route, 1)
                dve.wait_ge(route, at("route", 7))

            def router1(at):
                probabilities(at)
                nc.vector.tensor_tensor(biased[:], prob[:], c1b_sb[:].unsqueeze(1).broadcast_to([128, NB, E]),
                                        ALU.add).then_inc(route, 1)
                dve.wait_ge(route, at("route", 2))
                pairs = biased[:].rearrange("p b (n r) -> p b n r", r=2)
                nc.vector.tensor_tensor(gsum[:], pairs[:, :, :, 0], pairs[:, :, :, 1], ALU.add).then_inc(route, 1)
                dve.wait_ge(route, at("route", 3))
                ranks(at, 3, gsum, before4, E // 2, cmp_a[:, :, 0:E // 2, 0:E // 2], cmp_b[:, :, 0:E // 2, 0:E // 2])
                nc.vector.tensor_scalar(gsel[:], rank[:, :, 0:E // 2], 2.0, None, ALU.is_lt).then_inc(route, 1)
                dve.wait_ge(route, at("route", 9))
                nc.vector.tensor_tensor(choice[:].rearrange("p b (n r) -> p b n r", r=2), pairs,
                                        gsel[:].unsqueeze(3).broadcast_to([128, NB, E // 2, 2]), ALU.mult).then_inc(route, 1)
                dve.wait_ge(route, at("route", 10))
                ranks(at, 10, choice, before, E, cmp_a[:], cmp_b[:])
                nc.vector.scalar_tensor_tensor(flat(wsel), flat(rank), 4.0, flat(prob), ALU.is_lt, ALU.mult).then_inc(route, 1)
                dve.wait_ge(route, at("route", 16))
                nc.vector.tensor_reduce(wsum[:], wsel[:], AX_X, ALU.add).then_inc(route, 1)
                dve.wait_ge(route, at("route", 17))
                nc.vector.tensor_scalar(wrec[:], wsum[:], 1e-20, 1 / ROUTE_SCALE, ALU.add, ALU.mult).then_inc(route, 1)
                dve.wait_ge(route, at("route", 18))
                nc.vector.reciprocal(wsum[:], wrec[:]).then_inc(route, 1)
                dve.wait_ge(route, at("route", 19))
                nc.vector.tensor_tensor(cw1[:], wsel[:], wsum[:].unsqueeze(2).broadcast_to([128, NB, E]),
                                        ALU.mult).then_inc(route, 1)
                dve.wait_ge(route, at("route", 20))

            def v_f0(g, at):
                if at.section is FIRST:
                    scale_ffn0()
                logits(at, r0b_sb[:].unsqueeze(1).broadcast_to([128, NB, E]), 0)
                for u in range(U0 + 1):
                    if u < U0:
                        for half in range(2):
                            dve.wait_ge(a_done, at("a_done", 2 + 2 * u + half))
                            nc.vector.tensor_tensor(hid[:, u % 2, half, :], bank(at, u0_job(u, half)), sg[:, half, :],
                                                    ALU.mult).then_inc(d_done, 1)
                    if u == 1:
                        router0(at)
                    if u >= 1:
                        y = bank(at, y0_job(u - 1)).rearrange("p (b d) -> p b d", b=NB)
                        if u == 1:
                            nc.vector.tensor_tensor(x2[:], y, x1[:], ALU.add).then_inc(d_done, 1)
                        else:
                            e = u - 2
                            dve.wait_ge(d_done, at("d_done", y0_job(e) + 1))
                            for b in range(NB):
                                add = nc.vector.scalar_tensor_tensor(x2[:, b, :], y[:, b, :], cw0[:, b, e:e + 1],
                                                                     x2[:, b, :], ALU.mult, ALU.add)
                            add.then_inc(d_done, 1)
                dve.wait_ge(d_done, at("d_done", D_JOBS["F0"]))
                norm_of(at, x2, xn["L1"], 7, xn2_ready)

            def v_f1(g, at):
                dve.wait_ge(m_full, at("m_full", 1))
                nc.vector.tensor_copy(lgt[:], PM[:, 0:NB * E].rearrange("p (b e) -> p b e", b=NB)).then_inc(m_done, 1)
                for u in range(U1 + 1):
                    if u < U1:
                        parts = 64 if u == 0 else 128
                        dve.wait_ge(a_done, at("a_done", 2 + u))
                        nc.vector.tensor_tensor(hid[0:parts, u % 2, 0, :], bank(at, u1_job(u))[0:parts, :],
                                                sg[0:parts, u % 2, :], ALU.mult).then_inc(d_done, 1)
                    if u == 1:
                        router1(at)
                        y = bank(at, y1_job(0)).rearrange("p (b d) -> p b d", b=NB)
                        store_taken(g, at)
                        nc.vector.tensor_tensor(y_out[:], y, x3[:], ALU.add).then_inc(d_done, 1)
                    if u >= 2:
                        for part in range(2):
                            dve.wait_ge(d_done, at("d_done", y1_job(u - 2, part if u > 2 else 0) + 1))
                            y = bank(at, y1_job(u - 1, part)).rearrange("p (b e d) -> p b e d", b=2, e=2)
                            for r in range(2):
                                e = 2 * (u - 2) + r
                                for b in range(2):
                                    tile = y_out[:, 2 * part + b, :]
                                    step = nc.vector.scalar_tensor_tensor(tile, y[:, b, r, :], cw1[:, 2 * part + b, e:e + 1],
                                                                          tile, ALU.mult, ALU.add)
                                    last = r == 1 and b == 1
                                    step.then_inc(d_done if last else added, 1)
                                if r == 0:
                                    dve.wait_ge(added, at("added", 3 * (2 * (u - 2) + part) + 2))

            def store_taken(g, at):
                dve.wait_ge(out_written, at("out"))

            def v_l0a_and_rest(g, at):
                v_l0a(g, at)
                if at.section is FIRST and at.index > 1:
                    scale_rest()

            run_stages(dve, {"N": v_n, "L0A": v_l0a_and_rest, "L0B": v_l0b, "L1": v_l1, "F0": v_f0, "F1": v_f1})

        @block.tensor
        def _(pe):
            def a_bank(at, k, needs=0):
                if k == 0:
                    if not (at.section is FIRST and at.index == 1):
                        pe.wait_ge(a_done, at("a_done"))
                elif max(k - A_BANKS + 1, needs) > 0:
                    pe.wait_ge(a_done, at("a_done", max(k - A_BANKS + 1, needs)))
                return PA[:, k % A_BANKS, :]

            def d_bank(at, k, needs=0):
                if k == 0:
                    if not (at.section is FIRST and at.index == 1):
                        pe.wait_ge(d_done, at("d_done"))
                elif max(k - D_BANKS + 1, needs) > 0:
                    pe.wait_ge(d_done, at("d_done", max(k - D_BANKS + 1, needs)))
                return PD[:, k % D_BANKS, :]

            def m_bank(at):
                if not (at.section is FIRST and at.index == 1):
                    pe.wait_ge(m_done, at("m_done"))
                return PM

            def turn_tiles(at, k, src, parts, width):
                dst = a_bank(at, k)
                for b in range(NB):
                    last = pe.transpose(dst[:, b * width:b * width + width], src[:, b, :], ident[0:parts, 0:parts])
                last.then_inc(a_full, 1)

            def head_norms(at, m):
                if m == 0:
                    m_bank(at)
                pe.wait_ge(qsq_ready, at("qsq", m + 1))
                for b in range(NB):
                    last = pe.matmul(PM[:, b * H + 2 * m:b * H + 2 * m + 2], qsq[:, m % 2, b * S:(b + 1) * S], halves[:],
                                     start=True, stop=True)
                if m == MT - 1:
                    last.then_inc(m_full, 1)

            def values(at, k, weights):
                b, half = k // 2, k % 2
                pe.matmul(d_bank(at, k)[0:SC, :], cT[:, b, :], weights[:, half * 512:half * 512 + 512],
                          start=True, stop=True).then_inc(d_full, 1)

            def t_l0a(g, at):
                if at.section is FIRST and at.index == 1:
                    pe.wait_ge(const, N_CONST)
                    pe.wait_ge(w_attn0, 32)
                pe.wait_ge(xn0_ready, at("xn0", -NB))
                turn_tiles(at, 0, xn["L0A"], 128, S)
                pe.wait_ge(xn0_ready, at("xn0"))
                turn_tiles(at, 1, c_in, SC, SC)
                for m in range(MT):
                    pe.matmul(a_bank(at, 2 + m, 1), win_sb[:, m * 128:(m + 1) * 128], xT[:], start=True, stop=True).then_inc(a_full, 1)
                    pe.wait_ge(a_done, at("a_done", 2))
                    values(at, m, win_sb)
                    if m >= 2:
                        head_norms(at, m - 2)
                for j in range(2 * NB):
                    b, t0 = j // 2, 4 * (j % 2)
                    pe.wait_ge(d_done, at("d_done", 2 * b + 2))
                    dst = a_bank(at, 2 + MT + j)
                    for i in range(4):
                        last = pe.transpose(dst[:, i * SC:(i + 1) * SC], v_sb[:, b, (t0 + i) * 128:(t0 + i + 1) * 128],
                                            ident[0:SC, 0:SC])
                    last.then_inc(a_full, 1)
                    if j < 2:
                        head_norms(at, MT - 2 + j)
                pe.wait_ge(nrm, at("nrm", 6))
                pe.transpose(d_bank(at, 2 * NB)[:, 0:128], qrow[:].rearrange("p a b -> p (a b)"), ident[:]).then_inc(d_full, 1)
                if at.section is FIRST and at.index > 1:
                    pe.wait_ge(scaled, 5)
                    pe.wait_ge(bvb, MT)
                    pe.wait_ge(m_done, at("m_done", 1))
                    for m in range(MT):
                        last = pe.matmul(PM[:, 0:D], oT[:].rearrange("p a b q -> p (a b) q")[:, m, :], wo_sb[:, m, :],
                                         start=(m == 0), stop=(m == MT - 1))
                    last.then_inc(bias1_full, 1)
                    pe.wait_ge(scaled, 7)
                    pe.wait_ge(w_small, N_SMALL)

            def attention_out(dst, k):
                b = k // 2
                for i in range(8):
                    h = 8 * (k % 2) + i
                    last = pe.matmul(dst[64 * (i % 2):64 * (i % 2) + 64, (i // 2) * S:(i // 2 + 1) * S],
                                     v_sb[:, b, h * DH:(h + 1) * DH], pT[:, (2 * k + i // 4) % RING, i % 4, :],
                                     start=True, stop=True)
                return last

            def project_out(k, weights):
                b, half = k // 2, k % 2
                for i in range(4):
                    last = pe.matmul(PM[:, b * D:(b + 1) * D], oT[:, k % 2, i, :], weights[:, 4 * half + i, :],
                                     start=(half == 0 and i == 0), stop=(half == 1 and i == 3))
                return last

            def t_l0b(g, at):
                pe.wait_ge(scaled, 3)
                for s in range(BLK + 6):
                    if s < BLK:
                        b = s * HB // H
                        if s == 0:
                            pe.wait_ge(a_done, at("a_done"))
                        dst = d_bank(at, s_job(s))
                        for i in range(HB):
                            h = (s * HB + i) % H
                            last = pe.matmul(dst[0:SC, i * S:(i + 1) * S], kz[:, b, h // 2, h % 2, :],
                                             qT[:, h // 2, b * S:(b + 1) * S], start=True, stop=True)
                        last.then_inc(d_full, 1)
                    if s >= 5 and s % 2 == 1 and (s - 5) // 2 < 2 * NB:
                        k = (s - 5) // 2
                        if k == 0:
                            m_bank(at)
                        pe.wait_ge(d_done, at("d_done", av_job(k) + 1))
                        last = project_out(k, wout_sb)
                        if k == 2 * NB - 1:
                            last.then_inc(m_full, 1)
                    if s >= 3 and s % 2 == 1 and (s - 3) // 2 < 2 * NB:
                        k = (s - 3) // 2
                        pe.wait_ge(vs_ready, at("vs", 0))
                        dst = d_bank(at, av_job(k), s_job(2 * k + 1) + 1)
                        attention_out(dst, k).then_inc(d_full, 1)

            def t_l1(g, at):
                pe.wait_ge(craw_loaded, at("craw_in"))
                pe.wait_ge(xn2_ready, at("xn2"))
                turn_tiles(at, 0, xn["L1"], 128, S)
                turn_tiles(at, 1, c_raw, SC, SC)
                for m in range(MT):
                    pe.matmul(a_bank(at, 2 + 2 * m, 2), wq_sb[:, m * 128:(m + 1) * 128], xT[:], start=True,
                              stop=True).then_inc(a_full, 1)
                    pe.matmul(a_bank(at, 3 + 2 * m)[:, 0:TC], wk_sb[:, m * 128:(m + 1) * 128],
                              cT[:].rearrange("p b k -> p (b k)"), start=True, stop=True).then_inc(a_full, 1)
                    values(at, m, wv_sb)
                for s in range(BLK + AV_LAG + 2):
                    if s < BLK:
                        b = s * HB // H
                        if s == 0:
                            pe.wait_ge(a_done, at("a_done", 2 + 2 * MT))
                        dst = d_bank(at, 2 * NB + s)
                        for i in range(2):
                            t = (s * HB + 2 * i) % H // 2
                            last = pe.matmul(dst[:, i * 2 * SC:(i + 1) * 2 * SC], qT[:, t, b * S:(b + 1) * S],
                                             kz[:, b, t, :, :].rearrange("p r k -> p (r k)"), start=True, stop=True)
                        last.then_inc(d_full, 1)
                    if T_LAG <= s < BLK + T_LAG:
                        n = s - T_LAG
                        dst = a_bank(at, t_job(n))
                        pe.wait_ge(pnorm, at("pnorm", n + 1))
                        for i in range(HB):
                            last = pe.transpose(dst[0:SC, i * S:(i + 1) * S], er[:, n % RING, i * SC:(i + 1) * SC], ident[:])
                        last.then_inc(a_full, 1)
                    if s >= AV_LAG + 2 and s % 2 == 0 and (s - AV_LAG - 2) // 2 < 2 * NB:
                        k = (s - AV_LAG - 2) // 2
                        if k == 0:
                            m_bank(at)
                        pe.wait_ge(a_done, at("a_done", ot_job(k) + 1))
                        last = project_out(k, wo_sb)
                        if k == 2 * NB - 1:
                            last.then_inc(m_full, 1)
                    if s >= AV_LAG and s % 2 == 0 and (s - AV_LAG) // 2 < 2 * NB:
                        k = (s - AV_LAG) // 2
                        dst = a_bank(at, ot_job(k), t_job(2 * k + 1) + 1)
                        attention_out(dst, k).then_inc(a_full, 1)

            def router(at, weights):
                m_bank(at)
                for b in range(NB):
                    last = pe.matmul(PM[:, b * E:(b + 1) * E], xTf[:, b * S:(b + 1) * S], weights[:], start=True, stop=True)
                last.then_inc(m_full, 1)

            def t_f0(g, at):
                if at.section is FIRST:
                    pe.wait_ge(scaled, 4)
                pe.wait_ge(xn1_ready, at("xn1"))
                turn_tiles(at, 0, xn["F0"], 128, S)
                pe.wait_ge(a_done, at("a_done", 1))
                router(at, w0r_sb)
                for u in range(U0 + 1):
                    if u < U0:
                        w = U0 - 1 if u == 0 else u - 1
                        for half in range(2):
                            cols = slice(half * 128, half * 128 + 128)
                            pe.matmul(a_bank(at, 1 + 2 * u + half), w0g_sb[:, w, cols], xTf[:], start=True, stop=True).then_inc(a_full, 1)
                            pe.matmul(d_bank(at, u0_job(u, half)), w0u_sb[:, w, cols], xTf[:], start=True, stop=True).then_inc(d_full, 1)
                    if u >= 1:
                        w = U0 - 1 if u == 1 else u - 2
                        dst = d_bank(at, y0_job(u - 1), u0_job(u - 1, 1) + 1)
                        for b in range(NB):
                            for half in range(2):
                                last = pe.matmul(dst[:, b * D:(b + 1) * D], hid[:, (u - 1) % 2, half, b * S:(b + 1) * S],
                                                 w0d_sb[:, w, half, :], start=(half == 0), stop=(half == 1))
                        last.then_inc(d_full, 1)

            def t_f1(g, at):
                pe.wait_ge(xn3_ready, at("xn3"))
                turn_tiles(at, 0, xn["F1"], 128, S)
                pe.wait_ge(a_done, at("a_done", 1))
                router(at, w1r_sb)
                for u in range(U1 + 1):
                    if u < U1:
                        w, rows = (U1 - 1, 64) if u == 0 else (u - 1, 128)
                        pe.matmul(a_bank(at, 1 + u)[0:rows, :], w1g_sb[:, w, 0:rows], xTf[:], start=True, stop=True).then_inc(a_full, 1)
                        pe.matmul(d_bank(at, u1_job(u))[0:rows, :], w1u_sb[:, w, 0:rows], xTf[:], start=True, stop=True).then_inc(d_full, 1)
                    if u == 1:
                        dst = d_bank(at, y1_job(0), u1_job(0) + 1)
                        for b in range(NB):
                            last = pe.matmul(dst[:, b * D:(b + 1) * D], hid[0:64, 0, 0, b * S:(b + 1) * S],
                                             w1d_sb[0:64, U1 - 1, 0, :], start=True, stop=True)
                        last.then_inc(d_full, 1)
                    if u >= 2:
                        for part in range(2):
                            dst = d_bank(at, y1_job(u - 1, part), u1_job(u - 1) + 1)
                            for i in range(2):
                                b = 2 * part + i
                                last = pe.matmul(dst[:, i * 256:(i + 1) * 256], hid[:, (u - 1) % 2, 0, b * S:(b + 1) * S],
                                                 w1d_sb[:, u - 2, :, :].rearrange("p r d -> p (r d)"), start=True, stop=True)
                            last.then_inc(d_full, 1)

            run_stages(pe, {"N": nothing, "L0A": t_l0a, "L0B": t_l0b, "L1": t_l1, "F0": t_f0, "F1": t_f1})


def kernel(**inputs):
    import numpy as _np
    import concourse.bacc as _bacc
    from concourse import mybir as _mybir
    from concourse.bass_utils import run_bass_kernel_spmd as _run

    w = {k: _np.asarray(v) for k, v in inputs.items()}

    def rows(a):
        return a.reshape(MT, 128, -1).transpose(1, 0, 2)

    def pairs(a):
        return a.transpose(1, 0, 2).reshape(D, E // 2, 128)

    def up0(routed, shared):
        return _np.concatenate([routed, shared[None]]).transpose(2, 0, 1)

    arrays = {
        "x": w["x"], "ctx_in": w["ctx_1024"], "mask": w["mask_BxS2_if1"], "g_xattn": w["g_xattn"], "g_ffn": w["g_ffn"],
        "ln_gamma": w["L0_xattn_ln_gamma"], "ln_beta": w["L0_xattn_ln_beta"],
        "w_in": w["L0_xattn_W_in"], "w_out": rows(w["L0_xattn_W_out"]), "b_out": w["L0_xattn_b_out"],
        "w0g": up0(w["L0_ffn_Wg"], w["L0_ffn_Wg_s"]), "w0u": up0(w["L0_ffn_Wu"], w["L0_ffn_Wu_s"]),
        "w0d": _np.concatenate([w["L0_ffn_Wd"], w["L0_ffn_Wd_s"][None]]).reshape(U0, D, 2, 128).transpose(3, 0, 2, 1),
        "w0r": w["L0_ffn_Wr"].T, "r0b": w["L0_ffn_rb"],
        "wq": w["L1_xattn_Wq"], "bq": w["L1_xattn_bq"].reshape(MT, 128).T,
        "wk": w["L1_xattn_Wk"], "bk": w["L1_xattn_bk"].reshape(MT, 128).T,
        "wv": w["L1_xattn_Wv"], "bv": w["L1_xattn_bv"].reshape(MT, 128).T,
        "wo": rows(w["L1_xattn_Wo"]), "bo": w["L1_xattn_bo"],
        "w1r": w["L1_ffn_gate_w"].T, "c1b": w["L1_ffn_correction_bias"],
        "w1g": pairs(w["L1_ffn_Wg"]), "w1u": pairs(w["L1_ffn_Wu"]),
        "w1d": w["L1_ffn_Wd"].reshape(E // 2, 2, 64, D).transpose(1, 2, 0, 3),
        "w1gs": w["L1_ffn_Wg_s"], "w1us": w["L1_ffn_Wu_s"], "w1ds": w["L1_ffn_Wd_s"],
    }
    arrays = {k: _np.ascontiguousarray(v) for k, v in arrays.items()}
    nc = _bacc.Bacc("TRN2", target_bir_lowering=False, num_devices=1)
    args = {k: nc.dram_tensor(k, a.shape, _mybir.dt.from_np(a.dtype), kind="ExternalInput").ap() for k, a in arrays.items()}
    out = nc.dram_tensor("out", (B, S, D), F32, kind="ExternalOutput").ap()
    scratch = nc.dram_tensor("scratch", (G, 128, 128), F32, kind="Internal").ap()
    flamingo_kernel(nc, **args, out=out, scratch=scratch)
    r = _run(nc, [arrays], core_ids=[0])
    return r.results[0]["out"]
```

```python
from contextlib import ExitStack

import concourse.bass as bass
from concourse import mybir

F32 = mybir.dt.float32
I32 = mybir.dt.int32
ALU = mybir.AluOpType
ACT = mybir.ActivationFunctionType
AX_X = mybir.AxisListType.X

B, S, D = 64, 128, 128
SC = 120
H, DH = 16, 64
HD = H * DH
MT = HD // 128
NB = 4
G = B // NB
T = NB * S
TC = NB * SC
E = 8
I0 = 256
U0 = E + 1
U1 = E // 2 + 1
LN_EPS = 1e-5
COS_EPS = 1e-8
HALF_LOG_COS_EPS = -9.210340371976182
NORM2_MIN = 1e-19
MASKED = -1e30
ROUTE_SCALE = 2.5

HB = 4
BLK = NB * H // HB
A_BANKS, D_BANKS = 4, 3
RING = 4

A_JOBS = {"L0A": 2 + MT, "KT": 2 * NB, "L1": 2 + 2 * MT + BLK + 2 * NB, "R1": 1, "F0": 1 + 2 * U0,
          "F0K": 1 + 2 * U0 + 2 * NB, "F1": U1}
D_JOBS = {"L0A": 2 * NB, "Q": 1, "L0B": BLK + 2 * NB, "L1": 2 * NB + BLK, "R1": 1, "F0": 2 * U0 + U0,
          "F0K": 2 * U0 + U0, "F1": U1 + 2 * (U1 - 1) + 1}
M_JOBS = {"L0A": 1, "L0B": 1, "L1": 1, "F0": 1, "F0K": 1}
LN1 = {"stat": NB, "aggr": NB, "rstd": 2}
RAISED = {
    "N": {"stat": 2 * NB, "aggr": 2 * NB, "rstd": 9, "xn0": 2 * NB, "x_in": 16, "c_in": 16},
    "L0A": {"vsq": NB, "kn2": NB, "qsq": MT, "qsq_used": MT - 1, "nrm": 8, "logs": 2},
    "KT": {"vs": NB},
    "Q": {"scr": 16},
    "L0B": LN1 | {"xn1": NB, "zadd": BLK, "tanh": BLK, "res": 1, "zq_in": 16 * BLK // RING, "ab_in": 32 * NB},
    "L1": LN1 | {"xn3": NB, "mask": 2, "rmax": 2 * BLK, "exp": BLK, "rsum": BLK, "pnorm": BLK, "res": 1},
    "F0": LN1 | {"xn2": NB, "route": 7, "gate": 1, "craw_in": 16, "mask_in": 16},
    "R1": {"gate1": 1, "route1": 20},
    "F1": {"out": 16, "added": 3 * 2 * (U1 - 1)},
}
RAISED["F0K"] = RAISED["F0"] | RAISED["KT"]
for _s in RAISED:
    RAISED[_s] = RAISED[_s] | {"a_full": A_JOBS.get(_s, 0), "a_done": A_JOBS.get(_s, 0),
                               "d_full": D_JOBS.get(_s, 0), "d_done": D_JOBS.get(_s, 0),
                               "m_full": M_JOBS.get(_s, 0), "m_done": M_JOBS.get(_s, 0)}

FIRST = [("N", 0), ("L0A", 0), ("KT", 0), ("Q", 0), ("L0B", 0), ("N", 1), ("L0A", 1), ("F0K", 0), ("Q", 1)]
LOOP = [("L0B", 1), ("N", 2), ("L1", 0), ("L0A", 2), ("R1", 0), ("F0K", 1), ("Q", 2), ("F1", 0)]
LAST = [("L0B", 1), ("L1", 0), ("R1", 0), ("F0", 1), ("F1", 0), ("L1", 1), ("R1", 1), ("F1", 1)]
TRIPS = G - 2


def raised(stages, sem):
    return sum(RAISED[s].get(sem, 0) for s, _ in stages)


class At:

    def __init__(self, section, index, t):
        self.section, self.index, self.t = section, index, t

    def stage(self):
        return self.section[self.index][0]

    def before(self):
        return At(self.section, self.index - 1, self.t)

    def latest(self, stage):
        return At(self.section, max(n for n in range(self.index) if self.section[n][0] == stage), self.t)

    def bank(self, done, banks, k):
        return (raised(self.section[:self.index], done) + k) % banks

    def freed(self, done, banks, k):
        if not any(raised(section, done) % banks for section in (FIRST, LOOP)):
            return k - banks + 1
        return max(k - banks + 1, -raised(self.section[:self.index], done))

    def __call__(self, sem, k=0):
        if self.section is FIRST:
            return raised(FIRST[: self.index], sem) + k
        if self.section is LOOP:
            each = raised(LOOP, sem)
            n = raised(FIRST, sem) + raised(LOOP[: self.index], sem) + k
            return self.t * each + n if each else n
        return raised(FIRST, sem) + TRIPS * raised(LOOP, sem) + raised(LAST[: self.index], sem) + k


def run_stages(eng, programs):
    for n, (stage, d) in enumerate(FIRST):
        programs.get(stage, nothing)(d, At(FIRST, n, 0))
    with eng.Fori(0, TRIPS) as t:
        for n, (stage, d) in enumerate(LOOP):
            programs.get(stage, nothing)(t + d, At(LOOP, n, t))
    for n, (stage, d) in enumerate(LAST):
        programs.get(stage, nothing)(TRIPS + d, At(LAST, n, 0))


def nothing(g, at):
    pass


def s_job(n):
    return n + sum(1 for k in range(2 * NB) if 2 * k + 3 < n)


def av_job(k):
    return min(2 * k + 4, BLK) + k


def g0_job(with_kt, u, half=0):
    return 1 + 2 * u + half + (min(u, 2 * NB) if with_kt else 0)


def kt_job(j):
    return 3 * j + 3


def v1_job(j):
    return j + (j > 4) + (j > 5)


def s1_job(n):
    return 2 * NB + n if n >= EARLY else (5, 7)[n]


L0B_LATE = 2
EARLY = 2
T_LAG, AV_LAG = 4, 6


def t_job(n):
    return 2 + 2 * MT + n + sum(1 for k in range(2 * NB) if 2 * k + 1 + AV_LAG - 1 < n + T_LAG)


def ot_job(k):
    return 2 + 2 * MT + min(2 * k + AV_LAG - T_LAG + 1, BLK) + k


def u0_job(u, half):
    return half if u == 0 else 2 + 3 * (u - 1) + half


def y0_job(u):
    return 3 * u + 4 if u < U0 - 1 else 3 * u + 2


def u1_job(u):
    return (0, 1)[u] if u < 2 else 3 * u - 3


def y1_job(u, part=0):
    if u == 0:
        return 2
    return (3 * u + 1 if u < U1 - 1 else 3 * u) + part


def flamingo_kernel(nc, x, ctx_in, mask, g_xattn, g_ffn, ln_gamma, ln_beta, w_in, w_out, b_out,
                    w0g, w0u, w0d, w0r, r0b, wq, bq, wk, bk, wv, bv, wo, bo,
                    w1r, c1b, w1g, w1u, w1d, w1gs, w1us, w1ds, out, scratch):
    with ExitStack() as ctx:
        def sb(name, shape, dt=F32):
            return ctx.enter_context(nc.sbuf_tensor(name, shape, dt))

        def sem(name):
            return ctx.enter_context(nc.semaphore(name))

        win_sb = sb("win_sb", [128, HD])
        wout_sb = sb("wout_sb", [128, MT, D])
        wq_sb = sb("wq_sb", [128, HD])
        wk_sb = sb("wk_sb", [128, HD])
        wv_sb = sb("wv_sb", [128, HD])
        wo_sb = sb("wo_sb", [128, MT, D])
        w0g_sb = sb("w0g_sb", [128, U0, I0])
        w0u_sb = sb("w0u_sb", [128, U0, I0])
        w0d_sb = sb("w0d_sb", [128, U0, 2, D])
        w1g_sb = sb("w1g_sb", [128, U1, 128])
        w1u_sb = sb("w1u_sb", [128, U1, 128])
        w1d_sb = sb("w1d_sb", [128, U1, 2, D])
        w0r_sb = sb("w0r_sb", [128, E])
        w1r_sb = sb("w1r_sb", [128, E])
        r0b_sb = sb("r0b_sb", [128, E])
        c1b_sb = sb("c1b_sb", [128, E])
        bq_sb = sb("bq_sb", [128, MT])
        bk_sb = sb("bk_sb", [128, MT])
        bv_sb = sb("bv_sb", [128, MT])
        gamma_sb = sb("gamma_sb", [128, 1])
        beta_sb = sb("beta_sb", [128, 1])
        bias0_sb = sb("bias0_sb", [128, D])
        bias1_sb = sb("bias1_sb", [128, D])
        gates_in = sb("gates_in", [128, 4])
        gates = sb("gates", [128, 4])
        ident = sb("ident", [128, 128])
        causal = sb("causal", [128, SC])
        halves = sb("halves", [128, 2])
        before = sb("before", [128, E, E])
        before4 = sb("before4", [128, E // 2, E // 2])
        eps4 = sb("eps4", [128, NB])
        minus_half = sb("minus_half", [128, NB])
        x_in = sb("x_in", [128, NB, D])
        c_in = sb("c_in", [SC, NB, D])
        c_raw = sb("c_raw", [SC, NB, D])
        mask_in = sb("mask_in", [128, TC], I32)
        maskb = sb("maskb", [128, NB, SC])
        x1 = sb("x1", [128, NB, D])
        x2 = sb("x2", [128, NB, D])
        x3 = sb("x3", [128, NB, D])
        y_out = sb("y_out", [128, NB, D])
        stats = sb("stats", [128, 5 * NB, 6])
        mv = sb("mv", [128, 5 * NB, 2])
        rst = sb("rst", [128, 10, NB])
        held = sb("held", [128, 1])
        xn = {k: sb(f"xn_{k}", [128, NB, D]) for k in ("L0A", "F0", "L1", "F1")}
        xT = sb("xT", [128, T])
        xTf = sb("xTf", [128, T])
        xT3 = sb("xT3", [128, T])
        cT = sb("cT", [128, NB, SC])
        qT = sb("qT", [128, MT, T])
        kz = sb("kz", [128, NB, MT, 2, SC])
        v_sb = sb("v_sb", [SC, NB, HD])
        qsq = sb("qsq", [128, 2, T])
        n2 = sb("n2", [128, 2, NB * H])
        lg2 = sb("lg2", [128, 2, NB * H])
        rn0 = sb("rn0", [128, 2, NB * H])
        nw = sb("nw", [128, 2, NB * H])
        nw2 = sb("nw2", [128, 2, NB * H])
        qrow = sb("qrow", [128, 2, NB * H])
        qrowT = sb("qrowT", [128, 128])
        zk = sb("zk", [SC, NB * H])
        rkh = sb("rkh", [SC, NB * H])
        er = sb("er", [128, RING, HB * S])
        pT_hid = sb("pT_hid", [128, RING * HB * S])
        pT = pT_hid[0:SC, :].rearrange("p (r h q) -> p r h q", r=RING, h=HB)
        hid = pT_hid[:].rearrange("p (u r t) -> p u r t", u=2, r=2)
        ab = sb("ab", [128, 2, NB, S])
        oT = sb("oT", [128, 2, NB, S])
        rmx = sb("rmx", [128, RING, HB])
        nmx = sb("nmx", [128, RING, HB])
        rsm = sb("rsm", [128, RING, HB])
        rrc = sb("rrc", [128, RING, HB])
        vsq = sb("vsq", [SC, HD])
        sg = oT[:].rearrange("p a b q -> p a (b q)")
        lgt = sb("lgt", [128, NB, E])
        gth = sb("gth", [128, NB, E])
        lgt1 = sb("lgt1", [128, NB, E])
        gth1 = sb("gth1", [128, NB, E])
        prob = sb("prob", [128, NB, E])
        prob1 = sb("prob1", [128, NB, E])
        biased = sb("biased", [128, NB, E])
        gsum = sb("gsum", [128, NB, E // 2])
        gsel = sb("gsel", [128, NB, E // 2])
        choice = sb("choice", [128, NB, E])
        cmp_a = sb("cmp_a", [128, NB, E, E])
        cmp_b = sb("cmp_b", [128, NB, E, E])
        rank = sb("rank", [128, NB, E])
        wsel = sb("wsel", [128, NB, E])
        wsum = sb("wsum", [128, NB])
        wrec = sb("wrec", [128, NB])
        cw0 = sb("cw0", [128, NB, E])
        cw1 = sb("cw1", [128, NB, E])

        PA = ctx.enter_context(nc.psum_tensor("PA", [128, A_BANKS, 512], F32))
        PD = ctx.enter_context(nc.psum_tensor("PD", [128, D_BANKS, 512], F32))
        PM = ctx.enter_context(nc.psum_tensor("PM", [128, 512], F32))

        w_attn0 = sem("w_attn0")
        w_small = sem("w_small")
        w_ffn0 = sem("w_ffn0")
        w_attn1 = sem("w_attn1")
        w_ffn1 = sem("w_ffn1")
        const = sem("const")
        gated = sem("gated")
        scaled = sem("scaled")
        bvb = sem("bvb")
        bias1_full = sem("bias1_full")
        a_full, a_done = sem("a_full"), sem("a_done")
        d_full, d_done = sem("d_full"), sem("d_done")
        m_full, m_done = sem("m_full"), sem("m_done")
        x_loaded, c_loaded = sem("x_loaded"), sem("c_loaded")
        craw_loaded, mask_loaded = sem("craw_loaded"), sem("mask_loaded")
        stat, aggr, rstd = sem("stat"), sem("aggr"), sem("rstd")
        xn0_ready, xn1_ready, xn2_ready, xn3_ready = sem("xn0_ready"), sem("xn1_ready"), sem("xn2_ready"), sem("xn3_ready")
        vsq_ready, kn2_ready = sem("vsq_ready"), sem("kn2_ready")
        qsq_ready, qsq_used = sem("qsq_ready"), sem("qsq_used")
        nrm, logs, scr_written = sem("nrm"), sem("logs"), sem("scr_written")
        zq_loaded = [sem(f"zq_loaded{i}") for i in range(RING)]
        ab_loaded = [sem(f"ab_loaded{i}") for i in range(2)]
        zadd, vs_ready, tanh_ready = sem("zadd"), sem("vs_ready"), sem("tanh_ready")
        res = sem("res")
        mask_ready = sem("mask_ready")
        rmax, exp_ready, rsum, pnorm = sem("rmax"), sem("exp_ready"), sem("rsum"), sem("pnorm")
        route, gate_ready, route1, gate1_ready = sem("route"), sem("gate_ready"), sem("route1"), sem("gate1_ready")
        added = sem("added")
        out_written = sem("out_written")

        x_g = x.rearrange("(g b) s d -> g s b d", b=NB)
        c_g = ctx_in.rearrange("(g b) s d -> g s b d", b=NB)
        out_g = out.rearrange("(g b) s d -> g s b d", b=NB)
        mask_g = mask.rearrange("(g b) s -> g (b s)", b=NB)

        SMALL = [(gamma_sb[:], ln_gamma.rearrange("(p a) -> p a", a=1)), (beta_sb[:], ln_beta.rearrange("(p a) -> p a", a=1)),
                 (gates_in[:, 0:2], g_xattn.rearrange("(a n) -> a n", a=1).broadcast_to([128, 2])),
                 (gates_in[:, 2:4], g_ffn.rearrange("(a n) -> a n", a=1).broadcast_to([128, 2])),
                 (bias0_sb[:], b_out.rearrange("(a n) -> a n", a=1).broadcast_to([128, D])),
                 (bias1_sb[:], bo.rearrange("(a n) -> a n", a=1).broadcast_to([128, D])),
                 (r0b_sb[:], r0b.rearrange("(a n) -> a n", a=1).broadcast_to([128, E])),
                 (c1b_sb[:], c1b.rearrange("(a n) -> a n", a=1).broadcast_to([128, E])),
                 (bq_sb[:], bq), (bk_sb[:], bk), (bv_sb[:], bv), (w0r_sb[:], w0r), (w1r_sb[:], w1r)]
        N_SMALL = 16 * len(SMALL)
        N_FFN1 = 16 * 9

        block = ctx.enter_context(nc.Block())

        @block.sync
        def _(sp):
            for dst, src in SMALL:
                sp.dma_start(dst, src).then_inc(w_small, 16)

            def s_n(g, at):
                if at.index:
                    sp.wait_ge(res, at("res"))
                sp.dma_start(x_in[:], x_g[g]).then_inc(x_loaded, 16)
                sp.dma_start(c_in[:], c_g[g]).then_inc(c_loaded, 16)

            def load_logs(g, n):
                sp.dma_start(er[0:SC, n % RING, :].rearrange("p (h q) -> p h q", h=HB),
                             scratch[g, n * HB:(n + 1) * HB, :].unsqueeze(0)
                             .broadcast_to([SC, HB, S])).then_inc(zq_loaded[n % RING], 16)

            def s_l0a(g, at):
                if at.section is FIRST and at.index == 1:
                    sp.dma_start(win_sb[:], w_in).then_inc(w_attn0, 16)
                    sp.dma_start(wout_sb[:], w_out).then_inc(w_attn0, 16)
                    sp.dma_start(w0g_sb[:], w0g).then_inc(w_ffn0, 16)
                    sp.dma_start(w0u_sb[:], w0u).then_inc(w_ffn0, 16)
                    sp.dma_start(w0d_sb[:], w0d).then_inc(w_ffn0, 16)
                if at.section is FIRST and at.index > 1:
                    for dst, src in ((wq_sb, wq), (wk_sb, wk), (wv_sb, wv), (wo_sb, wo)):
                        sp.dma_start(dst[:], src).then_inc(w_attn1, 16)
                    sp.dma_start(w1g_sb[:, 0:U1 - 1, :], w1g).then_inc(w_ffn1, 16)
                    sp.dma_start(w1u_sb[:, 0:U1 - 1, :], w1u).then_inc(w_ffn1, 16)
                    sp.dma_start(w1g_sb[:, U1 - 1, 0:64], w1gs).then_inc(w_ffn1, 16)
                    sp.dma_start(w1u_sb[:, U1 - 1, 0:64], w1us).then_inc(w_ffn1, 16)
                    for p in range(2):
                        sp.dma_start(w1d_sb[64 * p:64 * p + 64, 0:U1 - 1, p, :], w1d[p]).then_inc(w_ffn1, 16)
                    sp.dma_start(w1d_sb[0:64, U1 - 1, 0, :], w1ds).then_inc(w_ffn1, 16)

            def s_q(g, at):
                sp.wait_ge(d_done, at("d_done", 1))
                sp.dma_start(scratch[g], qrowT[:]).then_inc(scr_written, 16)
                sp.wait_ge(scr_written, at("scr", 16))
                for n in range(RING):
                    load_logs(g, n)

            def s_l0b(g, at):
                for k in range(2 * NB):
                    if k >= 2:
                        sp.wait_ge(d_done, at("d_done", av_job(k - 2) + 1))
                    rows = scratch[g, NB * H + k * 8:NB * H + k * 8 + 8, :].rearrange("(m r) q -> r m q", r=2)
                    for p in range(2):
                        sp.dma_start(ab[64 * p:64 * p + 64, k % 2, :, :],
                                     rows[p].unsqueeze(0).broadcast_to([64, NB, S])).then_inc(ab_loaded[k % 2], 16)
                    for n in (2 * k + RING, 2 * k + RING + 1):
                        if n < BLK:
                            sp.wait_ge(d_done, at("d_done", s_job(n - RING) + 1))
                            load_logs(g, n)

            def s_f0(g, at):
                if at.section is not FIRST:
                    sp.wait_ge(mask_ready, at("mask"))
                    sp.wait_ge(a_done, at("a_done"))
                sp.dma_start(c_raw[:], c_g[g]).then_inc(craw_loaded, 16)
                sp.dma_start(mask_in[:], mask_g[g].rearrange("(a n) -> a n", a=1).broadcast_to([128, TC])).then_inc(mask_loaded, 16)

            def s_f1(g, at):
                sp.wait_ge(d_done, at("d_done", D_JOBS["F1"]))
                sp.dma_start(out_g[g], y_out[:]).then_inc(out_written, 16)

            run_stages(sp, {"N": s_n, "L0A": s_l0a, "Q": s_q, "L0B": s_l0b, "F0": s_f0, "F0K": s_f0, "F1": s_f1})
            sp.wait_ge(out_written, 16 * G)
            sp.wait_ge(scr_written, 16 * G)

        N_CONST = 16

        @block.gpsimd
        def _(pool):
            for tile, value in ((ident, 0.0), (causal, 0.0), (halves, 0.0), (before, 1.0), (before4, 1.0),
                                (eps4, LN_EPS), (minus_half, -0.5), (w1d_sb, 0.0), (n2, 1.0)):
                pool.memset(tile[:], value).then_inc(const, 1)
            pool.memset(kz[:], 0.0).then_inc(const, 1)
            pool.wait_ge(const, 10)
            pool.affine_select(out=ident[:], in_=ident[:], compare_op=ALU.not_equal, fill=1.0, base=0,
                               pattern=[[-1, 128]], channel_multiplier=1).then_inc(const, 1)
            pool.affine_select(out=causal[:], in_=causal[:], compare_op=ALU.is_ge, fill=MASKED, base=0,
                               pattern=[[-1, SC]], channel_multiplier=1).then_inc(const, 1)
            pool.wait_ge(const, 12)
            pool.memset(halves[0:64, 0:1], 1.0).then_inc(const, 1)
            pool.wait_ge(const, 13)
            pool.memset(halves[64:128, 1:2], 1.0).then_inc(const, 1)
            pool.wait_ge(const, 14)
            pool.affine_select(out=before[:], in_=before[:], compare_op=ALU.is_ge, fill=0.0, base=-1,
                               pattern=[[1, E], [-1, E]], channel_multiplier=0).then_inc(const, 1)
            pool.affine_select(out=before4[:], in_=before4[:], compare_op=ALU.is_ge, fill=0.0, base=-1,
                               pattern=[[1, E // 2], [-1, E // 2]], channel_multiplier=0).then_inc(const, 1)
            pool.wait_ge(const, N_CONST)

            def rstd_of(at, k, n, src, dst, parts=128):
                pool.tensor_tensor(rst[0:parts, dst, :], src, eps4[0:parts, :], ALU.add).then_inc(rstd, 1)
                pool.wait_ge(rstd, at("rstd", k + 1))
                pool.tensor_tensor(rst[0:parts, dst, :], rst[0:parts, dst, :], minus_half[0:parts, :], ALU.pow).then_inc(rstd, 1)

            def p_n(g, at):
                pool.wait_ge(aggr, at("aggr", NB))
                rstd_of(at, 0, 2, mv[:, 0:NB, 1], 0)
                pool.wait_ge(rstd, at("rstd", 2))
                pool.tensor_tensor(rst[:, 1, :], rst[:, 0, :], rst[:, 0, :], ALU.mult).then_inc(rstd, 1)
                pool.wait_ge(rstd, at("rstd", 3))
                pool.tensor_tensor(rst[:, 1, :], rst[:, 1, :], mv[:, 0:NB, 1], ALU.mult).then_inc(rstd, 1)
                pool.wait_ge(rstd, at("rstd", 4))
                rstd_of(at, 4, 2, rst[:, 1, :], 2)
                pool.wait_ge(rstd, at("rstd", 6))
                pool.tensor_tensor(rst[:, 3, :], rst[:, 2, :], rst[:, 0, :], ALU.mult).then_inc(rstd, 1)
                pool.wait_ge(aggr, at("aggr", 2 * NB))
                rstd_of(at, 7, 2, mv[0:SC, NB:2 * NB, 1], 4, SC)

            def p_ln(at, slot):
                pool.wait_ge(aggr, at("aggr", NB))
                rstd_of(at, 0, 2, mv[:, (slot - 3) * NB:(slot - 2) * NB, 1], slot)

            def p_l0a(g, at):
                for m in range(MT):
                    pool.wait_ge(a_done, at("a_done", 2 + m + 1))
                    if m >= 2:
                        pool.wait_ge(qsq_used, at("qsq_used", m - 1))
                    pool.tensor_tensor(qsq[:, m % 2, :], qT[:, m, :], qT[:, m, :], ALU.mult).then_inc(qsq_ready, 1)

            def scale_values(at, job_of):
                pool.wait_ge(nrm, at("nrm"))
                for b in range(NB):
                    pool.wait_ge(a_full, at("a_full", job_of(2 * b + 1) + 1))
                    val = v_sb[:, b, :].rearrange("p (h d) -> p h d", h=H)
                    pool.tensor_tensor(val, val, rkh[:, b * H:(b + 1) * H].unsqueeze(2).broadcast_to([SC, H, DH]),
                                       ALU.mult).then_inc(vs_ready, 1)

            def p_kt(g, at):
                scale_values(at, lambda j: j)

            def p_l0b(g, at):
                pool.wait_ge(nrm, at("nrm"))
                for n in range(BLK):
                    pool.wait_ge(zq_loaded[n % RING], at("zq_in", 16 * (n // RING + 1)))
                    blk = er[0:SC, n % RING, :].rearrange("p (h q) -> p h q", h=HB)
                    pool.tensor_tensor(blk, blk, zk[:, n * HB:(n + 1) * HB].unsqueeze(2).broadcast_to([SC, HB, S]),
                                       ALU.add).then_inc(zadd, 1)
                p_ln(at, 5)

            def p_l1(g, at):
                for n in range(BLK):
                    blk = er[:, n % RING, 0:HB * SC].rearrange("p (h k) -> p h k", h=HB)
                    pool.wait_ge(rsum, at("rsum", n + 1))
                    pool.tensor_tensor(blk, blk, rrc[:, n % RING, :].unsqueeze(2).broadcast_to([128, HB, SC]),
                                       ALU.mult).then_inc(pnorm, 1)
                p_ln(at, 6)

            def p_f0(g, at):
                if at.stage() == "F0K":
                    scale_values(at, kt_job)
                p_ln(at, 7)

            run_stages(pool, {"N": p_n, "L0A": p_l0a, "KT": p_kt, "L0B": p_l0b, "L1": p_l1, "F0": p_f0, "F0K": p_f0})

        @block.scalar
        def _(act):
            act.wait_ge(w_small, N_SMALL)
            nc.scalar.activation(gates[:], gates_in[:], ACT.Tanh).then_inc(gated, 1)

            def bank(at, k):
                act.wait_ge(a_full, at("a_full", k + 1))
                return PA[:, at.bank("a_done", A_BANKS, k), :]

            def a_l0a(g, at):
                nc.scalar.activation(xT[:], bank(at, 0), ACT.Identity, bias=beta_sb[:, 0:1],
                                     scale=gamma_sb[:, 0:1]).then_inc(a_done, 1)
                nc.scalar.activation(cT[:], bank(at, 1)[:, 0:TC].rearrange("p (b k) -> p b k", b=NB), ACT.Identity,
                                     bias=beta_sb[:, 0:1], scale=gamma_sb[:, 0:1]).then_inc(a_done, 1)

                def square(b):
                    act.wait_ge(d_done, at("d_done", 2 * b + 2))
                    if b >= 1:
                        act.wait_ge(kn2_ready, at("kn2", b))
                    nc.scalar.activation(vsq[:], v_sb[:, b, :], ACT.Square).then_inc(vsq_ready, 1)

                for m in range(MT):
                    nc.scalar.activation(qT[:, m, :], bank(at, 2 + m), ACT.Copy).then_inc(a_done, 1)
                    if m >= 3 and m % 2 == 1:
                        square((m - 3) // 2)
                square(NB - 1)

            def keys(at, job, j):
                b, t0 = j // 2, 4 * (j % 2)
                src = bank(at, job)[:, 0:4 * SC].rearrange("p (t k) -> p t k", t=4)
                nc.scalar.activation(kz[0:64, b, t0:t0 + 4, 0, :], src[0:64], ACT.Copy)
                nc.scalar.activation(kz[64:128, b, t0:t0 + 4, 1, :], src[64:128], ACT.Copy).then_inc(a_done, 1)

            def a_kt(g, at):
                log_norms(at.latest("L0A"))
                for j in range(2 * NB):
                    keys(at, j, j)

            def log_norms(at):
                act.wait_ge(nrm, at("nrm", 2))
                nc.scalar.activation(lg2[:], n2[:], ACT.Ln).then_inc(logs, 1)
                act.wait_ge(logs, at("logs", 1))
                nc.scalar.activation(rn0[:], lg2[:], ACT.Exp, scale=-0.5).then_inc(logs, 1)

            def a_l0b(g, at):
                for n in range(BLK):
                    act.wait_ge(zadd, at("zadd", n + 1))
                    nc.scalar.activation(er[0:SC, n % RING, :], er[0:SC, n % RING, :], ACT.Tanh).then_inc(tanh_ready, 1)

            def a_l1(g, at):
                act.wait_ge(w_small, N_SMALL)
                nc.scalar.activation(xT[:], bank(at, 0), ACT.Copy).then_inc(a_done, 1)
                nc.scalar.activation(cT[:], bank(at, 1)[:, 0:TC].rearrange("p (b k) -> p b k", b=NB),
                                     ACT.Copy).then_inc(a_done, 1)
                for m in range(MT):
                    nc.scalar.activation(qT[:, m, :], bank(at, 2 + 2 * m), ACT.Identity,
                                         bias=bq_sb[:, m:m + 1]).then_inc(a_done, 1)
                    src = bank(at, 3 + 2 * m)[:, 0:TC].rearrange("p (b k) -> p b k", b=NB)
                    nc.scalar.activation(kz[0:64, :, m, 0, :], src[0:64], ACT.Identity, bias=bk_sb[0:64, m:m + 1])
                    nc.scalar.activation(kz[64:128, :, m, 1, :], src[64:128], ACT.Identity,
                                         bias=bk_sb[64:128, m:m + 1]).then_inc(a_done, 1)
                for s in range(BLK + AV_LAG):
                    if 1 <= s <= BLK:
                        n = s - 1
                        act.wait_ge(rmax, at("rmax", 2 * n + 2))
                        for i in range(HB):
                            row = er[:, n % RING, i * SC:(i + 1) * SC]
                            last = nc.scalar.activation(row, row, ACT.Exp, bias=nmx[:, n % RING, i:i + 1], scale=DH ** -0.5,
                                                        accum_out=rsm[:, n % RING, i:i + 1])
                        last.then_inc(exp_ready, 1)
                    if T_LAG <= s < BLK + T_LAG:
                        n = s - T_LAG
                        nc.scalar.activation(pT[:, n % RING, :, :], bank(at, t_job(n))[0:SC, :].rearrange(
                            "p (h q) -> p h q", h=HB), ACT.Copy).then_inc(a_done, 1)
                    if s >= AV_LAG and (s - AV_LAG) % 2 == 0:
                        k = (s - AV_LAG) // 2
                        nc.scalar.activation(oT[:, k % 2, :, :], bank(at, ot_job(k)).rearrange("p (m q) -> p m q", m=NB),
                                             ACT.Copy).then_inc(a_done, 1)

            def a_f0(g, at):
                nc.scalar.activation(xTf[:], bank(at, 0), ACT.Copy).then_inc(a_done, 1)
                with_kt = at.stage() == "F0K"
                if with_kt:
                    log_norms(at.latest("L0A"))
                if at.before().stage() == "R1":
                    act.wait_ge(d_done, at.before()("d_done", 1))
                    nc.scalar.activation(gth1[:], lgt1[:], ACT.Tanh, scale=0.5).then_inc(gate1_ready, 1)
                act.wait_ge(m_done, at("m_done", 1))
                nc.scalar.activation(gth[:], lgt[:], ACT.Tanh, scale=0.5).then_inc(gate_ready, 1)
                for j in range(2 * U0):
                    if j >= 2:
                        act.wait_ge(d_done, at("d_done", u0_job((j - 2) // 2, j % 2) + 1))
                    nc.scalar.activation(sg[:, j % 2, :], bank(at, g0_job(with_kt, j // 2, j % 2)), ACT.Silu).then_inc(a_done, 1)
                    if with_kt and j % 2 == 1 and j // 2 < 2 * NB:
                        keys(at, kt_job(j // 2), j // 2)

            def a_r1(g, at):
                nc.scalar.activation(xT3[:], bank(at, 0), ACT.Copy).then_inc(a_done, 1)

            def a_f1(g, at):
                if at.before().stage() == "R1":
                    act.wait_ge(d_done, at.before()("d_done", 1))
                    nc.scalar.activation(gth1[:], lgt1[:], ACT.Tanh, scale=0.5).then_inc(gate1_ready, 1)
                for j in range(U1):
                    if j >= 2:
                        act.wait_ge(d_done, at("d_done", u1_job(j - 2) + 1))
                    parts = 64 if j == 0 else 128
                    nc.scalar.activation(sg[0:parts, j % 2, :], bank(at, j)[0:parts, :], ACT.Silu).then_inc(a_done, 1)

            run_stages(act, {"L0A": a_l0a, "KT": a_kt, "F0K": a_f0, "L0B": a_l0b, "L1": a_l1, "R1": a_r1, "F0": a_f0, "F1": a_f1})

        @block.vector
        def _(dve):
            dve.wait_ge(const, N_CONST)
            dve.wait_ge(gated, 1)
            dve.wait_ge(w_attn0, 32)
            nc.vector.tensor_scalar(wout_sb[:], wout_sb[:], gates[:, 0:1], 0.5, ALU.mult, ALU.mult).then_inc(scaled, 1)
            nc.vector.tensor_scalar(bias0_sb[:], bias0_sb[:], gates[:, 0:1], None, ALU.mult).then_inc(scaled, 1)
            nc.vector.tensor_scalar(bias1_sb[:], bias1_sb[:], gates[:, 1:2], None, ALU.mult).then_inc(scaled, 1)

            def scale_ffn0():
                dve.wait_ge(w_ffn0, 48)
                nc.vector.tensor_scalar(w0d_sb[:], w0d_sb[:], gates[:, 2:3], None, ALU.mult).then_inc(scaled, 1)

            def scale_rest():
                dve.wait_ge(w_attn1, 64)
                nc.vector.tensor_scalar(wo_sb[:], wo_sb[:], gates[:, 1:2], None, ALU.mult).then_inc(scaled, 1)
                for m in range(MT):
                    nc.vector.tensor_copy(oT[:].rearrange("p a b q -> p (a b) q")[:, m, :],
                                          bv_sb[:, m:m + 1].broadcast_to([128, 128])).then_inc(bvb, 1)
                dve.wait_ge(w_ffn1, 16 * 7)
                nc.vector.tensor_scalar(w1d_sb[:], w1d_sb[:], gates[:, 3:4], None, ALU.mult).then_inc(scaled, 1)
                dve.wait_ge(bias1_full, 1)
                nc.vector.tensor_tensor(bias1_sb[:], PM[:, 0:D], bias1_sb[:], ALU.add).then_inc(scaled, 1)

            def bank(at, k):
                dve.wait_ge(d_full, at("d_full", k + 1))
                return PD[:, at.bank("d_done", D_BANKS, k), :]

            def row_stats(at, k, src, slot, parts):
                for b in range(NB):
                    nc.vector.bn_stats(stats[0:parts, slot + b, :], src[:, b, :]).then_inc(stat, 1)
                dve.wait_ge(stat, at("stat", k + NB))
                nc.vector.tensor_copy(held[0:parts, :], stats[0:parts, slot, 0:1])
                for b in range(NB):
                    nc.vector.bn_aggr(mv[0:parts, slot + b, :], stats[0:parts, slot + b, :]).then_inc(aggr, 1)

            def normalise(src, dst, slot, r, parts, ready):
                for b in range(NB):
                    nc.vector.tensor_scalar(dst[:, b, :], src[:, b, :], mv[0:parts, slot + b, 0:1],
                                            rst[0:parts, r, b:b + 1], ALU.subtract, ALU.mult).then_inc(ready, 1)

            def v_n(g, at):
                if at.section is FIRST and at.index:
                    scale_ffn0()
                dve.wait_ge(x_loaded, at("x_in", 16))
                row_stats(at, 0, x_in, 0, 128)
                dve.wait_ge(c_loaded, at("c_in", 16))
                row_stats(at, NB, c_in, NB, SC)
                if at.index:
                    finish_norm(at.before(), x1, xn["F0"], 5, xn1_ready)
                dve.wait_ge(rstd, at("rstd", 7))
                normalise(x_in, xn["L0A"], 0, 3, 128, xn0_ready)
                dve.wait_ge(rstd, at("rstd", 9))
                normalise(c_in, c_in, NB, 4, SC, xn0_ready)

            def v_l0a(g, at):
                def key_norms(b):
                    dve.wait_ge(vsq_ready, at("vsq", b + 1))
                    nc.vector.tensor_reduce(nw[0:SC, 1, b * H:(b + 1) * H],
                                            vsq[:].rearrange("p (h d) -> p h d", h=H), AX_X, ALU.add).then_inc(kn2_ready, 1)

                for j in range(2 * NB):
                    b, half = j // 2, j % 2
                    nc.vector.tensor_copy(v_sb[:, b, half * 512:half * 512 + 512], bank(at, j)[0:SC, :]).then_inc(d_done, 1)
                    if j >= 4 and j % 2 == 0:
                        key_norms((j - 4) // 2)
                    if j == 1 and at.before().stage() == "L1":
                        finish_norm(at.before(), x3, xn["F1"], 6, xn3_ready)
                key_norms(NB - 2)
                key_norms(NB - 1)
                dve.wait_ge(kn2_ready, at("kn2", NB))
                nc.vector.tensor_scalar(n2[0:SC, 1, :], nw[0:SC, 1, :], NORM2_MIN, None, ALU.max).then_inc(nrm, 1)
                dve.wait_ge(m_full, at("m_full", 1))
                nc.vector.tensor_scalar(n2[:, 0, :], PM[:, 0:NB * H], NORM2_MIN, None, ALU.max).then_inc(m_done, 1)
                dve.wait_ge(m_done, at("m_done", 1))
                nc.vector.tensor_scalar(nw[:], n2[:], -0.5, None, ALU.mult).then_inc(nrm, 1)
                dve.wait_ge(logs, at("logs", 2))
                dve.wait_ge(nrm, at("nrm", 2))
                nc.vector.tensor_tensor(nw2[:], rn0[:], rn0[:], ALU.mult).then_inc(nrm, 1)
                dve.wait_ge(nrm, at("nrm", 3))
                nc.vector.tensor_tensor(nw2[:], nw2[:], nw[:], ALU.mult).then_inc(nrm, 1)
                nc.vector.tensor_scalar(qrow[:, 0, :], lg2[:, 0, :], 0.25, None, ALU.mult).then_inc(nrm, 1)
                dve.wait_ge(nrm, at("nrm", 5))
                nc.vector.scalar_tensor_tensor(qrow[:, 1, :], nw2[:, 0, :], 1.5, rn0[:, 0, :], ALU.add, ALU.mult).then_inc(nrm, 1)
                nc.vector.scalar_tensor_tensor(rkh[:], nw2[0:SC, 1, :], 1.5, rn0[0:SC, 1, :], ALU.add, ALU.mult).then_inc(nrm, 1)
                nc.vector.tensor_scalar(zk[:], lg2[0:SC, 1, :], 0.25, -HALF_LOG_COS_EPS, ALU.mult, ALU.add).then_inc(nrm, 1)

            def residual(at, src, bias, dst):
                dve.wait_ge(m_full, at("m_full", 1))
                nc.vector.tensor_tensor(dst[:], PM[:].rearrange("p (b d) -> p b d", b=NB), src[:], ALU.add).then_inc(m_done, 1)
                dve.wait_ge(m_done, at("m_done", 1))
                nc.vector.tensor_tensor(dst[:], dst[:], bias[:].unsqueeze(1).broadcast_to([128, NB, D]), ALU.add).then_inc(res, 1)
                dve.wait_ge(res, at("res", 1))

            def finish_norm(at, src, dst, r, ready):
                dve.wait_ge(rstd, at("rstd", 2))
                normalise(src, dst, (r - 3) * NB, r, 128, ready)

            def v_l0b(g, at):
                dve.wait_ge(scaled, 3)
                for s in range(BLK + 4):
                    if s < BLK:
                        dve.wait_ge(tanh_ready, at("tanh", s + 1))
                        nc.vector.scalar_tensor_tensor(pT[:, s % RING, :, :].rearrange("p h q -> p (h q)"),
                                                       er[0:SC, s % RING, :], 1.0, bank(at, s_job(s))[0:SC, :],
                                                       ALU.add, ALU.mult).then_inc(d_done, 1)
                    if s >= 3 and s % 2 == 1 and (s - 3) // 2 < 2 * NB:
                        k = (s - 3) // 2
                        dve.wait_ge(ab_loaded[k % 2], at("ab_in", 32 * (k // 2 + 1)))
                        nc.vector.tensor_tensor(oT[:, k % 2, :, :], bank(at, av_job(k)).rearrange("p (m q) -> p m q", m=NB),
                                                ab[:, k % 2, :, :], ALU.mult).then_inc(d_done, 1)
                residual(at, x_in, bias0_sb, x1)
                row_stats(at, 0, x1, 2 * NB, 128)
                if at.section is LAST:
                    finish_norm(at, x1, xn["F0"], 5, xn1_ready)

            def v_l1(g, at):
                dve.wait_ge(mask_loaded, at("mask_in"))
                nc.vector.tensor_scalar(maskb[:].rearrange("p b k -> p (b k)"), mask_in[:], 0.0, MASKED,
                                        ALU.is_equal, ALU.mult).then_inc(mask_ready, 1)
                dve.wait_ge(mask_ready, at("mask", 1))
                nc.vector.tensor_tensor(maskb[:], maskb[:], causal[:].unsqueeze(1).broadcast_to([128, NB, SC]),
                                        ALU.add).then_inc(mask_ready, 1)

                def masked_scores(n):
                    blk = er[:, n % RING, 0:HB * SC].rearrange("p (h k) -> p h k", h=HB)
                    if n >= RING:
                        dve.wait_ge(a_full, at("a_full", t_job(n - RING) + 1))
                    nc.vector.tensor_tensor(blk, bank(at, s1_job(n))[:, 0:HB * SC].rearrange("p (h k) -> p h k", h=HB),
                                            maskb[:, n * HB // H, :].unsqueeze(1).broadcast_to([128, HB, SC]),
                                            ALU.add).then_inc(d_done, 1)
                    dve.wait_ge(d_done, at("d_done", s1_job(n) + 1))
                    nc.vector.tensor_reduce(rmx[:, n % RING, :], blk, AX_X, ALU.max).then_inc(rmax, 1)
                    dve.wait_ge(rmax, at("rmax", 2 * n + 1))
                    nc.vector.tensor_scalar(nmx[:, n % RING, :], rmx[:, n % RING, :], -DH ** -0.5, None, ALU.mult).then_inc(rmax, 1)

                for j in range(2 * NB):
                    b, half = j // 2, j % 2
                    nc.vector.tensor_copy(v_sb[:, b, half * 512:half * 512 + 512], bank(at, v1_job(j))[0:SC, :]).then_inc(d_done, 1)
                    if j == 4:
                        dve.wait_ge(mask_ready, at("mask", 2))
                    if j in (4, 5):
                        masked_scores(j - 4)
                for s in range(EARLY, BLK + 2):
                    if s < BLK:
                        masked_scores(s)
                    if s >= 2:
                        n = s - 2
                        dve.wait_ge(exp_ready, at("exp", n + 1))
                        nc.vector.reciprocal(rrc[:, n % RING, :], rsm[:, n % RING, :]).then_inc(rsum, 1)
                residual(at, x2, bias1_sb, x3)
                row_stats(at, 0, x3, 3 * NB, 128)
                if at.section is LAST:
                    finish_norm(at, x3, xn["F1"], 6, xn3_ready)

            def ranks(done, name, at, k, scores, tri, n, beats, ties):
                mine = scores[:, :, 0:n].unsqueeze(3).broadcast_to([128, NB, n, n])
                other = scores[:, :, 0:n].unsqueeze(2).broadcast_to([128, NB, n, n])
                tri_b = tri[:].unsqueeze(1).broadcast_to([128, NB, n, n])
                nc.vector.tensor_tensor(beats, other, mine, ALU.is_gt).then_inc(done, 1)
                nc.vector.tensor_tensor(ties, other, mine, ALU.is_ge).then_inc(done, 1)
                dve.wait_ge(done, at(name, k + 2))
                nc.vector.tensor_tensor(ties, ties, tri_b, ALU.mult).then_inc(done, 1)
                dve.wait_ge(done, at(name, k + 3))
                nc.vector.tensor_tensor(beats, beats, ties, ALU.max).then_inc(done, 1)
                dve.wait_ge(done, at(name, k + 4))
                nc.vector.tensor_reduce(rank[:, :, 0:n], beats, AX_X, ALU.add).then_inc(done, 1)
                dve.wait_ge(done, at(name, k + 5))

            pairs = biased[:].rearrange("p b (n r) -> p b n r", r=2)

            def flat(tile):
                return tile[:].rearrange("p b e -> p (b e)")

            def router0(at):
                dve.wait_ge(gate_ready, at("gate", 1))
                nc.vector.tensor_scalar(prob[:], gth[:], 0.5, 0.5, ALU.mult, ALU.add).then_inc(route, 1)
                dve.wait_ge(route, at("route", 1))
                ranks(route, "route", at, 1, prob, before, E, cmp_a[:], cmp_b[:])
                nc.vector.scalar_tensor_tensor(flat(cw0), flat(rank), 2.0, flat(prob), ALU.is_lt, ALU.mult).then_inc(route, 1)
                dve.wait_ge(route, at("route", 7))

            def router1(at):
                dve.wait_ge(gate1_ready, at("gate1", 1))
                nc.vector.tensor_scalar(prob1[:], gth1[:], 0.5, 0.5, ALU.mult, ALU.add).then_inc(route1, 1)
                dve.wait_ge(route1, at("route1", 1))
                nc.vector.tensor_tensor(biased[:], prob1[:], c1b_sb[:].unsqueeze(1).broadcast_to([128, NB, E]),
                                        ALU.add).then_inc(route1, 1)
                dve.wait_ge(route1, at("route1", 2))
                nc.vector.tensor_tensor(gsum[:], pairs[:, :, :, 0], pairs[:, :, :, 1], ALU.add).then_inc(route1, 1)
                dve.wait_ge(route1, at("route1", 3))

            def router1_groups(at):
                ranks(route1, "route1", at, 3, gsum, before4, E // 2, cmp_a[:, :, 0:E // 2, 0:E // 2], cmp_b[:, :, 0:E // 2, 0:E // 2])
                nc.vector.tensor_scalar(gsel[:], rank[:, :, 0:E // 2], 2.0, None, ALU.is_lt).then_inc(route1, 1)
                dve.wait_ge(route1, at("route1", 9))
                nc.vector.tensor_tensor(choice[:].rearrange("p b (n r) -> p b n r", r=2), pairs,
                                        gsel[:].unsqueeze(3).broadcast_to([128, NB, E // 2, 2]), ALU.mult).then_inc(route1, 1)
                dve.wait_ge(route1, at("route1", 10))

            def router1_experts(at):
                ranks(route1, "route1", at, 10, choice, before, E, cmp_a[:], cmp_b[:])
                nc.vector.scalar_tensor_tensor(flat(wsel), flat(rank), 4.0, flat(prob1), ALU.is_lt, ALU.mult).then_inc(route1, 1)
                dve.wait_ge(route1, at("route1", 16))
                nc.vector.tensor_reduce(wsum[:], wsel[:], AX_X, ALU.add).then_inc(route1, 1)
                dve.wait_ge(route1, at("route1", 17))
                nc.vector.tensor_scalar(wrec[:], wsum[:], 1e-20, 1 / ROUTE_SCALE, ALU.add, ALU.mult).then_inc(route1, 1)
                dve.wait_ge(route1, at("route1", 18))
                nc.vector.reciprocal(wsum[:], wrec[:]).then_inc(route1, 1)
                dve.wait_ge(route1, at("route1", 19))
                nc.vector.tensor_tensor(cw1[:], wsel[:], wsum[:].unsqueeze(2).broadcast_to([128, NB, E]),
                                        ALU.mult).then_inc(route1, 1)
                dve.wait_ge(route1, at("route1", 20))

            def v_f0(g, at):
                dve.wait_ge(m_full, at("m_full", 1))
                nc.vector.tensor_tensor(lgt[:], PM[:, 0:NB * E].rearrange("p (b e) -> p b e", b=NB),
                                        r0b_sb[:].unsqueeze(1).broadcast_to([128, NB, E]), ALU.add).then_inc(m_done, 1)
                for u in range(U0 + 1):
                    if u < U0:
                        for half in range(2):
                            dve.wait_ge(a_done, at("a_done", g0_job(at.stage() == "F0K", u, half) + 1))
                            nc.vector.tensor_tensor(hid[:, u % 2, half, :], bank(at, u0_job(u, half)), sg[:, half, :],
                                                    ALU.mult).then_inc(d_done, 1)
                    if u == 1:
                        router0(at)
                    if u in (3, 4, 5) and at.before().stage() == "R1":
                        (router1, router1_groups, router1_experts)[u - 3](at.before())
                    if u >= 1:
                        y = bank(at, y0_job(u - 1)).rearrange("p (b d) -> p b d", b=NB)
                        if u == 1:
                            nc.vector.tensor_tensor(x2[:], y, x1[:], ALU.add).then_inc(d_done, 1)
                        else:
                            e = u - 2
                            dve.wait_ge(d_done, at("d_done", y0_job(e) + 1))
                            for b in range(NB):
                                add = nc.vector.scalar_tensor_tensor(x2[:, b, :], y[:, b, :], cw0[:, b, e:e + 1],
                                                                     x2[:, b, :], ALU.mult, ALU.add)
                            add.then_inc(d_done, 1)
                dve.wait_ge(d_done, at("d_done", D_JOBS["F0"]))
                row_stats(at, 0, x2, 4 * NB, 128)
                if at.section is LAST:
                    finish_norm(at, x2, xn["L1"], 7, xn2_ready)

            def v_q(g, at):
                nc.vector.tensor_copy(qrowT[:], bank(at, 0)[:, 0:128]).then_inc(d_done, 1)
                if at.section is FIRST and at.before().stage() == "F0K":
                    finish_norm(at.before(), x2, xn["L1"], 7, xn2_ready)
                if at.section is FIRST and at.before().stage() == "F0K":
                    scale_rest()

            def v_r1(g, at):
                nc.vector.tensor_copy(lgt1[:], bank(at, 0)[:, 0:NB * E].rearrange("p (b e) -> p b e", b=NB)).then_inc(d_done, 1)

            def v_f1(g, at):
                for u in range(U1 + 1):
                    if u < U1:
                        parts = 64 if u == 0 else 128
                        dve.wait_ge(a_done, at("a_done", 1 + u))
                        nc.vector.tensor_tensor(hid[0:parts, u % 2, 0, :], bank(at, u1_job(u))[0:parts, :],
                                                sg[0:parts, u % 2, :], ALU.mult).then_inc(d_done, 1)
                    if u == 1:
                        if at.before().stage() == "R1":
                            router1(at.before())
                            router1_groups(at.before())
                            router1_experts(at.before())
                        y = bank(at, y1_job(0)).rearrange("p (b d) -> p b d", b=NB)
                        store_taken(g, at)
                        nc.vector.tensor_tensor(y_out[:], y, x3[:], ALU.add).then_inc(d_done, 1)
                    if u == 2 and at.section is LOOP:
                        finish_norm(at.latest("F0K"), x2, xn["L1"], 7, xn2_ready)
                    if u >= 2:
                        for part in range(2):
                            dve.wait_ge(d_done, at("d_done", y1_job(u - 2, part if u > 2 else 0) + 1))
                            y = bank(at, y1_job(u - 1, part)).rearrange("p (b e d) -> p b e d", b=2, e=2)
                            for r in range(2):
                                e = 2 * (u - 2) + r
                                for b in range(2):
                                    tile = y_out[:, 2 * part + b, :]
                                    step = nc.vector.scalar_tensor_tensor(tile, y[:, b, r, :], cw1[:, 2 * part + b, e:e + 1],
                                                                          tile, ALU.mult, ALU.add)
                                    last = r == 1 and b == 1
                                    step.then_inc(d_done if last else added, 1)
                                if r == 0:
                                    dve.wait_ge(added, at("added", 3 * (2 * (u - 2) + part) + 2))

            def store_taken(g, at):
                dve.wait_ge(out_written, at("out"))

            run_stages(dve, {"N": v_n, "L0A": v_l0a, "Q": v_q, "L0B": v_l0b, "L1": v_l1, "R1": v_r1, "F0": v_f0, "F0K": v_f0, "F1": v_f1})

        @block.tensor
        def _(pe):
            def a_bank(at, k, needs=-10 ** 6):
                done = at("a_done", max(at.freed("a_done", A_BANKS, k), needs))
                if at.section is not FIRST or done > 0:
                    pe.wait_ge(a_done, done)
                return PA[:, at.bank("a_done", A_BANKS, k), :]

            def d_bank(at, k, needs=-10 ** 6):
                done = at("d_done", max(at.freed("d_done", D_BANKS, k), needs))
                if at.section is not FIRST or done > 0:
                    pe.wait_ge(d_done, done)
                return PD[:, at.bank("d_done", D_BANKS, k), :]

            def m_bank(at):
                if not (at.section is FIRST and at.index == 1):
                    pe.wait_ge(m_done, at("m_done"))
                return PM

            def turn_tiles(at, k, src, parts, width):
                dst = a_bank(at, k)
                for b in range(NB):
                    last = pe.transpose(dst[:, b * width:b * width + width], src[:, b, :], ident[0:parts, 0:parts])
                last.then_inc(a_full, 1)

            def head_norms(at, m):
                if m == 0:
                    m_bank(at)
                pe.wait_ge(qsq_ready, at("qsq", m + 1))
                for b in range(NB):
                    last = pe.matmul(PM[:, b * H + 2 * m:b * H + 2 * m + 2], qsq[:, m % 2, b * S:(b + 1) * S], halves[:],
                                     start=True, stop=True)
                last.then_inc(m_full if m == MT - 1 else qsq_used, 1)

            def last_head_norms(at):
                head_norms(at, MT - 2)
                head_norms(at, MT - 1)

            def values(at, job, weights, j):
                b, half = j // 2, j % 2
                pe.matmul(d_bank(at, job)[0:SC, :], cT[:, b, :], weights[:, half * 512:half * 512 + 512],
                          start=True, stop=True).then_inc(d_full, 1)

            def t_l0a(g, at):
                if at.section is FIRST and at.index == 1:
                    pe.wait_ge(const, N_CONST)
                    pe.wait_ge(w_attn0, 32)
                pe.wait_ge(xn0_ready, at("xn0", -NB))
                turn_tiles(at, 0, xn["L0A"], 128, S)
                pe.wait_ge(xn0_ready, at("xn0"))
                turn_tiles(at, 1, c_in, SC, SC)
                if at.before().stage() == "L1":
                    finish_l1(at.before())
                for m in range(MT):
                    pe.matmul(a_bank(at, 2 + m, 1), win_sb[:, m * 128:(m + 1) * 128], xT[:], start=True, stop=True).then_inc(a_full, 1)
                    pe.wait_ge(a_done, at("a_done", 2))
                    values(at, m, win_sb, m)
                    if m >= 2:
                        head_norms(at, m - 2)

            def turn_keys(at, job, j):
                b, t0 = j // 2, 4 * (j % 2)
                dst = a_bank(at, job)
                for i in range(4):
                    last = pe.transpose(dst[:, i * SC:(i + 1) * SC], v_sb[:, b, (t0 + i) * 128:(t0 + i + 1) * 128],
                                        ident[0:SC, 0:SC])
                last.then_inc(a_full, 1)

            def t_kt(g, at):
                pe.wait_ge(d_done, at("d_done"))
                for j in range(2 * NB):
                    turn_keys(at, j, j)
                    if j == 1:
                        last_head_norms(at.latest("L0A"))

            def t_q(g, at):
                pe.wait_ge(nrm, at("nrm", -2))
                pe.transpose(d_bank(at, 0)[:, 0:128], qrow[:].rearrange("p a b -> p (a b)"), ident[:]).then_inc(d_full, 1)
                if at.section is FIRST and at.before().stage() == "F0K":
                    pe.wait_ge(scaled, 5)
                    pe.wait_ge(bvb, MT)
                    pe.wait_ge(m_done, at("m_done"))
                    for m in range(MT):
                        last = pe.matmul(PM[:, 0:D], oT[:].rearrange("p a b q -> p (a b) q")[:, m, :], wo_sb[:, m, :],
                                         start=(m == 0), stop=(m == MT - 1))
                    last.then_inc(bias1_full, 1)
                    pe.wait_ge(scaled, 7)
                    pe.wait_ge(w_small, N_SMALL)

            def attention_out(dst, k):
                b = k // 2
                for i in range(8):
                    h = 8 * (k % 2) + i
                    last = pe.matmul(dst[64 * (i % 2):64 * (i % 2) + 64, (i // 2) * S:(i // 2 + 1) * S],
                                     v_sb[:, b, h * DH:(h + 1) * DH], pT[:, (2 * k + i // 4) % RING, i % 4, :],
                                     start=True, stop=True)
                return last

            def project_out(k, weights):
                b, half = k // 2, k % 2
                for i in range(4):
                    last = pe.matmul(PM[:, b * D:(b + 1) * D], oT[:, k % 2, i, :], weights[:, 4 * half + i, :],
                                     start=(half == 0 and i == 0), stop=(half == 1 and i == 3))
                return last

            def t_l0b(g, at):
                pe.wait_ge(scaled, 3)
                for s in range(BLK + 4):
                    if s < BLK:
                        b = s * HB // H
                        if s == 0:
                            pe.wait_ge(a_done, at("a_done"))
                        dst = d_bank(at, s_job(s))
                        for i in range(HB):
                            h = (s * HB + i) % H
                            last = pe.matmul(dst[0:SC, i * S:(i + 1) * S], kz[:, b, h // 2, h % 2, :],
                                             qT[:, h // 2, b * S:(b + 1) * S], start=True, stop=True)
                        last.then_inc(d_full, 1)
                    if s >= 5 and s % 2 == 1 and (s - 5) // 2 < 2 * NB - L0B_LATE:
                        k = (s - 5) // 2
                        if k == 0:
                            m_bank(at)
                        pe.wait_ge(d_done, at("d_done", av_job(k) + 1))
                        project_out(k, wout_sb)
                    if s >= 3 and s % 2 == 1 and (s - 3) // 2 < 2 * NB:
                        k = (s - 3) // 2
                        pe.wait_ge(vs_ready, at("vs", 0))
                        dst = d_bank(at, av_job(k), s_job(2 * k + 1) + 1)
                        attention_out(dst, k).then_inc(d_full, 1)
                if at.section is FIRST:
                    finish_l0b(at)

            def finish_l0b(at):
                for k in range(2 * NB - L0B_LATE, 2 * NB):
                    pe.wait_ge(d_done, at("d_done", av_job(k) + 1))
                    last = project_out(k, wout_sb)
                last.then_inc(m_full, 1)

            def finish_l1(at):
                pe.wait_ge(a_done, at("a_done", ot_job(2 * NB - 1) + 1))
                project_out(2 * NB - 1, wo_sb).then_inc(m_full, 1)

            def t_l1(g, at):
                pe.wait_ge(craw_loaded, at("craw_in"))
                pe.wait_ge(xn2_ready, at("xn2"))
                turn_tiles(at, 0, xn["L1"], 128, S)
                turn_tiles(at, 1, c_raw, SC, SC)
                if at.before().stage() in ("L0B", "N"):
                    finish_l0b(at.latest("L0B"))

                def scores(n):
                    b = n * HB // H
                    dst = d_bank(at, s1_job(n))
                    if n < EARLY:
                        pe.wait_ge(a_done, at("a_done", 2 + 4 * (n + 1)))
                    for i in range(2):
                        t = (n * HB + 2 * i) % H // 2
                        last = pe.matmul(dst[:, i * 2 * SC:(i + 1) * 2 * SC], qT[:, t, b * S:(b + 1) * S],
                                         kz[:, b, t, :, :].rearrange("p r k -> p (r k)"), start=True, stop=True)
                    last.then_inc(d_full, 1)

                for m in range(MT):
                    pe.matmul(a_bank(at, 2 + 2 * m, 2), wq_sb[:, m * 128:(m + 1) * 128], xT[:], start=True,
                              stop=True).then_inc(a_full, 1)
                    pe.matmul(a_bank(at, 3 + 2 * m)[:, 0:TC], wk_sb[:, m * 128:(m + 1) * 128],
                              cT[:].rearrange("p b k -> p (b k)"), start=True, stop=True).then_inc(a_full, 1)
                    if m >= 2:
                        values(at, v1_job(m - 2), wv_sb, m - 2)
                    if m >= 6:
                        scores(m - 6)
                for j in (2 * NB - 2, 2 * NB - 1):
                    values(at, v1_job(j), wv_sb, j)
                for s in range(EARLY, BLK + AV_LAG + 2):
                    if s < BLK:
                        if s == EARLY:
                            pe.wait_ge(a_done, at("a_done", 2 + 2 * MT))
                        scores(s)
                    if T_LAG <= s < BLK + T_LAG:
                        n = s - T_LAG
                        dst = a_bank(at, t_job(n))
                        pe.wait_ge(pnorm, at("pnorm", n + 1))
                        for i in range(HB):
                            last = pe.transpose(dst[0:SC, i * S:(i + 1) * S], er[:, n % RING, i * SC:(i + 1) * SC], ident[:])
                        last.then_inc(a_full, 1)
                    if s >= AV_LAG + 2 and s % 2 == 0 and (s - AV_LAG - 2) // 2 < 2 * NB - 1:
                        k = (s - AV_LAG - 2) // 2
                        if k == 0:
                            m_bank(at)
                        pe.wait_ge(a_done, at("a_done", ot_job(k) + 1))
                        project_out(k, wo_sb)
                    if s >= AV_LAG and s % 2 == 0 and (s - AV_LAG) // 2 < 2 * NB:
                        k = (s - AV_LAG) // 2
                        dst = a_bank(at, ot_job(k), t_job(2 * k + 1) + 1)
                        attention_out(dst, k).then_inc(a_full, 1)
                if at.section is LAST:
                    finish_l1(at)

            def router(dst, xT_of, weights):
                for b in range(NB):
                    last = pe.matmul(dst[:, b * E:(b + 1) * E], xT_of[:, b * S:(b + 1) * S], weights[:], start=True, stop=True)
                return last

            def t_f0(g, at):
                if at.section is FIRST:
                    pe.wait_ge(scaled, 4)
                pe.wait_ge(xn1_ready, at("xn1"))
                turn_tiles(at, 0, xn["F0"], 128, S)
                with_kt = at.stage() == "F0K"
                if at.before().stage() == "L0A":
                    last_head_norms(at.before())
                m_bank(at)
                pe.wait_ge(a_done, at("a_done", 1))
                router(PM, xTf, w0r_sb).then_inc(m_full, 1)
                for u in range(U0 + 1):
                    if u < U0:
                        w = U0 - 1 if u == 0 else u - 1
                        for half in range(2):
                            cols = slice(half * 128, half * 128 + 128)
                            pe.matmul(a_bank(at, g0_job(with_kt, u, half)), w0g_sb[:, w, cols], xTf[:], start=True, stop=True).then_inc(a_full, 1)
                            pe.matmul(d_bank(at, u0_job(u, half)), w0u_sb[:, w, cols], xTf[:], start=True, stop=True).then_inc(d_full, 1)
                    if with_kt and u < 2 * NB:
                        turn_keys(at, kt_job(u), u)
                    if u >= 1:
                        w = U0 - 1 if u == 1 else u - 2
                        dst = d_bank(at, y0_job(u - 1), u0_job(u - 1, 1) + 1)
                        for b in range(NB):
                            for half in range(2):
                                last = pe.matmul(dst[:, b * D:(b + 1) * D], hid[:, (u - 1) % 2, half, b * S:(b + 1) * S],
                                                 w0d_sb[:, w, half, :], start=(half == 0), stop=(half == 1))
                        last.then_inc(d_full, 1)

            def t_r1(g, at):
                pe.wait_ge(xn3_ready, at("xn3"))
                turn_tiles(at, 0, xn["F1"], 128, S)
                if at.before().stage() == "L0A":
                    last_head_norms(at.before())
                dst = d_bank(at, 0)
                pe.wait_ge(a_done, at("a_done", 1))
                router(dst, xT3, w1r_sb).then_inc(d_full, 1)

            def t_f1(g, at):
                for u in range(U1 + 1):
                    if u < U1:
                        w, rows = (U1 - 1, 64) if u == 0 else (u - 1, 128)
                        pe.matmul(a_bank(at, u)[0:rows, :], w1g_sb[:, w, 0:rows], xT3[:], start=True, stop=True).then_inc(a_full, 1)
                        pe.matmul(d_bank(at, u1_job(u))[0:rows, :], w1u_sb[:, w, 0:rows], xT3[:], start=True, stop=True).then_inc(d_full, 1)
                    if u == 1:
                        dst = d_bank(at, y1_job(0), u1_job(0) + 1)
                        for b in range(NB):
                            last = pe.matmul(dst[:, b * D:(b + 1) * D], hid[0:64, 0, 0, b * S:(b + 1) * S],
                                             w1d_sb[0:64, U1 - 1, 0, :], start=True, stop=True)
                        last.then_inc(d_full, 1)
                    if u >= 2:
                        for part in range(2):
                            dst = d_bank(at, y1_job(u - 1, part), u1_job(u - 1) + 1)
                            for i in range(2):
                                b = 2 * part + i
                                last = pe.matmul(dst[:, i * 256:(i + 1) * 256], hid[:, (u - 1) % 2, 0, b * S:(b + 1) * S],
                                                 w1d_sb[:, u - 2, :, :].rearrange("p r d -> p (r d)"), start=True, stop=True)
                            last.then_inc(d_full, 1)

            run_stages(pe, {"L0A": t_l0a, "KT": t_kt, "F0K": t_f0, "Q": t_q, "L0B": t_l0b, "L1": t_l1, "R1": t_r1, "F0": t_f0, "F1": t_f1})


def kernel(**inputs):
    import numpy as _np
    import concourse.bacc as _bacc
    from concourse import mybir as _mybir
    from concourse.bass_utils import run_bass_kernel_spmd as _run

    w = {k: _np.asarray(v) for k, v in inputs.items()}

    def rows(a):
        return a.reshape(MT, 128, -1).transpose(1, 0, 2)

    def pairs(a):
        return a.transpose(1, 0, 2).reshape(D, E // 2, 128)

    def up0(routed, shared):
        return _np.concatenate([routed, shared[None]]).transpose(2, 0, 1)

    arrays = {
        "x": w["x"], "ctx_in": w["ctx_1024"], "mask": w["mask_BxS2_if1"], "g_xattn": w["g_xattn"], "g_ffn": w["g_ffn"],
        "ln_gamma": w["L0_xattn_ln_gamma"], "ln_beta": w["L0_xattn_ln_beta"],
        "w_in": w["L0_xattn_W_in"], "w_out": rows(w["L0_xattn_W_out"]), "b_out": w["L0_xattn_b_out"],
        "w0g": up0(w["L0_ffn_Wg"], w["L0_ffn_Wg_s"]), "w0u": up0(w["L0_ffn_Wu"], w["L0_ffn_Wu_s"]),
        "w0d": _np.concatenate([w["L0_ffn_Wd"], w["L0_ffn_Wd_s"][None]]).reshape(U0, D, 2, 128).transpose(3, 0, 2, 1),
        "w0r": w["L0_ffn_Wr"].T, "r0b": w["L0_ffn_rb"],
        "wq": w["L1_xattn_Wq"], "bq": w["L1_xattn_bq"].reshape(MT, 128).T,
        "wk": w["L1_xattn_Wk"], "bk": w["L1_xattn_bk"].reshape(MT, 128).T,
        "wv": w["L1_xattn_Wv"], "bv": w["L1_xattn_bv"].reshape(MT, 128).T,
        "wo": rows(w["L1_xattn_Wo"]), "bo": w["L1_xattn_bo"],
        "w1r": w["L1_ffn_gate_w"].T, "c1b": w["L1_ffn_correction_bias"],
        "w1g": pairs(w["L1_ffn_Wg"]), "w1u": pairs(w["L1_ffn_Wu"]),
        "w1d": w["L1_ffn_Wd"].reshape(E // 2, 2, 64, D).transpose(1, 2, 0, 3),
        "w1gs": w["L1_ffn_Wg_s"], "w1us": w["L1_ffn_Wu_s"], "w1ds": w["L1_ffn_Wd_s"],
    }
    arrays = {k: _np.ascontiguousarray(v) for k, v in arrays.items()}
    nc = _bacc.Bacc("TRN2", target_bir_lowering=False, num_devices=1)
    args = {k: nc.dram_tensor(k, a.shape, _mybir.dt.from_np(a.dtype), kind="ExternalInput").ap() for k, a in arrays.items()}
    out = nc.dram_tensor("out", (B, S, D), F32, kind="ExternalOutput").ap()
    scratch = nc.dram_tensor("scratch", (G, 128, 128), F32, kind="Internal").ap()
    flamingo_kernel(nc, **args, out=out, scratch=scratch)
    r = _run(nc, [arrays], core_ids=[0])
    return r.results[0]["out"]
```

```python
from contextlib import ExitStack

import concourse.bass as bass
from concourse import mybir

F32 = mybir.dt.float32
F32R = mybir.dt.float32r
I32 = mybir.dt.int32
ALU = mybir.AluOpType
ACT = mybir.ActivationFunctionType
AX_X = mybir.AxisListType.X

B, S, D = 64, 128, 128
SC = 120
H, DH = 16, 64
HD = H * DH
MT = HD // 128
NB = 4
G = B // NB
T = NB * S
TC = NB * SC
E = 8
I0 = 256
U0 = E + 1
U1 = E // 2 + 1
LN_EPS = 1e-5
COS_EPS = 1e-8
HALF_LOG_COS_EPS = -9.210340371976182
NORM2_MIN = 1e-19
MASKED = -1e30
ROUTE_SCALE = 2.5

HB = 4
BLK = NB * H // HB
A_BANKS, D_BANKS = 4, 3
RING = 4
D_HALVES = 6

A_JOBS = {"L0A": 2 + MT, "KT": 2 * NB, "L1": 2 + 2 * MT + BLK + 2 * NB - D_HALVES, "R1": 1, "F0": 1 + 2 * U0,
          "F0K": 1 + 2 * U0 + 2 * NB, "F1": U1}
D_JOBS = {"L0A": 2 * NB, "Q": 1, "L0B": BLK + 2 * NB, "L1": 2 * NB + BLK + D_HALVES, "R1": 1, "F0": 2 * U0 + U0,
          "F0K": 2 * U0 + U0, "F1": U1 + 2 * (U1 - 1) + 1}
M_JOBS = {"L0A": 2, "L0B": 1, "L1": 1, "F0": 1, "F0K": 1}
LN1 = {"stat": NB, "aggr": NB, "rstd": 2}
RAISED = {
    "N": {"stat": 2 * NB, "aggr": 2 * NB, "rstd": 9, "xn0": 2 * NB, "x_in": 16, "c_in": 16},
    "L0A": {"vsq": NB, "kn2": NB, "qsq": MT, "qsq_used": MT - 1, "nrm": 8, "logs": 2, "hi": 2, "lo": 2},
    "KT": {"vs": NB},
    "Q": {"scr": 16, "xb": 1},
    "L0B": LN1 | {"xn1": NB, "zadd": BLK, "tanh": BLK, "zq_in": 16 * BLK // RING, "ab_in": 32 * NB},
    "L1": LN1 | {"hi": 2, "lo": 2, "xn3": NB, "mask": 2, "rmax": 2 * BLK, "exp": BLK, "rsum": BLK, "pnorm": BLK, "xb": 1},
    "F0": LN1 | {"xn2": NB, "route": 7, "gate": 1, "craw_in": 16, "mask_in": 16},
    "R1": {"lo": 1, "gate1": 1, "route1": 20},
    "F1": {"out": 16, "added": 3 * 2 * (U1 - 1)},
}
RAISED["F0K"] = RAISED["F0"] | RAISED["KT"]
for _s in RAISED:
    RAISED[_s] = RAISED[_s] | {"a_full": A_JOBS.get(_s, 0), "a_done": A_JOBS.get(_s, 0),
                               "d_full": D_JOBS.get(_s, 0), "d_done": D_JOBS.get(_s, 0),
                               "m_full": M_JOBS.get(_s, 0), "m_done": M_JOBS.get(_s, 0)}

FIRST = [("N", 0), ("L0A", 0), ("KT", 0), ("Q", 0), ("N", 1), ("L0B", 0), ("L0A", 1), ("F0K", 0), ("Q", 1)]
LOOP = [("N", 2), ("L0B", 1), ("L1", 0), ("L0A", 2), ("R1", 0), ("F0K", 1), ("Q", 2), ("F1", 0)]
LAST = [("L0B", 1), ("L1", 0), ("R1", 0), ("F0", 1), ("F1", 0), ("L1", 1), ("R1", 1), ("F1", 1)]
TRIPS = G - 2


def raised(stages, sem):
    return sum(RAISED[s].get(sem, 0) for s, _ in stages)


class At:

    def __init__(self, section, index, t):
        self.section, self.index, self.t = section, index, t

    def stage(self):
        return self.section[self.index][0]

    def before(self):
        return At(self.section, self.index - 1, self.t)

    def coming(self, stage):
        return At(self.section, min(n for n in range(self.index, len(self.section)) if self.section[n][0] == stage), self.t)

    def latest(self, stage):
        return At(self.section, max(n for n in range(self.index) if self.section[n][0] == stage), self.t)

    def bank(self, done, banks, k):
        return (raised(self.section[:self.index], done) + k) % banks

    def freed(self, done, banks, k):
        if not any(raised(section, done) % banks for section in (FIRST, LOOP)):
            return k - banks + 1
        return max(k - banks + 1, -raised(self.section[:self.index], done))

    def __call__(self, sem, k=0):
        if self.section is FIRST:
            return raised(FIRST[: self.index], sem) + k
        if self.section is LOOP:
            each = raised(LOOP, sem)
            n = raised(FIRST, sem) + raised(LOOP[: self.index], sem) + k
            return self.t * each + n if each else n
        return raised(FIRST, sem) + TRIPS * raised(LOOP, sem) + raised(LAST[: self.index], sem) + k


def run_stages(eng, programs):
    for n, (stage, d) in enumerate(FIRST):
        programs.get(stage, nothing)(d, At(FIRST, n, 0))
    with eng.Fori(0, TRIPS) as t:
        for n, (stage, d) in enumerate(LOOP):
            programs.get(stage, nothing)(t + d, At(LOOP, n, t))
    for n, (stage, d) in enumerate(LAST):
        programs.get(stage, nothing)(TRIPS + d, At(LAST, n, 0))


def nothing(g, at):
    pass


def s_job(n):
    return n + sum(1 for k in range(2 * NB) if 2 * k + 3 < n)


def av_job(k):
    return min(2 * k + 4, BLK) + k


def g0_job(with_kt, u, half=0):
    return 1 + 2 * u + half + (min(u, 2 * NB) if with_kt else 0)


def kt_job(j):
    return 3 * j + 3


def v1_job(j):
    return j + (j > 4) + (j > 5)


def s1_job(n):
    if n < EARLY:
        return (5, 7)[n]
    return 2 * NB + n + sum(1 for k in range(D_HALVES) if 2 * k + AV_LAG < n)


def ov_job(k):
    return 2 * NB + min(2 * k + AV_LAG + 1, BLK) + k


L0B_LATE = 2
EARLY = 2
T_LAG, AV_LAG = 4, 6


def t_job(n):
    return 2 + 2 * MT + n + sum(1 for k in range(D_HALVES, 2 * NB) if 2 * k + AV_LAG < n + T_LAG)


def ot_job(k):
    return 2 + 2 * MT + min(2 * k + AV_LAG - T_LAG + 1, BLK) + k - D_HALVES


def u0_job(u, half):
    return half if u == 0 else 2 + 3 * (u - 1) + half


def y0_job(u):
    return 3 * u + 4 if u < U0 - 1 else 3 * u + 2


def u1_job(u):
    return (0, 1)[u] if u < 2 else 3 * u - 3


def y1_job(u, part=0):
    if u == 0:
        return 2
    return (3 * u + 1 if u < U1 - 1 else 3 * u) + part


def flamingo_kernel(nc, x, ctx_in, mask, g_xattn, g_ffn, ln_gamma, ln_beta, w_in, w_out, b_out,
                    w0g, w0u, w0d, w0r, r0b, wq, bq, wk, bk, wv, bv, wo, bo,
                    w1r, c1b, w1g, w1u, w1d, w1gs, w1us, w1ds, out, scratch):
    with ExitStack() as ctx:
        def sb(name, shape, dt=F32):
            return ctx.enter_context(nc.sbuf_tensor(name, shape, dt))

        def sem(name):
            return ctx.enter_context(nc.semaphore(name))

        win_hi, win_lo = sb("win_hi", [128, HD], F32R), sb("win_lo", [128, HD], F32R)
        wout_sb = sb("wout_sb", [128, MT, D])
        wq_hi, wq_lo = sb("wq_hi", [128, HD], F32R), sb("wq_lo", [128, HD], F32R)
        wk_hi, wk_lo = sb("wk_hi", [128, HD], F32R), sb("wk_lo", [128, HD], F32R)
        wv_hi, wv_lo = sb("wv_hi", [128, HD], F32R), sb("wv_lo", [128, HD], F32R)
        wo_sb = sb("wo_sb", [128, MT, D])
        w0g_sb = sb("w0g_sb", [128, U0, I0])
        w0u_sb = sb("w0u_sb", [128, U0, I0])
        w0d_sb = sb("w0d_sb", [128, U0, 2, D])
        w1g_hi, w1g_lo = sb("w1g_hi", [128, U1, 128], F32R), sb("w1g_lo", [128, U1, 128], F32R)
        w1u_hi, w1u_lo = sb("w1u_hi", [128, U1, 128], F32R), sb("w1u_lo", [128, U1, 128], F32R)
        w1d_sb = sb("w1d_sb", [128, U1, 2, D])
        w0r_sb = sb("w0r_sb", [128, E])
        w1r_sb = sb("w1r_sb", [128, E])
        r0b_sb = sb("r0b_sb", [128, E])
        c1b_sb = sb("c1b_sb", [128, E])
        bq_sb = sb("bq_sb", [128, MT])
        bk_sb = sb("bk_sb", [128, MT])
        bv_sb = sb("bv_sb", [128, MT])
        gamma_sb = sb("gamma_sb", [128, 1])
        beta_sb = sb("beta_sb", [128, 1])
        bias0_sb = sb("bias0_sb", [128, D])
        bias1_sb = sb("bias1_sb", [128, D])
        gates_in = sb("gates_in", [128, 4])
        gates = sb("gates", [128, 4])
        ident = sb("ident", [128, 128])
        causal = sb("causal", [128, SC])
        head_of = sb("head_of", [128, MT, H])
        before = sb("before", [128, E, E])
        before4 = sb("before4", [128, E // 2, E // 2])
        eps4 = sb("eps4", [128, NB])
        minus_half = sb("minus_half", [128, NB])
        x_in = sb("x_in", [128, NB, D])
        c_in = sb("c_in", [SC, NB, D])
        c_raw = sb("c_raw", [SC, NB, D])
        mask_in = sb("mask_in", [128, TC], I32)
        maskb = mask_in[:].bitcast(F32).rearrange("p (b k) -> p b k", b=NB)
        x1 = sb("x1", [128, NB, D])
        x2 = sb("x2", [128, NB, D])
        x3 = sb("x3", [128, NB, D])
        stats = sb("stats", [128, 5 * NB, 6])
        mv = sb("mv", [128, 5 * NB, 2])
        rst = sb("rst", [128, 10, NB])
        held = sb("held", [128, 1])
        xn = {k: sb(f"xn_{k}", [128, NB, D]) for k in ("L0A", "F0", "L1")}
        xn["F1"] = xn["L1"]
        xT, xT_lo = sb("xT", [128, T], F32R), sb("xT_lo", [128, T], F32R)
        cx_hi, cx_lo = sb("cx_hi", [128, T], F32R), sb("cx_lo", [128, T], F32R)
        cT, cT_lo = (part[:, 0:TC].rearrange("p (b k) -> p b k", b=NB) for part in (cx_hi, cx_lo))
        qT = sb("qT", [128, MT, T])
        kz = sb("kz", [128, NB, MT, 2, SC])
        v_sb = sb("v_sb", [SC, NB, HD])
        n2 = sb("n2", [128, 2, NB * H])
        lg2 = sb("lg2", [128, 2, NB * H])
        rn0 = sb("rn0", [128, 2, NB * H])
        nw = sb("nw", [128, 2, NB * H])
        nw2 = sb("nw2", [128, 2, NB * H])
        qrow = sb("qrow", [128, 2, NB * H])
        qrowT = sb("qrowT", [128, 128])
        zk = sb("zk", [SC, NB * H])
        rkh = sb("rkh", [SC, NB * H])
        er = sb("er", [128, RING, HB * S])
        pT_hid = sb("pT_hid", [128, RING * HB * S])
        pT = pT_hid[0:SC, :].rearrange("p (r h q) -> p r h q", r=RING, h=HB)
        hid = pT_hid[:].rearrange("p (u r t) -> p u r t", u=2, r=2)
        hsum = er[0:H, 0, :]
        ab = sb("ab", [128, 2, NB, S])
        oT = sb("oT", [128, 2, NB, S])
        qsq = [oT[:].rearrange("p a b q -> p a (b q)")[:, k, :] for k in range(2)] + [er[:, 2, :], er[:, 3, :]]
        vsq = ab[0:SC].rearrange("p a b q -> p (a b q)")
        w_whole = qT[:].rearrange("p m t -> p (m t)").rearrange("p (w n) -> p w n", n=HD)
        x_all, c_all = er[:, 1, :], er[:, 0, 0:TC]
        xTf = er[:, 2, :]
        w1_whole = pT_hid[:, 0:2 * U1 * 128].rearrange("p (w n) -> p w n", w=2)
        rmx = sb("rmx", [128, RING, HB])
        nmx = sb("nmx", [128, RING, HB])
        rsm = sb("rsm", [128, RING, HB])
        rrc = sb("rrc", [128, RING, HB])
        sg = oT[:].rearrange("p a b q -> p a (b q)")
        lgt = sb("lgt", [128, NB, E])
        gth = sb("gth", [128, NB, E])
        lgt1 = sb("lgt1", [128, NB, E])
        gth1 = sb("gth1", [128, NB, E])
        prob = sb("prob", [128, NB, E])
        prob1 = sb("prob1", [128, NB, E])
        biased = sb("biased", [128, NB, E])
        gsum = sb("gsum", [128, NB, E // 2])
        gsel = sb("gsel", [128, NB, E // 2])
        choice = sb("choice", [128, NB, E])
        cmp_a = sb("cmp_a", [128, NB, E, E])
        cmp_b = sb("cmp_b", [128, NB, E, E])
        rank = sb("rank", [128, NB, E])
        wsel = sb("wsel", [128, NB, E])
        wsum = sb("wsum", [128, NB])
        wrec = sb("wrec", [128, NB])
        cw0 = sb("cw0", [128, NB, E])
        cw1 = sb("cw1", [128, NB, E])

        PA = ctx.enter_context(nc.psum_tensor("PA", [128, A_BANKS, 512], F32))
        PD = ctx.enter_context(nc.psum_tensor("PD", [128, D_BANKS, 512], F32))
        PM = ctx.enter_context(nc.psum_tensor("PM", [128, 512], F32))

        w_proj = sem("w_proj")
        w_attn0 = sem("w_attn0")
        w_small = sem("w_small")
        w_ffn0 = sem("w_ffn0")
        w_attn1 = sem("w_attn1")
        w_ffn1 = sem("w_ffn1")
        const = sem("const")
        w_hi, w_lo = sem("w_hi"), sem("w_lo")
        hi_ready, lo_ready = sem("hi_ready"), sem("lo_ready")
        gated = sem("gated")
        scaled = sem("scaled")
        bvb = sem("bvb")
        bias1_full = sem("bias1_full")
        a_full, a_done = sem("a_full"), sem("a_done")
        d_full, d_done = sem("d_full"), sem("d_done")
        m_full, m_done = sem("m_full"), sem("m_done")
        x_loaded, c_loaded = sem("x_loaded"), sem("c_loaded")
        craw_loaded, mask_loaded = sem("craw_loaded"), sem("mask_loaded")
        stat, aggr, rstd = sem("stat"), sem("aggr"), sem("rstd")
        xn0_ready, xn1_ready, xn2_ready, xn3_ready = sem("xn0_ready"), sem("xn1_ready"), sem("xn2_ready"), sem("xn3_ready")
        vsq_ready, kn2_ready = sem("vsq_ready"), sem("kn2_ready")
        qsq_ready, qsq_used = sem("qsq_ready"), sem("qsq_used")
        nrm, logs, scr_written = sem("nrm"), sem("logs"), sem("scr_written")
        zq_loaded = [sem(f"zq_loaded{i}") for i in range(RING)]
        ab_loaded = [sem(f"ab_loaded{i}") for i in range(2)]
        zadd, vs_ready, tanh_ready = sem("zadd"), sem("vs_ready"), sem("tanh_ready")
        xb_ready = sem("xb_ready")
        mask_ready = sem("mask_ready")
        rmax, exp_ready, rsum, pnorm = sem("rmax"), sem("exp_ready"), sem("rsum"), sem("pnorm")
        route, gate_ready, route1, gate1_ready = sem("route"), sem("gate_ready"), sem("route1"), sem("gate1_ready")
        added = sem("added")
        out_written = sem("out_written")

        x_g = x.rearrange("(g b) s d -> g s b d", b=NB)
        c_g = ctx_in.rearrange("(g b) s d -> g s b d", b=NB)
        out_g = out.rearrange("(g b) s d -> g s b d", b=NB)
        mask_g = mask.rearrange("(g b) s -> g (b s)", b=NB)

        SMALL = [(gamma_sb[:], ln_gamma.rearrange("(p a) -> p a", a=1)), (beta_sb[:], ln_beta.rearrange("(p a) -> p a", a=1)),
                 (gates_in[:, 0:2], g_xattn.rearrange("(a n) -> a n", a=1).broadcast_to([128, 2])),
                 (gates_in[:, 2:4], g_ffn.rearrange("(a n) -> a n", a=1).broadcast_to([128, 2])),
                 (bias0_sb[:], b_out.rearrange("(a n) -> a n", a=1).broadcast_to([128, D])),
                 (bias1_sb[:], bo.rearrange("(a n) -> a n", a=1).broadcast_to([128, D])),
                 (r0b_sb[:], r0b.rearrange("(a n) -> a n", a=1).broadcast_to([128, E])),
                 (c1b_sb[:], c1b.rearrange("(a n) -> a n", a=1).broadcast_to([128, E])),
                 (bq_sb[:], bq), (bk_sb[:], bk), (bv_sb[:], bv), (w0r_sb[:], w0r), (w1r_sb[:], w1r)]
        N_SMALL = 16 * len(SMALL)
        N_FFN1 = 16 * 9

        N_W1 = (U1 - 1) * 128 + 64
        PARTS = [(hi[:], lo[:], w_whole[:, k, :]) for k, (hi, lo) in
                 enumerate(((win_hi, win_lo), (wq_hi, wq_lo), (wk_hi, wk_lo), (wv_hi, wv_lo)))]
        PARTS += [tuple(part[:].rearrange("p u n -> p (u n)")[:, 0:N_W1] for part in parts) + (w1_whole[:, k, 0:N_W1],)
                  for k, parts in enumerate(((w1g_hi, w1g_lo), (w1u_hi, w1u_lo)))]

        block = ctx.enter_context(nc.Block())

        @block.sync
        def _(sp):
            def load_small():
                for dst, src in SMALL:
                    sp.dma_start(dst, src).then_inc(w_small, 16)

            def s_n(g, at):
                if not (at.section is FIRST and at.index == 0):
                    sp.wait_ge(xb_ready, at("xb"))
                sp.dma_start(x_in[:], x_g[g]).then_inc(x_loaded, 16)
                sp.dma_start(c_in[:], c_g[g]).then_inc(c_loaded, 16)

            def load_logs(g, n):
                sp.dma_start(er[0:SC, n % RING, :].rearrange("p (h q) -> p h q", h=HB),
                             scratch[g, n * HB:(n + 1) * HB, :].unsqueeze(0)
                             .broadcast_to([SC, HB, S])).then_inc(zq_loaded[n % RING], 16)

            def s_l0a(g, at):
                if at.section is FIRST and at.index == 1:
                    for k, src in enumerate((w_in, wq, wk, wv)):
                        sp.dma_start(w_whole[:, k, :], src).then_inc(w_proj, 16)
                    for k, (routed, shared) in enumerate(((w1g, w1gs), (w1u, w1us))):
                        sp.dma_start(w1_whole[:, k, 0:N_W1 - 64].rearrange("p (u n) -> p u n", u=U1 - 1), routed).then_inc(w_proj, 16)
                        sp.dma_start(w1_whole[:, k, N_W1 - 64:N_W1], shared).then_inc(w_proj, 16)
                    load_small()
                    sp.dma_start(wout_sb[:], w_out).then_inc(w_attn0, 16)
                    sp.dma_start(w0g_sb[:], w0g).then_inc(w_ffn0, 16)
                    sp.dma_start(w0u_sb[:], w0u).then_inc(w_ffn0, 16)
                    sp.dma_start(w0d_sb[:], w0d).then_inc(w_ffn0, 16)
                if at.section is FIRST and at.index > 1:
                    sp.dma_start(wo_sb[:], wo).then_inc(w_attn1, 16)
                    for p in range(2):
                        sp.dma_start(w1d_sb[64 * p:64 * p + 64, 0:U1 - 1, p, :], w1d[p]).then_inc(w_ffn1, 16)
                    sp.dma_start(w1d_sb[0:64, U1 - 1, 0, :], w1ds).then_inc(w_ffn1, 16)

            def s_q(g, at):
                sp.wait_ge(d_done, at("d_done", 1))
                sp.dma_start(scratch[g], qrowT[:]).then_inc(scr_written, 16)
                sp.wait_ge(scr_written, at("scr", 16))
                for n in range(RING):
                    load_logs(g, n)

            def s_l0b(g, at):
                for k in range(2 * NB):
                    if k >= 2:
                        sp.wait_ge(d_done, at("d_done", av_job(k - 2) + 1))
                    rows = scratch[g, NB * H + k * 8:NB * H + k * 8 + 8, :].rearrange("(m r) q -> r m q", r=2)
                    for p in range(2):
                        sp.dma_start(ab[64 * p:64 * p + 64, k % 2, :, :],
                                     rows[p].unsqueeze(0).broadcast_to([64, NB, S])).then_inc(ab_loaded[k % 2], 16)
                    for n in (2 * k + RING, 2 * k + RING + 1):
                        if n < BLK:
                            sp.wait_ge(d_done, at("d_done", s_job(n - RING) + 1))
                            load_logs(g, n)

            def s_f0(g, at):
                if at.section is not FIRST:
                    sp.wait_ge(mask_ready, at("mask"))
                    sp.wait_ge(a_done, at("a_done"))
                sp.dma_start(c_raw[:], c_g[g]).then_inc(craw_loaded, 16)
                sp.dma_start(mask_in[:], mask_g[g].rearrange("(a n) -> a n", a=1).broadcast_to([128, TC])).then_inc(mask_loaded, 16)

            def s_f1(g, at):
                sp.wait_ge(d_done, at("d_done", D_JOBS["F1"]))
                sp.dma_start(out_g[g], x3[:]).then_inc(out_written, 16)

            run_stages(sp, {"N": s_n, "L0A": s_l0a, "Q": s_q, "L0B": s_l0b, "F0": s_f0, "F0K": s_f0, "F1": s_f1})
            sp.wait_ge(out_written, 16 * G + 16)
            sp.wait_ge(scr_written, 16 * G)

        N_CONST = 16

        @block.gpsimd
        def _(pool):
            for tile, value in ((ident, 0.0), (causal, 0.0), (head_of, 0.0), (before, 1.0), (before4, 1.0),
                                (eps4, LN_EPS), (minus_half, -0.5), (w1d_sb, 0.0), (n2, 1.0)):
                pool.memset(tile[:], value).then_inc(const, 1)
            pool.memset(x3[:], 0.0).then_inc(out_written, 16)
            pool.memset(kz[:], 0.0).then_inc(const, 1)
            pool.wait_ge(const, 10)
            pool.affine_select(out=ident[:], in_=ident[:], compare_op=ALU.not_equal, fill=1.0, base=0,
                               pattern=[[-1, 128]], channel_multiplier=1).then_inc(const, 1)
            pool.affine_select(out=causal[:], in_=causal[:], compare_op=ALU.is_ge, fill=MASKED, base=0,
                               pattern=[[-1, SC]], channel_multiplier=1).then_inc(const, 1)
            pool.wait_ge(const, 12)
            by_head = head_of[:].rearrange("p m h -> p (m h)")
            pool.memset(by_head[0:64, 0::H + 2], 1.0).then_inc(const, 1)
            pool.wait_ge(const, 13)
            pool.memset(by_head[64:128, 1::H + 2], 1.0).then_inc(const, 1)
            pool.wait_ge(const, 14)
            pool.affine_select(out=before[:], in_=before[:], compare_op=ALU.is_ge, fill=0.0, base=-1,
                               pattern=[[1, E], [-1, E]], channel_multiplier=0).then_inc(const, 1)
            pool.affine_select(out=before4[:], in_=before4[:], compare_op=ALU.is_ge, fill=0.0, base=-1,
                               pattern=[[1, E // 2], [-1, E // 2]], channel_multiplier=0).then_inc(const, 1)
            pool.wait_ge(const, N_CONST)

            def rstd_of(at, k, n, src, dst, parts=128):
                pool.tensor_tensor(rst[0:parts, dst, :], src, eps4[0:parts, :], ALU.add).then_inc(rstd, 1)
                pool.wait_ge(rstd, at("rstd", k + 1))
                pool.tensor_tensor(rst[0:parts, dst, :], rst[0:parts, dst, :], minus_half[0:parts, :], ALU.pow).then_inc(rstd, 1)

            def p_n(g, at):
                if at.section is FIRST and at.index == 0:
                    input_norms(at)

            def input_norms(at):
                pool.wait_ge(aggr, at("aggr", NB))
                rstd_of(at, 0, 2, mv[:, 0:NB, 1], 0)
                pool.wait_ge(rstd, at("rstd", 2))
                pool.tensor_tensor(rst[:, 1, :], rst[:, 0, :], rst[:, 0, :], ALU.mult).then_inc(rstd, 1)
                pool.wait_ge(rstd, at("rstd", 3))
                pool.tensor_tensor(rst[:, 1, :], rst[:, 1, :], mv[:, 0:NB, 1], ALU.mult).then_inc(rstd, 1)
                pool.wait_ge(rstd, at("rstd", 4))
                rstd_of(at, 4, 2, rst[:, 1, :], 2)
                pool.wait_ge(rstd, at("rstd", 6))
                pool.tensor_tensor(rst[:, 3, :], rst[:, 2, :], rst[:, 0, :], ALU.mult).then_inc(rstd, 1)
                pool.wait_ge(aggr, at("aggr", 2 * NB))
                rstd_of(at, 7, 2, mv[0:SC, NB:2 * NB, 1], 4, SC)

            def p_ln(at, slot):
                pool.wait_ge(aggr, at("aggr", NB))
                rstd_of(at, 0, 2, mv[:, (slot - 3) * NB:(slot - 2) * NB, 1], slot)

            def p_l0a(g, at):
                for m in range(MT):
                    pool.wait_ge(a_done, at("a_done", 2 + m + 1))
                    if m >= 4:
                        pool.wait_ge(qsq_used, at("qsq_used", m - 3))
                    pool.tensor_tensor(qsq[m % 4], qT[:, m, :], qT[:, m, :], ALU.mult).then_inc(qsq_ready, 1)

            def scale_values(at, job_of):
                pool.wait_ge(nrm, at("nrm"))
                for b in range(NB):
                    pool.wait_ge(a_full, at("a_full", job_of(2 * b + 1) + 1))
                    val = v_sb[:, b, :].rearrange("p (h d) -> p h d", h=H)
                    pool.tensor_tensor(val, val, rkh[:, b * H:(b + 1) * H].unsqueeze(2).broadcast_to([SC, H, DH]),
                                       ALU.mult).then_inc(vs_ready, 1)

            def p_kt(g, at):
                scale_values(at, lambda j: j)

            def p_q(g, at):
                if at.before().stage() == "F0K":
                    pool.wait_ge(d_done, at.before()("d_done", y0_job(0) + 1))
                pool.wait_ge(scaled, 2)
                pool.wait_ge(x_loaded, at("x_in"))
                pool.tensor_tensor(x1[:], x_in[:], bias0_sb[:].unsqueeze(1).broadcast_to([128, NB, D]), ALU.add).then_inc(xb_ready, 1)

            def p_l0b(g, at):
                pool.wait_ge(nrm, at("nrm"))
                for n in range(BLK):
                    if n == 10 and at.section is not LAST:
                        input_norms(at.before())
                    pool.wait_ge(zq_loaded[n % RING], at("zq_in", 16 * (n // RING + 1)))
                    blk = er[0:SC, n % RING, :].rearrange("p (h q) -> p h q", h=HB)
                    pool.tensor_tensor(blk, blk, zk[:, n * HB:(n + 1) * HB].unsqueeze(2).broadcast_to([SC, HB, S]),
                                       ALU.add).then_inc(zadd, 1)
                p_ln(at, 5)

            def p_l1(g, at):
                pool.wait_ge(scaled, 7)
                pool.wait_ge(xn2_ready, at("xn2"))
                pool.tensor_tensor(x2[:], x2[:], bias1_sb[:].unsqueeze(1).broadcast_to([128, NB, D]), ALU.add).then_inc(xb_ready, 1)
                for n in range(BLK):
                    blk = er[:, n % RING, 0:HB * SC].rearrange("p (h k) -> p h k", h=HB)
                    pool.wait_ge(rsum, at("rsum", n + 1))
                    pool.tensor_tensor(blk, blk, rrc[:, n % RING, :].unsqueeze(2).broadcast_to([128, HB, SC]),
                                       ALU.mult).then_inc(pnorm, 1)
                p_ln(at, 6)

            def p_f0(g, at):
                if at.stage() == "F0K":
                    scale_values(at, kt_job)
                p_ln(at, 7)

            run_stages(pool, {"N": p_n, "L0A": p_l0a, "KT": p_kt, "Q": p_q, "L0B": p_l0b, "L1": p_l1, "F0": p_f0, "F0K": p_f0})

        @block.scalar
        def _(act):
            act.wait_ge(w_small, N_SMALL)
            nc.scalar.activation(gates[:], gates_in[:], ACT.Tanh).then_inc(gated, 1)

            act.wait_ge(w_proj, 16 * (4 + 2 * 2))
            for hi, lo, whole in PARTS:
                nc.scalar.activation(hi, whole, ACT.Copy).then_inc(w_hi, 1)

            def bank(at, k):
                act.wait_ge(a_full, at("a_full", k + 1))
                return PA[:, at.bank("a_done", A_BANKS, k), :]

            def inputs(at, k, **norm):
                width, hi, whole = ((T, xT[:], x_all), (TC, cT.rearrange("p b k -> p (b k)"), c_all))[k]
                src = bank(at, k)[:, 0:width]
                func = ACT.Identity if norm else ACT.Copy
                nc.scalar.activation(hi, src, func, **norm).then_inc(hi_ready, 1)
                nc.scalar.activation(whole, src, func, **norm).then_inc(a_done, 1)

            def a_l0a(g, at):
                for k in range(2):
                    inputs(at, k, bias=beta_sb[:, 0:1], scale=gamma_sb[:, 0:1])

                def square(b):
                    act.wait_ge(d_done, at("d_done", 2 * b + 2))
                    if b >= 1:
                        act.wait_ge(kn2_ready, at("kn2", b))
                    nc.scalar.activation(vsq[:], v_sb[:, b, :], ACT.Square).then_inc(vsq_ready, 1)

                for m in range(MT):
                    nc.scalar.activation(qT[:, m, :], bank(at, 2 + m), ACT.Copy).then_inc(a_done, 1)
                    if m >= 3 and m % 2 == 1:
                        square((m - 3) // 2)
                square(NB - 1)

            def keys(at, job, j):
                b, t0 = j // 2, 4 * (j % 2)
                src = bank(at, job)[:, 0:4 * SC].rearrange("p (t k) -> p t k", t=4)
                nc.scalar.activation(kz[0:64, b, t0:t0 + 4, 0, :], src[0:64], ACT.Copy)
                nc.scalar.activation(kz[64:128, b, t0:t0 + 4, 1, :], src[64:128], ACT.Copy).then_inc(a_done, 1)

            def a_kt(g, at):
                log_norms(at.latest("L0A"))
                for j in range(2 * NB):
                    keys(at, j, j)

            def log_norms(at):
                act.wait_ge(nrm, at("nrm", 2))
                nc.scalar.activation(lg2[:], n2[:], ACT.Ln).then_inc(logs, 1)
                act.wait_ge(logs, at("logs", 1))
                nc.scalar.activation(rn0[:], lg2[:], ACT.Exp, scale=-0.5).then_inc(logs, 1)

            def a_l0b(g, at):
                for n in range(BLK):
                    act.wait_ge(zadd, at("zadd", n + 1))
                    nc.scalar.activation(er[0:SC, n % RING, :], er[0:SC, n % RING, :], ACT.Tanh).then_inc(tanh_ready, 1)

            def a_l1(g, at):
                act.wait_ge(w_small, N_SMALL)
                if at.before().stage() == "L0B":
                    act.wait_ge(d_done, at.latest("L0B")("d_done", s_job(BLK - RING + 1) + 1))
                for k in range(2):
                    inputs(at, k)
                for m in range(MT):
                    nc.scalar.activation(qT[:, m, :], bank(at, 2 + 2 * m), ACT.Identity,
                                         bias=bq_sb[:, m:m + 1]).then_inc(a_done, 1)
                    src = bank(at, 3 + 2 * m)[:, 0:TC].rearrange("p (b k) -> p b k", b=NB)
                    nc.scalar.activation(kz[0:64, :, m, 0, :], src[0:64], ACT.Identity, bias=bk_sb[0:64, m:m + 1])
                    nc.scalar.activation(kz[64:128, :, m, 1, :], src[64:128], ACT.Identity,
                                         bias=bk_sb[64:128, m:m + 1]).then_inc(a_done, 1)
                for s in range(BLK + AV_LAG):
                    if 1 <= s <= BLK:
                        n = s - 1
                        act.wait_ge(rmax, at("rmax", 2 * n + 2))
                        for i in range(HB):
                            row = er[:, n % RING, i * SC:(i + 1) * SC]
                            last = nc.scalar.activation(row, row, ACT.Exp, bias=nmx[:, n % RING, i:i + 1], scale=DH ** -0.5,
                                                        accum_out=rsm[:, n % RING, i:i + 1])
                        last.then_inc(exp_ready, 1)
                    if T_LAG <= s < BLK + T_LAG:
                        n = s - T_LAG
                        nc.scalar.activation(pT[:, n % RING, :, :], bank(at, t_job(n))[0:SC, :].rearrange(
                            "p (h q) -> p h q", h=HB), ACT.Copy).then_inc(a_done, 1)
                    if s >= AV_LAG + 2 * D_HALVES and (s - AV_LAG) % 2 == 0:
                        k = (s - AV_LAG) // 2
                        nc.scalar.activation(oT[:, k % 2, :, :], bank(at, ot_job(k)).rearrange("p (m q) -> p m q", m=NB),
                                             ACT.Copy).then_inc(a_done, 1)

            def a_f0(g, at):
                nc.scalar.activation(xTf, bank(at, 0), ACT.Copy).then_inc(a_done, 1)
                with_kt = at.stage() == "F0K"
                if with_kt:
                    log_norms(at.latest("L0A"))
                if at.before().stage() == "R1":
                    act.wait_ge(d_done, at.before()("d_done", 1))
                    nc.scalar.activation(gth1[:], lgt1[:], ACT.Tanh, scale=0.5).then_inc(gate1_ready, 1)
                act.wait_ge(m_done, at("m_done", 1))
                nc.scalar.activation(gth[:], lgt[:], ACT.Tanh, scale=0.5).then_inc(gate_ready, 1)
                for j in range(2 * U0):
                    if j >= 2:
                        act.wait_ge(d_done, at("d_done", u0_job((j - 2) // 2, j % 2) + 1))
                    nc.scalar.activation(sg[:, j % 2, :], bank(at, g0_job(with_kt, j // 2, j % 2)), ACT.Silu).then_inc(a_done, 1)
                    if with_kt and j % 2 == 1 and j // 2 < 2 * NB:
                        keys(at, kt_job(j // 2), j // 2)

            def a_r1(g, at):
                nc.scalar.activation(cx_hi[:], bank(at, 0), ACT.Copy)
                nc.scalar.activation(x_all, bank(at, 0), ACT.Copy).then_inc(a_done, 1)

            def a_f1(g, at):
                if at.before().stage() == "R1":
                    act.wait_ge(d_done, at.before()("d_done", 1))
                    nc.scalar.activation(gth1[:], lgt1[:], ACT.Tanh, scale=0.5).then_inc(gate1_ready, 1)
                for j in range(U1):
                    if j >= 2:
                        act.wait_ge(d_done, at("d_done", u1_job(j - 2) + 1))
                    parts = 64 if j == 0 else 128
                    nc.scalar.activation(sg[0:parts, j % 2, :], bank(at, j)[0:parts, :], ACT.Silu).then_inc(a_done, 1)

            run_stages(act, {"L0A": a_l0a, "KT": a_kt, "F0K": a_f0, "L0B": a_l0b, "L1": a_l1, "R1": a_r1, "F0": a_f0, "F1": a_f1})

        @block.vector
        def _(dve):
            for k, (hi, lo, whole) in enumerate(PARTS):
                dve.wait_ge(w_hi, k + 1)
                nc.vector.tensor_tensor(lo, whole, hi.bitcast(F32), ALU.subtract).then_inc(w_lo, 1)
            dve.wait_ge(const, N_CONST)
            dve.wait_ge(gated, 1)
            dve.wait_ge(w_attn0, 16)
            nc.vector.tensor_scalar(wout_sb[:], wout_sb[:], gates[:, 0:1], 0.5, ALU.mult, ALU.mult).then_inc(scaled, 1)
            nc.vector.tensor_scalar(bias0_sb[:], bias0_sb[:], gates[:, 0:1], None, ALU.mult).then_inc(scaled, 1)
            nc.vector.tensor_scalar(bias1_sb[:], bias1_sb[:], gates[:, 1:2], None, ALU.mult).then_inc(scaled, 1)

            def scale_ffn0():
                dve.wait_ge(w_ffn0, 48)
                nc.vector.tensor_scalar(w0d_sb[:], w0d_sb[:], gates[:, 2:3], None, ALU.mult).then_inc(scaled, 1)

            def scale_rest():
                dve.wait_ge(w_attn1, 16)
                nc.vector.tensor_scalar(wo_sb[:], wo_sb[:], gates[:, 1:2], None, ALU.mult).then_inc(scaled, 1)
                for m in range(MT):
                    nc.vector.tensor_copy(oT[:].rearrange("p a b q -> p (a b) q")[:, m, :],
                                          bv_sb[:, m:m + 1].broadcast_to([128, 128])).then_inc(bvb, 1)
                dve.wait_ge(w_ffn1, 16 * 3)
                nc.vector.tensor_scalar(w1d_sb[:], w1d_sb[:], gates[:, 3:4], None, ALU.mult).then_inc(scaled, 1)
                dve.wait_ge(bias1_full, 1)
                nc.vector.tensor_tensor(bias1_sb[:], PM[:, 0:D], bias1_sb[:], ALU.add).then_inc(scaled, 1)

            def bank(at, k):
                dve.wait_ge(d_full, at("d_full", k + 1))
                return PD[:, at.bank("d_done", D_BANKS, k), :]

            def row_stats(at, k, src, slot, parts):
                for b in range(NB):
                    nc.vector.bn_stats(stats[0:parts, slot + b, :], src[:, b, :]).then_inc(stat, 1)
                dve.wait_ge(stat, at("stat", k + NB))
                nc.vector.tensor_copy(held[0:parts, :], stats[0:parts, slot, 0:1])
                for b in range(NB):
                    nc.vector.bn_aggr(mv[0:parts, slot + b, :], stats[0:parts, slot + b, :]).then_inc(aggr, 1)

            def normalise(src, dst, slot, r, parts, ready):
                for b in range(NB):
                    nc.vector.tensor_scalar(dst[:, b, :], src[:, b, :], mv[0:parts, slot + b, 0:1],
                                            rst[0:parts, r, b:b + 1], ALU.subtract, ALU.mult).then_inc(ready, 1)

            def input_norms(at, step):
                if step == 0:
                    dve.wait_ge(x_loaded, at("x_in", 16))
                    row_stats(at, 0, x_in, 0, 128)
                if step == 1:
                    dve.wait_ge(c_loaded, at("c_in", 16))
                    row_stats(at, NB, c_in, NB, SC)
                if step == 2:
                    dve.wait_ge(rstd, at("rstd", 7))
                    normalise(x_in, xn["L0A"], 0, 3, 128, xn0_ready)
                if step == 3:
                    dve.wait_ge(rstd, at("rstd", 9))
                    normalise(c_in, c_in, NB, 4, SC, xn0_ready)

            def v_n(g, at):
                if at.section is FIRST and at.index == 0:
                    for step in range(4):
                        input_norms(at, step)
                elif at.section is FIRST:
                    scale_ffn0()

            def lower_parts(at):
                dve.wait_ge(a_done, at("a_done", 1))
                nc.vector.tensor_tensor(xT_lo[:], x_all, xT[:].bitcast(F32), ALU.subtract).then_inc(lo_ready, 1)
                dve.wait_ge(a_done, at("a_done", 2))
                nc.vector.tensor_tensor(cT_lo, c_all.rearrange("p (b k) -> p b k", b=NB), cT.bitcast(F32),
                                        ALU.subtract).then_inc(lo_ready, 1)

            def v_l0a(g, at):
                if at.section is FIRST:
                    lower_parts(at)

                def key_norms(b):
                    dve.wait_ge(vsq_ready, at("vsq", b + 1))
                    nc.vector.tensor_reduce(nw[0:SC, 1, b * H:(b + 1) * H],
                                            vsq[:].rearrange("p (h d) -> p h d", h=H), AX_X, ALU.add).then_inc(kn2_ready, 1)

                for j in range(2 * NB):
                    b, half = j // 2, j % 2
                    nc.vector.tensor_copy(v_sb[:, b, half * 512:half * 512 + 512], bank(at, j)[0:SC, :]).then_inc(d_done, 1)
                    if j >= 4 and j % 2 == 0:
                        key_norms((j - 4) // 2)
                    if j == 1 and at.before().stage() == "L1":
                        finish_norm(at.before(), x3, xn["F1"], 6, xn3_ready)
                    if j == 1 and at.before().stage() == "L0B":
                        finish_norm(at.before(), x1, xn["F0"], 5, xn1_ready)
                key_norms(NB - 2)
                key_norms(NB - 1)
                dve.wait_ge(kn2_ready, at("kn2", NB))
                nc.vector.tensor_scalar(n2[0:SC, 1, :], nw[0:SC, 1, :], NORM2_MIN, None, ALU.max).then_inc(nrm, 1)
                dve.wait_ge(m_full, at("m_full", 1))
                nc.vector.tensor_copy(hsum, PM[0:H, :]).then_inc(m_done, 1)
                dve.wait_ge(m_full, at("m_full", 2))
                nc.vector.tensor_scalar(n2[:, 0, :], PM[:, 0:NB * H], NORM2_MIN, None, ALU.max).then_inc(m_done, 1)
                dve.wait_ge(m_done, at("m_done", 2))
                nc.vector.tensor_scalar(nw[:], n2[:], -0.5, None, ALU.mult).then_inc(nrm, 1)
                dve.wait_ge(logs, at("logs", 2))
                dve.wait_ge(nrm, at("nrm", 2))
                nc.vector.tensor_tensor(nw2[:], rn0[:], rn0[:], ALU.mult).then_inc(nrm, 1)
                dve.wait_ge(nrm, at("nrm", 3))
                nc.vector.tensor_tensor(nw2[:], nw2[:], nw[:], ALU.mult).then_inc(nrm, 1)
                nc.vector.tensor_scalar(qrow[:, 0, :], lg2[:, 0, :], 0.25, None, ALU.mult).then_inc(nrm, 1)
                dve.wait_ge(nrm, at("nrm", 5))
                nc.vector.scalar_tensor_tensor(qrow[:, 1, :], nw2[:, 0, :], 1.5, rn0[:, 0, :], ALU.add, ALU.mult).then_inc(nrm, 1)
                nc.vector.scalar_tensor_tensor(rkh[:], nw2[0:SC, 1, :], 1.5, rn0[0:SC, 1, :], ALU.add, ALU.mult).then_inc(nrm, 1)
                nc.vector.tensor_scalar(zk[:], lg2[0:SC, 1, :], 0.25, -HALF_LOG_COS_EPS, ALU.mult, ALU.add).then_inc(nrm, 1)

            def residual(at, src, dst):
                dve.wait_ge(xb_ready, at("xb", 1 if at.stage() == "L1" else 0))
                dve.wait_ge(m_full, at("m_full", 1))
                nc.vector.tensor_tensor(dst[:], PM[:].rearrange("p (b d) -> p b d", b=NB), src[:], ALU.add).then_inc(m_done, 1)
                dve.wait_ge(m_done, at("m_done", 1))

            def finish_norm(at, src, dst, r, ready):
                dve.wait_ge(rstd, at("rstd", 2))
                normalise(src, dst, (r - 3) * NB, r, 128, ready)

            def v_l0b(g, at):
                dve.wait_ge(scaled, 3)
                for s in range(BLK + 4):
                    if s < BLK:
                        dve.wait_ge(tanh_ready, at("tanh", s + 1))
                        nc.vector.scalar_tensor_tensor(pT[:, s % RING, :, :].rearrange("p h q -> p (h q)"),
                                                       er[0:SC, s % RING, :], 1.0, bank(at, s_job(s))[0:SC, :],
                                                       ALU.add, ALU.mult).then_inc(d_done, 1)
                    if s >= 3 and s % 2 == 1 and (s - 3) // 2 < 2 * NB:
                        if s in (7, 9, 13, 15) and at.section is not LAST:
                            input_norms(at.before(), (7, 9, 13, 15).index(s))
                        k = (s - 3) // 2
                        dve.wait_ge(ab_loaded[k % 2], at("ab_in", 32 * (k // 2 + 1)))
                        nc.vector.tensor_tensor(oT[:, k % 2, :, :], bank(at, av_job(k)).rearrange("p (m q) -> p m q", m=NB),
                                                ab[:, k % 2, :, :], ALU.mult).then_inc(d_done, 1)
                if at.section is not FIRST:
                    lower_parts(at.coming("L1"))
                residual(at, x1, x1)
                row_stats(at, 0, x1, 2 * NB, 128)

            def v_l1(g, at):
                if at.before().stage() == "F1":
                    lower_parts(at)
                dve.wait_ge(mask_loaded, at("mask_in"))
                nc.vector.tensor_scalar(maskb.rearrange("p b k -> p (b k)"), mask_in[:], 0.0, MASKED,
                                        ALU.is_equal, ALU.mult).then_inc(mask_ready, 1)
                dve.wait_ge(mask_ready, at("mask", 1))
                nc.vector.tensor_tensor(maskb, maskb, causal[:].unsqueeze(1).broadcast_to([128, NB, SC]),
                                        ALU.add).then_inc(mask_ready, 1)

                def masked_scores(n):
                    blk = er[:, n % RING, 0:HB * SC].rearrange("p (h k) -> p h k", h=HB)
                    if n >= RING:
                        dve.wait_ge(a_full, at("a_full", t_job(n - RING) + 1))
                    nc.vector.tensor_tensor(blk, bank(at, s1_job(n))[:, 0:HB * SC].rearrange("p (h k) -> p h k", h=HB),
                                            maskb[:, n * HB // H, :].unsqueeze(1).broadcast_to([128, HB, SC]),
                                            ALU.add).then_inc(d_done, 1)
                    dve.wait_ge(d_done, at("d_done", s1_job(n) + 1))
                    nc.vector.tensor_reduce(rmx[:, n % RING, :], blk, AX_X, ALU.max).then_inc(rmax, 1)
                    dve.wait_ge(rmax, at("rmax", 2 * n + 1))
                    nc.vector.tensor_scalar(nmx[:, n % RING, :], rmx[:, n % RING, :], -DH ** -0.5, None, ALU.mult).then_inc(rmax, 1)

                for j in range(2 * NB):
                    b, half = j // 2, j % 2
                    nc.vector.tensor_copy(v_sb[:, b, half * 512:half * 512 + 512], bank(at, v1_job(j))[0:SC, :]).then_inc(d_done, 1)
                    if j == 4:
                        dve.wait_ge(mask_ready, at("mask", 2))
                    if j in (4, 5):
                        masked_scores(j - 4)
                for s in range(EARLY, BLK + 2):
                    if s < BLK:
                        masked_scores(s)
                    if s == 5 and at.before().stage() == "L0B":
                        finish_norm(at.before(), x1, xn["F0"], 5, xn1_ready)
                    if s >= 2:
                        n = s - 2
                        dve.wait_ge(exp_ready, at("exp", n + 1))
                        nc.vector.reciprocal(rrc[:, n % RING, :], rsm[:, n % RING, :]).then_inc(rsum, 1)
                    if s >= AV_LAG and (s - AV_LAG) % 2 == 0 and (s - AV_LAG) // 2 < D_HALVES:
                        k = (s - AV_LAG) // 2
                        nc.vector.tensor_copy(oT[:, k % 2, :, :], bank(at, ov_job(k)).rearrange("p (m q) -> p m q", m=NB)).then_inc(d_done, 1)
                if at.section is LOOP:
                    lower_parts(at.coming("L0A"))
                dve.wait_ge(out_written, at("out", 16))
                residual(at, x2, x3)
                row_stats(at, 0, x3, 3 * NB, 128)
                if at.section is LAST:
                    finish_norm(at, x3, xn["F1"], 6, xn3_ready)

            def ranks(done, name, at, k, scores, tri, n, beats, ties):
                mine = scores[:, :, 0:n].unsqueeze(3).broadcast_to([128, NB, n, n])
                other = scores[:, :, 0:n].unsqueeze(2).broadcast_to([128, NB, n, n])
                tri_b = tri[:].unsqueeze(1).broadcast_to([128, NB, n, n])
                nc.vector.tensor_tensor(beats, other, mine, ALU.is_gt).then_inc(done, 1)
                nc.vector.tensor_tensor(ties, other, mine, ALU.is_ge).then_inc(done, 1)
                dve.wait_ge(done, at(name, k + 2))
                nc.vector.tensor_tensor(ties, ties, tri_b, ALU.mult).then_inc(done, 1)
                dve.wait_ge(done, at(name, k + 3))
                nc.vector.tensor_tensor(beats, beats, ties, ALU.max).then_inc(done, 1)
                dve.wait_ge(done, at(name, k + 4))
                nc.vector.tensor_reduce(rank[:, :, 0:n], beats, AX_X, ALU.add).then_inc(done, 1)
                dve.wait_ge(done, at(name, k + 5))

            pairs = biased[:].rearrange("p b (n r) -> p b n r", r=2)

            def flat(tile):
                return tile[:].rearrange("p b e -> p (b e)")

            def router0(at):
                dve.wait_ge(gate_ready, at("gate", 1))
                nc.vector.tensor_scalar(prob[:], gth[:], 0.5, 0.5, ALU.mult, ALU.add).then_inc(route, 1)
                dve.wait_ge(route, at("route", 1))
                ranks(route, "route", at, 1, prob, before, E, cmp_a[:], cmp_b[:])
                nc.vector.scalar_tensor_tensor(flat(cw0), flat(rank), 2.0, flat(prob), ALU.is_lt, ALU.mult).then_inc(route, 1)
                dve.wait_ge(route, at("route", 7))

            def router1(at):
                dve.wait_ge(gate1_ready, at("gate1", 1))
                nc.vector.tensor_scalar(prob1[:], gth1[:], 0.5, 0.5, ALU.mult, ALU.add).then_inc(route1, 1)
                dve.wait_ge(route1, at("route1", 1))
                nc.vector.tensor_tensor(biased[:], prob1[:], c1b_sb[:].unsqueeze(1).broadcast_to([128, NB, E]),
                                        ALU.add).then_inc(route1, 1)
                dve.wait_ge(route1, at("route1", 2))
                nc.vector.tensor_tensor(gsum[:], pairs[:, :, :, 0], pairs[:, :, :, 1], ALU.add).then_inc(route1, 1)
                dve.wait_ge(route1, at("route1", 3))

            def router1_groups(at):
                ranks(route1, "route1", at, 3, gsum, before4, E // 2, cmp_a[:, :, 0:E // 2, 0:E // 2], cmp_b[:, :, 0:E // 2, 0:E // 2])
                nc.vector.tensor_scalar(gsel[:], rank[:, :, 0:E // 2], 2.0, None, ALU.is_lt).then_inc(route1, 1)
                dve.wait_ge(route1, at("route1", 9))
                nc.vector.tensor_tensor(choice[:].rearrange("p b (n r) -> p b n r", r=2), pairs,
                                        gsel[:].unsqueeze(3).broadcast_to([128, NB, E // 2, 2]), ALU.mult).then_inc(route1, 1)
                dve.wait_ge(route1, at("route1", 10))

            def router1_experts(at):
                ranks(route1, "route1", at, 10, choice, before, E, cmp_a[:], cmp_b[:])
                nc.vector.scalar_tensor_tensor(flat(wsel), flat(rank), 4.0, flat(prob1), ALU.is_lt, ALU.mult).then_inc(route1, 1)
                dve.wait_ge(route1, at("route1", 16))
                nc.vector.tensor_reduce(wsum[:], wsel[:], AX_X, ALU.add).then_inc(route1, 1)
                dve.wait_ge(route1, at("route1", 17))
                nc.vector.tensor_scalar(wrec[:], wsum[:], 1e-20, 1 / ROUTE_SCALE, ALU.add, ALU.mult).then_inc(route1, 1)
                dve.wait_ge(route1, at("route1", 18))
                nc.vector.reciprocal(wsum[:], wrec[:]).then_inc(route1, 1)
                dve.wait_ge(route1, at("route1", 19))
                nc.vector.tensor_tensor(cw1[:], wsel[:], wsum[:].unsqueeze(2).broadcast_to([128, NB, E]),
                                        ALU.mult).then_inc(route1, 1)
                dve.wait_ge(route1, at("route1", 20))

            def v_f0(g, at):
                dve.wait_ge(m_full, at("m_full", 1))
                nc.vector.tensor_tensor(lgt[:], PM[:, 0:NB * E].rearrange("p (b e) -> p b e", b=NB),
                                        r0b_sb[:].unsqueeze(1).broadcast_to([128, NB, E]), ALU.add).then_inc(m_done, 1)
                for u in range(U0 + 1):
                    if u < U0:
                        for half in range(2):
                            dve.wait_ge(a_done, at("a_done", g0_job(at.stage() == "F0K", u, half) + 1))
                            nc.vector.tensor_tensor(hid[:, u % 2, half, :], bank(at, u0_job(u, half)), sg[:, half, :],
                                                    ALU.mult).then_inc(d_done, 1)
                    if u == 1:
                        router0(at)
                    if u in (3, 4, 5) and at.before().stage() == "R1":
                        (router1, router1_groups, router1_experts)[u - 3](at.before())
                    if u >= 1:
                        y = bank(at, y0_job(u - 1)).rearrange("p (b d) -> p b d", b=NB)
                        if u == 1:
                            nc.vector.tensor_tensor(x2[:], y, x1[:], ALU.add).then_inc(d_done, 1)
                        else:
                            e = u - 2
                            dve.wait_ge(d_done, at("d_done", y0_job(e) + 1))
                            for b in range(NB):
                                add = nc.vector.scalar_tensor_tensor(x2[:, b, :], y[:, b, :], cw0[:, b, e:e + 1],
                                                                     x2[:, b, :], ALU.mult, ALU.add)
                            add.then_inc(d_done, 1)
                dve.wait_ge(d_done, at("d_done", D_JOBS["F0"]))
                row_stats(at, 0, x2, 4 * NB, 128)
                if at.section is LAST:
                    finish_norm(at, x2, xn["L1"], 7, xn2_ready)

            def v_q(g, at):
                nc.vector.tensor_copy(qrowT[:], bank(at, 0)[:, 0:128]).then_inc(d_done, 1)
                if at.section is FIRST and at.before().stage() == "F0K":
                    finish_norm(at.before(), x2, xn["L1"], 7, xn2_ready)
                if at.section is FIRST and at.before().stage() == "F0K":
                    scale_rest()

            def v_r1(g, at):
                dve.wait_ge(a_done, at("a_done", 1))
                nc.vector.tensor_tensor(cx_lo[:], x_all, cx_hi[:].bitcast(F32), ALU.subtract).then_inc(lo_ready, 1)
                nc.vector.tensor_copy(lgt1[:], bank(at, 0)[:, 0:NB * E].rearrange("p (b e) -> p b e", b=NB)).then_inc(d_done, 1)

            def v_f1(g, at):
                for u in range(U1 + 1):
                    if u < U1:
                        parts = 64 if u == 0 else 128
                        dve.wait_ge(a_done, at("a_done", 1 + u))
                        nc.vector.tensor_tensor(hid[0:parts, u % 2, 0, :], bank(at, u1_job(u))[0:parts, :],
                                                sg[0:parts, u % 2, :], ALU.mult).then_inc(d_done, 1)
                    if u == 1:
                        if at.before().stage() == "R1":
                            router1(at.before())
                            router1_groups(at.before())
                            router1_experts(at.before())
                        y = bank(at, y1_job(0)).rearrange("p (b d) -> p b d", b=NB)
                        nc.vector.tensor_tensor(x3[:], y, x3[:], ALU.add).then_inc(d_done, 1)
                    if u == 2 and at.section is LOOP:
                        finish_norm(at.latest("F0K"), x2, xn["L1"], 7, xn2_ready)
                    if u >= 2:
                        for part in range(2):
                            dve.wait_ge(d_done, at("d_done", y1_job(u - 2, part if u > 2 else 0) + 1))
                            y = bank(at, y1_job(u - 1, part)).rearrange("p (b e d) -> p b e d", b=2, e=2)
                            for r in range(2):
                                e = 2 * (u - 2) + r
                                for b in range(2):
                                    tile = x3[:, 2 * part + b, :]
                                    step = nc.vector.scalar_tensor_tensor(tile, y[:, b, r, :], cw1[:, 2 * part + b, e:e + 1],
                                                                          tile, ALU.mult, ALU.add)
                                    last = r == 1 and b == 1
                                    step.then_inc(d_done if last else added, 1)
                                if r == 0:
                                    dve.wait_ge(added, at("added", 3 * (2 * (u - 2) + part) + 2))

            run_stages(dve, {"N": v_n, "L0A": v_l0a, "Q": v_q, "L0B": v_l0b, "L1": v_l1, "R1": v_r1, "F0": v_f0, "F0K": v_f0, "F1": v_f1})

        @block.tensor
        def _(pe):
            def a_bank(at, k, needs=-10 ** 6):
                done = at("a_done", max(at.freed("a_done", A_BANKS, k), needs))
                if at.section is not FIRST or done > 0:
                    pe.wait_ge(a_done, done)
                return PA[:, at.bank("a_done", A_BANKS, k), :]

            def d_bank(at, k, needs=-10 ** 6):
                done = at("d_done", max(at.freed("d_done", D_BANKS, k), needs))
                if at.section is not FIRST or done > 0:
                    pe.wait_ge(d_done, done)
                return PD[:, at.bank("d_done", D_BANKS, k), :]

            def m_bank(at):
                if not (at.section is FIRST and at.index == 1):
                    pe.wait_ge(m_done, at("m_done"))
                return PM

            def turn_tiles(at, k, src, parts, width):
                dst = a_bank(at, k)
                for b in range(NB):
                    last = pe.transpose(dst[:, b * width:b * width + width], src[:, b, :], ident[0:parts, 0:parts])
                last.then_inc(a_full, 1)

            def head_norms(at, m):
                if m == 0:
                    m_bank(at)
                pe.wait_ge(qsq_ready, at("qsq", m + 1))
                pe.matmul(PM[0:H, :], head_of[:, m, :], qsq[m % 4], start=(m == 0),
                          stop=(m == MT - 1)).then_inc(m_full if m == MT - 1 else qsq_used, 1)

            def last_head_norms(at):
                for m in range(MT - 3, MT):
                    head_norms(at, m)

            def turn_head_norms(at):
                pe.wait_ge(m_done, at("m_done", 1))
                for b in range(NB):
                    last = pe.matmul(PM[:, b * H:(b + 1) * H], hsum[:, b * S:(b + 1) * S], ident[0:H, 0:H], start=True, stop=True)
                last.then_inc(m_full, 1)

            def product(dst, left, right, rest=None):
                pe.matmul(dst, left[0], right[0], start=True, stop=False)
                pe.matmul(dst, left[1], right[0], start=False, stop=False)
                if rest is not None:
                    pe.wait_ge(lo_ready, rest)
                return pe.matmul(dst, left[0], right[1], start=False, stop=True)

            def values(at, job, weights, j):
                b, half = j // 2, j % 2
                cols = slice(half * 512, half * 512 + 512)
                product(d_bank(at, job)[0:SC, :], (cT[:, b, :], cT_lo[:, b, :]),
                        (weights[0][:, cols], weights[1][:, cols])).then_inc(d_full, 1)

            def t_l0a(g, at):
                if at.section is FIRST and at.index == 1:
                    pe.wait_ge(const, N_CONST)
                    pe.wait_ge(w_lo, len(PARTS))
                pe.wait_ge(xn0_ready, at("xn0", -NB))
                turn_tiles(at, 0, xn["L0A"], 128, S)
                pe.wait_ge(xn0_ready, at("xn0"))
                turn_tiles(at, 1, c_in, SC, SC)
                if at.before().stage() == "L1":
                    finish_l1(at.before())
                for m in range(MT):
                    rows = slice(m * 128, (m + 1) * 128)
                    dst = a_bank(at, 2 + m)
                    if m == 0:
                        pe.wait_ge(hi_ready, at("hi", 1))
                    product(dst, (win_hi[:, rows], win_lo[:, rows]), (xT[:], xT_lo[:]),
                            at("lo", 1) if m == 0 else None).then_inc(a_full, 1)
                    if m == 0:
                        pe.wait_ge(lo_ready, at("lo", 2))
                    values(at, m, (win_hi, win_lo), m)
                    if m >= 3:
                        head_norms(at, m - 3)

            def turn_keys(at, job, j):
                b, t0 = j // 2, 4 * (j % 2)
                dst = a_bank(at, job)
                for i in range(4):
                    last = pe.transpose(dst[:, i * SC:(i + 1) * SC], v_sb[:, b, (t0 + i) * 128:(t0 + i + 1) * 128],
                                        ident[0:SC, 0:SC])
                last.then_inc(a_full, 1)

            def t_kt(g, at):
                pe.wait_ge(d_done, at("d_done"))
                for j in range(2 * NB):
                    turn_keys(at, j, j)
                    if j == 1:
                        last_head_norms(at.latest("L0A"))
                    if j == 3:
                        turn_head_norms(at.latest("L0A"))

            def t_q(g, at):
                pe.wait_ge(nrm, at("nrm", -2))
                pe.transpose(d_bank(at, 0)[:, 0:128], qrow[:].rearrange("p a b -> p (a b)"), ident[:]).then_inc(d_full, 1)
                if at.section is FIRST and at.before().stage() == "F0K":
                    pe.wait_ge(scaled, 5)
                    pe.wait_ge(bvb, MT)
                    pe.wait_ge(m_done, at("m_done"))
                    for m in range(MT):
                        last = pe.matmul(PM[:, 0:D], oT[:].rearrange("p a b q -> p (a b) q")[:, m, :], wo_sb[:, m, :],
                                         start=(m == 0), stop=(m == MT - 1))
                    last.then_inc(bias1_full, 1)
                    pe.wait_ge(scaled, 7)
                    pe.wait_ge(w_small, N_SMALL)

            def attention_out(dst, k):
                b = k // 2
                for i in range(8):
                    h = 8 * (k % 2) + i
                    last = pe.matmul(dst[64 * (i % 2):64 * (i % 2) + 64, (i // 2) * S:(i // 2 + 1) * S],
                                     v_sb[:, b, h * DH:(h + 1) * DH], pT[:, (2 * k + i // 4) % RING, i % 4, :],
                                     start=True, stop=True)
                return last

            def project_out(k, weights):
                b, half = k // 2, k % 2
                for i in range(4):
                    last = pe.matmul(PM[:, b * D:(b + 1) * D], oT[:, k % 2, i, :], weights[:, 4 * half + i, :],
                                     start=(half == 0 and i == 0), stop=(half == 1 and i == 3))
                return last

            def t_l0b(g, at):
                pe.wait_ge(scaled, 3)
                for s in range(BLK + 4):
                    if s < BLK:
                        b = s * HB // H
                        if s == 0:
                            pe.wait_ge(a_done, at("a_done"))
                        dst = d_bank(at, s_job(s))
                        for i in range(HB):
                            h = (s * HB + i) % H
                            last = pe.matmul(dst[0:SC, i * S:(i + 1) * S], kz[:, b, h // 2, h % 2, :],
                                             qT[:, h // 2, b * S:(b + 1) * S], start=True, stop=True)
                        last.then_inc(d_full, 1)
                    if s >= 5 and s % 2 == 1 and (s - 5) // 2 < 2 * NB - L0B_LATE:
                        k = (s - 5) // 2
                        if k == 0:
                            m_bank(at)
                        pe.wait_ge(d_done, at("d_done", av_job(k) + 1))
                        project_out(k, wout_sb)
                    if s >= 3 and s % 2 == 1 and (s - 3) // 2 < 2 * NB:
                        k = (s - 3) // 2
                        pe.wait_ge(vs_ready, at("vs", 0))
                        dst = d_bank(at, av_job(k), s_job(2 * k + 1) + 1)
                        attention_out(dst, k).then_inc(d_full, 1)
                if at.section is FIRST:
                    finish_l0b(at)

            def finish_l0b(at):
                for k in range(2 * NB - L0B_LATE, 2 * NB):
                    pe.wait_ge(d_done, at("d_done", av_job(k) + 1))
                    last = project_out(k, wout_sb)
                last.then_inc(m_full, 1)

            def finish_l1(at):
                pe.wait_ge(a_done, at("a_done", ot_job(2 * NB - 1) + 1))
                project_out(2 * NB - 1, wo_sb).then_inc(m_full, 1)

            def t_l1(g, at):
                pe.wait_ge(craw_loaded, at("craw_in"))
                pe.wait_ge(xn2_ready, at("xn2"))
                turn_tiles(at, 0, xn["L1"], 128, S)
                turn_tiles(at, 1, c_raw, SC, SC)
                if at.before().stage() == "L0B":
                    finish_l0b(at.latest("L0B"))

                def scores(n):
                    b = n * HB // H
                    dst = d_bank(at, s1_job(n))
                    if n < EARLY:
                        pe.wait_ge(a_done, at("a_done", 2 + 4 * (n + 1)))
                    for i in range(2):
                        t = (n * HB + 2 * i) % H // 2
                        last = pe.matmul(dst[:, i * 2 * SC:(i + 1) * 2 * SC], qT[:, t, b * S:(b + 1) * S],
                                         kz[:, b, t, :, :].rearrange("p r k -> p (r k)"), start=True, stop=True)
                    last.then_inc(d_full, 1)

                for m in range(MT):
                    rows = slice(m * 128, (m + 1) * 128)
                    dst = a_bank(at, 2 + 2 * m)
                    if m == 0:
                        pe.wait_ge(hi_ready, at("hi", 1))
                    product(dst, (wq_hi[:, rows], wq_lo[:, rows]), (xT[:], xT_lo[:]),
                            at("lo", 1) if m == 0 else None).then_inc(a_full, 1)
                    dst = a_bank(at, 3 + 2 * m)[:, 0:TC]
                    if m == 0:
                        pe.wait_ge(hi_ready, at("hi", 2))
                    product(dst, (wk_hi[:, rows], wk_lo[:, rows]),
                            (cT.rearrange("p b k -> p (b k)"), cT_lo.rearrange("p b k -> p (b k)")),
                            at("lo", 2) if m == 0 else None).then_inc(a_full, 1)
                    if m >= 2:
                        values(at, v1_job(m - 2), (wv_hi, wv_lo), m - 2)
                    if m >= 6:
                        scores(m - 6)
                for j in (2 * NB - 2, 2 * NB - 1):
                    values(at, v1_job(j), (wv_hi, wv_lo), j)
                for s in range(EARLY, BLK + AV_LAG + 2):
                    if s < BLK:
                        if s == EARLY:
                            pe.wait_ge(a_done, at("a_done", 2 + 2 * MT))
                        scores(s)
                    if T_LAG <= s < BLK + T_LAG:
                        n = s - T_LAG
                        dst = a_bank(at, t_job(n))
                        pe.wait_ge(pnorm, at("pnorm", n + 1))
                        for i in range(HB):
                            last = pe.transpose(dst[0:SC, i * S:(i + 1) * S], er[:, n % RING, i * SC:(i + 1) * SC], ident[:])
                        last.then_inc(a_full, 1)
                    if s >= AV_LAG + 2 and s % 2 == 0 and (s - AV_LAG - 2) // 2 < 2 * NB - 1:
                        k = (s - AV_LAG - 2) // 2
                        if k == 0:
                            m_bank(at)
                        if k < D_HALVES:
                            pe.wait_ge(d_done, at("d_done", ov_job(k) + 1))
                        else:
                            pe.wait_ge(a_done, at("a_done", ot_job(k) + 1))
                        project_out(k, wo_sb)
                    if s >= AV_LAG and s % 2 == 0 and (s - AV_LAG) // 2 < 2 * NB:
                        k = (s - AV_LAG) // 2
                        if k < D_HALVES:
                            dst = d_bank(at, ov_job(k))
                            pe.wait_ge(a_done, at("a_done", t_job(2 * k + 1) + 1))
                            attention_out(dst, k).then_inc(d_full, 1)
                        else:
                            dst = a_bank(at, ot_job(k), t_job(2 * k + 1) + 1)
                            attention_out(dst, k).then_inc(a_full, 1)
                if at.section is LAST:
                    finish_l1(at)

            def router(dst, xT_of, weights):
                for b in range(NB):
                    last = pe.matmul(dst[:, b * E:(b + 1) * E], xT_of[:, b * S:(b + 1) * S], weights[:], start=True, stop=True)
                return last

            def t_f0(g, at):
                if at.section is FIRST:
                    pe.wait_ge(scaled, 4)
                pe.wait_ge(xn1_ready, at("xn1"))
                with_kt = at.stage() == "F0K"
                if at.before().stage() == "L0A":
                    last_head_norms(at.before())
                turn_tiles(at, 0, xn["F0"], 128, S)
                if with_kt:
                    turn_head_norms(at.latest("L0A"))
                m_bank(at)
                pe.wait_ge(a_done, at("a_done", 1))
                router(PM, xTf, w0r_sb).then_inc(m_full, 1)
                for u in range(U0 + 1):
                    if u < U0:
                        w = U0 - 1 if u == 0 else u - 1
                        for half in range(2):
                            cols = slice(half * 128, half * 128 + 128)
                            pe.matmul(a_bank(at, g0_job(with_kt, u, half)), w0g_sb[:, w, cols], xTf, start=True, stop=True).then_inc(a_full, 1)
                            pe.matmul(d_bank(at, u0_job(u, half)), w0u_sb[:, w, cols], xTf, start=True, stop=True).then_inc(d_full, 1)
                    if with_kt and u < 2 * NB:
                        turn_keys(at, kt_job(u), u)
                    if u >= 1:
                        w = U0 - 1 if u == 1 else u - 2
                        dst = d_bank(at, y0_job(u - 1), u0_job(u - 1, 1) + 1)
                        for b in range(NB):
                            for half in range(2):
                                last = pe.matmul(dst[:, b * D:(b + 1) * D], hid[:, (u - 1) % 2, half, b * S:(b + 1) * S],
                                                 w0d_sb[:, w, half, :], start=(half == 0), stop=(half == 1))
                        last.then_inc(d_full, 1)

            def t_r1(g, at):
                pe.wait_ge(xn3_ready, at("xn3"))
                turn_tiles(at, 0, xn["F1"], 128, S)
                if at.before().stage() == "L0A":
                    last_head_norms(at.before())
                dst = d_bank(at, 0)
                pe.wait_ge(a_done, at("a_done", 1))
                router(dst, x_all, w1r_sb).then_inc(d_full, 1)

            def t_f1(g, at):
                for u in range(U1 + 1):
                    if u < U1:
                        w, rows = (U1 - 1, 64) if u == 0 else (u - 1, 128)
                        if u == 0:
                            pe.wait_ge(lo_ready, at("lo"))
                        product(a_bank(at, u)[0:rows, :], (w1g_hi[:, w, 0:rows], w1g_lo[:, w, 0:rows]),
                                (cx_hi[:], cx_lo[:])).then_inc(a_full, 1)
                        product(d_bank(at, u1_job(u))[0:rows, :], (w1u_hi[:, w, 0:rows], w1u_lo[:, w, 0:rows]),
                                (cx_hi[:], cx_lo[:])).then_inc(d_full, 1)
                    if u == 1:
                        dst = d_bank(at, y1_job(0), u1_job(0) + 1)
                        for b in range(NB):
                            last = pe.matmul(dst[:, b * D:(b + 1) * D], hid[0:64, 0, 0, b * S:(b + 1) * S],
                                             w1d_sb[0:64, U1 - 1, 0, :], start=True, stop=True)
                        last.then_inc(d_full, 1)
                    if u >= 2:
                        for part in range(2):
                            dst = d_bank(at, y1_job(u - 1, part), u1_job(u - 1) + 1)
                            for i in range(2):
                                b = 2 * part + i
                                last = pe.matmul(dst[:, i * 256:(i + 1) * 256], hid[:, (u - 1) % 2, 0, b * S:(b + 1) * S],
                                                 w1d_sb[:, u - 2, :, :].rearrange("p r d -> p (r d)"), start=True, stop=True)
                            last.then_inc(d_full, 1)

            run_stages(pe, {"L0A": t_l0a, "KT": t_kt, "F0K": t_f0, "Q": t_q, "L0B": t_l0b, "L1": t_l1, "R1": t_r1, "F0": t_f0, "F1": t_f1})


def kernel(**inputs):
    import numpy as _np
    import concourse.bacc as _bacc
    from concourse import mybir as _mybir
    from concourse.bass_utils import run_bass_kernel_spmd as _run

    w = {k: _np.asarray(v) for k, v in inputs.items()}

    def rows(a):
        return a.reshape(MT, 128, -1).transpose(1, 0, 2)

    def pairs(a):
        return a.transpose(1, 0, 2).reshape(D, E // 2, 128)

    def up0(routed, shared):
        return _np.concatenate([routed, shared[None]]).transpose(2, 0, 1)

    arrays = {
        "x": w["x"], "ctx_in": w["ctx_1024"], "mask": w["mask_BxS2_if1"], "g_xattn": w["g_xattn"], "g_ffn": w["g_ffn"],
        "ln_gamma": w["L0_xattn_ln_gamma"], "ln_beta": w["L0_xattn_ln_beta"],
        "w_in": w["L0_xattn_W_in"], "w_out": rows(w["L0_xattn_W_out"]), "b_out": w["L0_xattn_b_out"],
        "w0g": up0(w["L0_ffn_Wg"], w["L0_ffn_Wg_s"]), "w0u": up0(w["L0_ffn_Wu"], w["L0_ffn_Wu_s"]),
        "w0d": _np.concatenate([w["L0_ffn_Wd"], w["L0_ffn_Wd_s"][None]]).reshape(U0, D, 2, 128).transpose(3, 0, 2, 1),
        "w0r": w["L0_ffn_Wr"].T, "r0b": w["L0_ffn_rb"],
        "wq": w["L1_xattn_Wq"], "bq": w["L1_xattn_bq"].reshape(MT, 128).T,
        "wk": w["L1_xattn_Wk"], "bk": w["L1_xattn_bk"].reshape(MT, 128).T,
        "wv": w["L1_xattn_Wv"], "bv": w["L1_xattn_bv"].reshape(MT, 128).T,
        "wo": rows(w["L1_xattn_Wo"]), "bo": w["L1_xattn_bo"],
        "w1r": w["L1_ffn_gate_w"].T, "c1b": w["L1_ffn_correction_bias"],
        "w1g": pairs(w["L1_ffn_Wg"]), "w1u": pairs(w["L1_ffn_Wu"]),
        "w1d": w["L1_ffn_Wd"].reshape(E // 2, 2, 64, D).transpose(1, 2, 0, 3),
        "w1gs": w["L1_ffn_Wg_s"], "w1us": w["L1_ffn_Wu_s"], "w1ds": w["L1_ffn_Wd_s"],
    }
    arrays = {k: _np.ascontiguousarray(v) for k, v in arrays.items()}
    nc = _bacc.Bacc("TRN2", target_bir_lowering=False, num_devices=1)
    args = {k: nc.dram_tensor(k, a.shape, _mybir.dt.from_np(a.dtype), kind="ExternalInput").ap() for k, a in arrays.items()}
    out = nc.dram_tensor("out", (B, S, D), F32, kind="ExternalOutput").ap()
    scratch = nc.dram_tensor("scratch", (G, 128, 128), F32, kind="Internal").ap()
    flamingo_kernel(nc, **args, out=out, scratch=scratch)
    r = _run(nc, [arrays], core_ids=[0])
    return r.results[0]["out"]
```
